# Optimizing a Trainium2 kernel written in Bass

```python
import numpy as np
import jax
import jax.numpy as jnp

def _softmax(x, axis=-1):
    return jax.nn.softmax(x, axis=axis)

def _gelu(x):
    return jax.nn.gelu(x, approximate=True)

def _silu(x):
    return jax.nn.silu(x)

def _sigmoid(x):
    return jax.nn.sigmoid(x)

def _layernorm(x, axis=-1, eps=1e-05):
    m = jnp.mean(x, axis=axis, keepdims=True)
    v = jnp.var(x, axis=axis, keepdims=True)
    return (x - m) / jnp.sqrt(v + eps)

def _scatter_add(tgt, idx, src, axis=0):
    return tgt.at[idx].add(src)

def _segment_sum(src, seg, n):
    return jax.ops.segment_sum(src, seg, n)
kernel_name = 'mk_adaln_d1_jaxref_r8_ba8739'

def setup_inputs(seed: int=0):
    np.random.seed(seed)
    _w = jnp.asarray

    def _L0_attn_setup():
        import jax, jax.numpy as jnp
        import numpy as np
        B, L, D_MODEL = (4, 256, 128)
        D_INNER = 2 * D_MODEL
        D_STATE = 64
        D_CONV = 4
        DT_RANK = D_MODEL // 16

        def _mamba_block(x, ln_w, ln_b, W_in, conv_w, conv_b, W_xproj, W_dt, b_dt, A_log, D, W_out):
            residual = x
            mu = jnp.mean(x, axis=-1, keepdims=True)
            var = jnp.mean(jnp.square(x - mu), axis=-1, keepdims=True)
            xn = (x - mu) * jax.lax.rsqrt(var + 1e-05) * ln_w + ln_b
            xz = xn @ W_in
            xi, z = jnp.split(xz, 2, axis=-1)
            xc = jnp.transpose(xi, (0, 2, 1))
            xc = jax.lax.conv_general_dilated(xc, conv_w, window_strides=(1,), padding=[(D_CONV - 1, 0)], feature_group_count=D_INNER, dimension_numbers=('NCH', 'OIH', 'NCH'))
            xc = jnp.transpose(xc, (0, 2, 1)) + conv_b
            u = jax.nn.silu(xc)
            x_dbl = u @ W_xproj
            dt_r = x_dbl[..., :DT_RANK]
            Bm = x_dbl[..., DT_RANK:DT_RANK + D_STATE]
            Cm = x_dbl[..., DT_RANK + D_STATE:]
            delta = jax.nn.softplus(dt_r @ W_dt + b_dt)
            A = -jnp.exp(A_log)

            def step(h, inputs):
                d_t, B_t, C_t, u_t = inputs
                dA = jnp.exp(d_t[:, :, None] * A)
                h = h * dA + (d_t * u_t)[:, :, None] * B_t[:, None, :]
                y_t = jnp.einsum('bdn,bn->bd', h, C_t)
                return (h, y_t)
            h0 = jnp.zeros((x.shape[0], D_INNER, D_STATE), x.dtype)
            seq = (jnp.transpose(delta, (1, 0, 2)), jnp.transpose(Bm, (1, 0, 2)), jnp.transpose(Cm, (1, 0, 2)), jnp.transpose(u, (1, 0, 2)))
            _, ys = jax.lax.scan(step, h0, seq)
            y = jnp.transpose(ys, (1, 0, 2)) + u * D
            y = y * jax.nn.silu(z)
            out = y @ W_out
            return residual + out
        key = jax.random.key(seed)
        ks = jax.random.split(key, 10)
        inp = {}
        inp['x'] = jax.random.normal(ks[0], (B, L, D_MODEL), dtype=jnp.float32)
        inp['ln_w'] = jnp.ones((D_MODEL,), jnp.float32)
        inp['ln_b'] = jnp.zeros((D_MODEL,), jnp.float32)
        inp['W_in'] = jax.random.normal(ks[1], (D_MODEL, 2 * D_INNER), jnp.float32) / np.sqrt(D_MODEL)
        inp['conv_w'] = jax.random.normal(ks[2], (D_INNER, 1, D_CONV), jnp.float32) / np.sqrt(D_CONV)
        inp['conv_b'] = jax.random.normal(ks[3], (D_INNER,), jnp.float32) * 0.01
        inp['W_xproj'] = jax.random.normal(ks[4], (D_INNER, DT_RANK + 2 * D_STATE), jnp.float32) / np.sqrt(D_INNER)
        inp['W_dt'] = jax.random.normal(ks[5], (DT_RANK, D_INNER), jnp.float32) / np.sqrt(DT_RANK)
        inp['b_dt'] = jax.random.normal(ks[6], (D_INNER,), jnp.float32) * 0.1 - 4.0
        inp['A_log'] = jnp.log(jnp.broadcast_to(jnp.arange(1, D_STATE + 1, dtype=jnp.float32), (D_INNER, D_STATE)))
        inp['D'] = jnp.ones((D_INNER,), jnp.float32)
        inp['W_out'] = jax.random.normal(ks[7], (D_INNER, D_MODEL), jnp.float32) / np.sqrt(D_INNER)
        return inp
    _L0_attn_in = _L0_attn_setup()

    def _L0_ffn_setup():
        import jax, jax.numpy as jnp
        import numpy as np
        DIM = 128
        DEPTH = 2
        HEADS = 8
        DIM_HEAD = 64
        WINDOW = 64
        INNER = HEADS * DIM_HEAD
        HID = int(DIM * 4 * 2 / 3)
        B, N = (2, 1024)
        QK_SCALE = 8.0

        def shift_token(t):
            t1, t2 = jnp.split(t, 2, axis=-1)
            t2 = jnp.pad(t2, ((0, 0), (1, 0), (0, 0)))[:, :-1]
            return jnp.concatenate([t1, t2], axis=-1)

        def l2norm(t):
            return t / jnp.clip(jnp.linalg.norm(t, axis=-1, keepdims=True), 1e-12)

        def rotate_half(x):
            x1, x2 = jnp.split(x, 2, axis=-1)
            return jnp.concatenate([-x2, x1], axis=-1)

        def rotary_xpos(q, k):
            n = q.shape[-2]
            half_idx = jnp.arange(0, DIM_HEAD, 2, dtype=jnp.float32)
            inv_freq = 1.0 / 10000.0 ** (half_idx / DIM_HEAD)
            t = jnp.arange(n, dtype=jnp.float32)
            freqs = t[:, None] * inv_freq[None, :]
            freqs = jnp.concatenate([freqs, freqs], axis=-1)
            base = (half_idx + 0.4 * DIM_HEAD) / (1.4 * DIM_HEAD)
            power = (t - n // 2) / float(WINDOW // 2)
            scale = base[None, :] ** power[:, None]
            scale = jnp.concatenate([scale, scale], axis=-1)
            cos, sin = (jnp.cos(freqs), jnp.sin(freqs))
            q = q * cos * scale + rotate_half(q) * sin * scale
            k = k * cos / scale + rotate_half(k) * sin / scale
            return (q, k)

        def local_attention(q, k, v):
            b, h, n, d = q.shape
            w = n // WINDOW
            bq = q.reshape(b, h, w, WINDOW, d) * QK_SCALE
            bk = k.reshape(b, h, w, WINDOW, d)
            bv = v.reshape(b, h, w, WINDOW, d)

            def look_around(t):
                p = jnp.pad(t, ((0, 0), (0, 0), (1, 0), (0, 0), (0, 0)))
                return jnp.concatenate([p[:, :, :w], p[:, :, 1:]], axis=3)
            bk, bv = (look_around(bk), look_around(bv))
            bt = jnp.arange(n).reshape(w, WINDOW)
            btp = jnp.pad(bt, ((1, 0), (0, 0)), constant_values=-1)
            btk = jnp.concatenate([btp[:w], btp[1:]], axis=1)
            sim = jnp.einsum('bhwid,bhwjd->bhwij', bq, bk)
            i = bt[:, :, None]
            j = btk[:, None, :]
            mask = (i < j) | (i > j + WINDOW) | (j == -1)
            sim = jnp.where(mask, -jnp.finfo(sim.dtype).max, sim)
            attn = jax.nn.softmax(sim, axis=-1)
            out = jnp.einsum('bhwij,bhwjd->bhwid', attn, bv)
            return out.reshape(b, h, n, d)

        def _layer(x, wqkv, qs, ksc, wo, lg, lb, w1, b1, w2, b2):
            b, n, _ = x.shape
            h = shift_token(x)
            qkv = h @ wqkv
            q, k, v = jnp.split(qkv, 3, axis=-1)
            to_heads = lambda t: t.reshape(b, n, HEADS, DIM_HEAD).transpose(0, 2, 1, 3)
            q, k, v = (to_heads(q), to_heads(k), to_heads(v))
            q = l2norm(q) * qs
            k = l2norm(k) * ksc
            q, k = rotary_xpos(q, k)
            o = local_attention(q, k, v)
            o = o.transpose(0, 2, 1, 3).reshape(b, n, INNER)
            x = x + o @ wo
            h = shift_token(x)
            mu = h.mean(-1, keepdims=True)
            var = h.var(-1, keepdims=True)
            h = (h - mu) / jnp.sqrt(var + 1e-05) * lg + lb
            h = h @ w1 + b1
            a, g = jnp.split(h, 2, axis=-1)
            h = a * jax.nn.gelu(g, approximate=False)
            x = x + h @ w2 + b2
            return x
        key = jax.random.key(seed)
        ks = jax.random.split(key, 6)
        return {'x': jax.random.normal(ks[0], (B, N, DIM), jnp.float32), 'wqkv': jax.random.normal(ks[1], (DEPTH, DIM, 3 * INNER), jnp.float32) * 0.02, 'q_scale': jnp.ones((DEPTH, DIM_HEAD), jnp.float32), 'k_scale': jnp.ones((DEPTH, DIM_HEAD), jnp.float32), 'wo': jax.random.normal(ks[2], (DEPTH, INNER, DIM), jnp.float32) * 0.02, 'ln_g': jnp.ones((DEPTH, DIM), jnp.float32), 'ln_b': jnp.zeros((DEPTH, DIM), jnp.float32), 'w1': jax.random.normal(ks[3], (DEPTH, DIM, 2 * HID), jnp.float32) * 0.02, 'b1': jnp.zeros((DEPTH, 2 * HID), jnp.float32), 'w2': jax.random.normal(ks[4], (DEPTH, HID, DIM), jnp.float32) * 0.02, 'b2': jnp.zeros((DEPTH, DIM), jnp.float32)}
    _L0_ffn_in = _L0_ffn_setup()
    _L0_c = _w((lambda *s: np.random.randn(*s).astype(np.float32) * 0.05)(4, 128))
    _L0_wmod = _w((lambda *s: np.random.randn(*s).astype(np.float32) * 0.05)(128, 6 * 128) * 128 ** (-0.5))
    _d = {'L0_attn_x': _L0_attn_in['x'], 'L0_attn_ln_w': _L0_attn_in['ln_w'], 'L0_attn_ln_b': _L0_attn_in['ln_b'], 'L0_attn_W_in': _L0_attn_in['W_in'], 'L0_attn_conv_w': _L0_attn_in['conv_w'], 'L0_attn_conv_b': _L0_attn_in['conv_b'], 'L0_attn_W_xproj': _L0_attn_in['W_xproj'], 'L0_attn_W_dt': _L0_attn_in['W_dt'], 'L0_attn_b_dt': _L0_attn_in['b_dt'], 'L0_attn_A_log': _L0_attn_in['A_log'], 'L0_attn_D': _L0_attn_in['D'], 'L0_attn_W_out': _L0_attn_in['W_out'], 'L0_ffn_wqkv': _L0_ffn_in['wqkv'], 'L0_ffn_q_scale': _L0_ffn_in['q_scale'], 'L0_ffn_k_scale': _L0_ffn_in['k_scale'], 'L0_ffn_wo': _L0_ffn_in['wo'], 'L0_ffn_ln_g': _L0_ffn_in['ln_g'], 'L0_ffn_ln_b': _L0_ffn_in['ln_b'], 'L0_ffn_w1': _L0_ffn_in['w1'], 'L0_ffn_b1': _L0_ffn_in['b1'], 'L0_ffn_w2': _L0_ffn_in['w2'], 'L0_ffn_b2': _L0_ffn_in['b2'], 'L0_c': _L0_c, 'L0_wmod': _L0_wmod}
    _x0 = _d['L0_attn_x']
    _d['L0_attn_x'] = jax.random.normal(jax.random.fold_in(jax.random.key(seed), 1), (4, 1024, 128), dtype=_x0.dtype)
    del _x0
    return _d

def reference(L0_attn_x, L0_attn_ln_w, L0_attn_ln_b, L0_attn_W_in, L0_attn_conv_w, L0_attn_conv_b, L0_attn_W_xproj, L0_attn_W_dt, L0_attn_b_dt, L0_attn_A_log, L0_attn_D, L0_attn_W_out, L0_ffn_wqkv, L0_ffn_q_scale, L0_ffn_k_scale, L0_ffn_wo, L0_ffn_ln_g, L0_ffn_ln_b, L0_ffn_w1, L0_ffn_b1, L0_ffn_w2, L0_ffn_b2, L0_c, L0_wmod):

    def _L0_attn_ref(x, ln_w, ln_b, W_in, conv_w, conv_b, W_xproj, W_dt, b_dt, A_log, D, W_out):
        import jax, jax.numpy as jnp
        import numpy as np
        B, L, D_MODEL = (4, 256, 128)
        D_INNER = 2 * D_MODEL
        D_STATE = 64
        D_CONV = 4
        DT_RANK = D_MODEL // 16

        def _mamba_block(x, ln_w, ln_b, W_in, conv_w, conv_b, W_xproj, W_dt, b_dt, A_log, D, W_out):
            residual = x
            mu = jnp.mean(x, axis=-1, keepdims=True)
            var = jnp.mean(jnp.square(x - mu), axis=-1, keepdims=True)
            xn = (x - mu) * jax.lax.rsqrt(var + 1e-05) * ln_w + ln_b
            xz = xn @ W_in
            xi, z = jnp.split(xz, 2, axis=-1)
            xc = jnp.transpose(xi, (0, 2, 1))
            xc = jax.lax.conv_general_dilated(xc, conv_w, window_strides=(1,), padding=[(D_CONV - 1, 0)], feature_group_count=D_INNER, dimension_numbers=('NCH', 'OIH', 'NCH'))
            xc = jnp.transpose(xc, (0, 2, 1)) + conv_b
            u = jax.nn.silu(xc)
            x_dbl = u @ W_xproj
            dt_r = x_dbl[..., :DT_RANK]
            Bm = x_dbl[..., DT_RANK:DT_RANK + D_STATE]
            Cm = x_dbl[..., DT_RANK + D_STATE:]
            delta = jax.nn.softplus(dt_r @ W_dt + b_dt)
            A = -jnp.exp(A_log)

            def step(h, inputs):
                d_t, B_t, C_t, u_t = inputs
                dA = jnp.exp(d_t[:, :, None] * A)
                h = h * dA + (d_t * u_t)[:, :, None] * B_t[:, None, :]
                y_t = jnp.einsum('bdn,bn->bd', h, C_t)
                return (h, y_t)
            h0 = jnp.zeros((x.shape[0], D_INNER, D_STATE), x.dtype)
            seq = (jnp.transpose(delta, (1, 0, 2)), jnp.transpose(Bm, (1, 0, 2)), jnp.transpose(Cm, (1, 0, 2)), jnp.transpose(u, (1, 0, 2)))
            _, ys = jax.lax.scan(step, h0, seq)
            y = jnp.transpose(ys, (1, 0, 2)) + u * D
            y = y * jax.nn.silu(z)
            out = y @ W_out
            return residual + out
        return _mamba_block(x, ln_w, ln_b, W_in, conv_w, conv_b, W_xproj, W_dt, b_dt, A_log, D, W_out)

    def _L0_ffn_ref(x, wqkv, q_scale, k_scale, wo, ln_g, ln_b, w1, b1, w2, b2):
        import jax, jax.numpy as jnp
        import numpy as np
        DIM = 128
        DEPTH = 2
        HEADS = 8
        DIM_HEAD = 64
        WINDOW = 64
        INNER = HEADS * DIM_HEAD
        HID = int(DIM * 4 * 2 / 3)
        B, N = (2, 1024)
        QK_SCALE = 8.0

        def shift_token(t):
            t1, t2 = jnp.split(t, 2, axis=-1)
            t2 = jnp.pad(t2, ((0, 0), (1, 0), (0, 0)))[:, :-1]
            return jnp.concatenate([t1, t2], axis=-1)

        def l2norm(t):
            return t / jnp.clip(jnp.linalg.norm(t, axis=-1, keepdims=True), 1e-12)

        def rotate_half(x):
            x1, x2 = jnp.split(x, 2, axis=-1)
            return jnp.concatenate([-x2, x1], axis=-1)

        def rotary_xpos(q, k):
            n = q.shape[-2]
            half_idx = jnp.arange(0, DIM_HEAD, 2, dtype=jnp.float32)
            inv_freq = 1.0 / 10000.0 ** (half_idx / DIM_HEAD)
            t = jnp.arange(n, dtype=jnp.float32)
            freqs = t[:, None] * inv_freq[None, :]
            freqs = jnp.concatenate([freqs, freqs], axis=-1)
            base = (half_idx + 0.4 * DIM_HEAD) / (1.4 * DIM_HEAD)
            power = (t - n // 2) / float(WINDOW // 2)
            scale = base[None, :] ** power[:, None]
            scale = jnp.concatenate([scale, scale], axis=-1)
            cos, sin = (jnp.cos(freqs), jnp.sin(freqs))
            q = q * cos * scale + rotate_half(q) * sin * scale
            k = k * cos / scale + rotate_half(k) * sin / scale
            return (q, k)

        def local_attention(q, k, v):
            b, h, n, d = q.shape
            w = n // WINDOW
            bq = q.reshape(b, h, w, WINDOW, d) * QK_SCALE
            bk = k.reshape(b, h, w, WINDOW, d)
            bv = v.reshape(b, h, w, WINDOW, d)

            def look_around(t):
                p = jnp.pad(t, ((0, 0), (0, 0), (1, 0), (0, 0), (0, 0)))
                return jnp.concatenate([p[:, :, :w], p[:, :, 1:]], axis=3)
            bk, bv = (look_around(bk), look_around(bv))
            bt = jnp.arange(n).reshape(w, WINDOW)
            btp = jnp.pad(bt, ((1, 0), (0, 0)), constant_values=-1)
            btk = jnp.concatenate([btp[:w], btp[1:]], axis=1)
            sim = jnp.einsum('bhwid,bhwjd->bhwij', bq, bk)
            i = bt[:, :, None]
            j = btk[:, None, :]
            mask = (i < j) | (i > j + WINDOW) | (j == -1)
            sim = jnp.where(mask, -jnp.finfo(sim.dtype).max, sim)
            attn = jax.nn.softmax(sim, axis=-1)
            out = jnp.einsum('bhwij,bhwjd->bhwid', attn, bv)
            return out.reshape(b, h, n, d)

        def _layer(x, wqkv, qs, ksc, wo, lg, lb, w1, b1, w2, b2):
            b, n, _ = x.shape
            h = shift_token(x)
            qkv = h @ wqkv
            q, k, v = jnp.split(qkv, 3, axis=-1)
            to_heads = lambda t: t.reshape(b, n, HEADS, DIM_HEAD).transpose(0, 2, 1, 3)
            q, k, v = (to_heads(q), to_heads(k), to_heads(v))
            q = l2norm(q) * qs
            k = l2norm(k) * ksc
            q, k = rotary_xpos(q, k)
            o = local_attention(q, k, v)
            o = o.transpose(0, 2, 1, 3).reshape(b, n, INNER)
            x = x + o @ wo
            h = shift_token(x)
            mu = h.mean(-1, keepdims=True)
            var = h.var(-1, keepdims=True)
            h = (h - mu) / jnp.sqrt(var + 1e-05) * lg + lb
            h = h @ w1 + b1
            a, g = jnp.split(h, 2, axis=-1)
            h = a * jax.nn.gelu(g, approximate=False)
            x = x + h @ w2 + b2
            return x
        for l in range(DEPTH):
            x = _layer(x, wqkv[l], q_scale[l], k_scale[l], wo[l], ln_g[l], ln_b[l], w1[l], b1[l], w2[l], b2[l])
        return x
    x = L0_attn_x
    mod = (_silu(L0_c) @ L0_wmod).reshape(L0_c.shape[0], 6, 1, -1)
    sa, ca, ga, sb, cb, gb = (mod[:, 0], mod[:, 1], mod[:, 2], mod[:, 3], mod[:, 4], mod[:, 5])
    ga = (2 * (ga >= 0) - 1) * jnp.maximum(jnp.abs(ga), 0.25)
    gb = (2 * (gb >= 0) - 1) * jnp.maximum(jnp.abs(gb), 0.25)
    h = _layernorm(x, axis=-1) * (1 + ca) + sa
    x = x + ga * _L0_attn_ref(h, L0_attn_ln_w, L0_attn_ln_b, L0_attn_W_in, L0_attn_conv_w, L0_attn_conv_b, L0_attn_W_xproj, L0_attn_W_dt, L0_attn_b_dt, L0_attn_A_log, L0_attn_D, L0_attn_W_out)
    h = _layernorm(x, axis=-1) * (1 + cb) + sb
    x = x + gb * _L0_ffn_ref(h, L0_ffn_wqkv, L0_ffn_q_scale, L0_ffn_k_scale, L0_ffn_wo, L0_ffn_ln_g, L0_ffn_ln_b, L0_ffn_w1, L0_ffn_b1, L0_ffn_w2, L0_ffn_b2)
    return x

_drawn_inputs = setup_inputs


def setup_inputs(seed=0):
    import zlib

    import numpy as np

    out = dict(_drawn_inputs(seed))
    spreads = {'L0_attn_ln_w': (1.0, 0.2),
     'L0_attn_ln_b': (0.0, 0.449),
     'L0_attn_D': (1.0, 0.6),
     'L0_ffn_q_scale': (1.0, 0.6),
     'L0_ffn_k_scale': (1.0, 0.6),
     'L0_ffn_ln_g': (1.0, 0.6),
     'L0_ffn_ln_b': (0.0, 0.8),
     'L0_ffn_b1': (0.0, 0.8),
     'L0_ffn_b2': (0.0, 0.788)}
    factors = {'L0_attn_conv_b': 8.0,
     'L0_attn_W_xproj': 2.719,
     'L0_attn_W_dt': 5.083,
     'L0_attn_b_dt': 8.0,
     'L0_attn_A_log': 3.212,
     'L0_ffn_wqkv': 8.0,
     'L0_ffn_wo': 8.0,
     'L0_ffn_w1': 8.0,
     'L0_ffn_w2': 8.0}
    for name, (base, spread) in spreads.items():
        noise = np.random.default_rng([zlib.crc32(name.encode()), seed]).standard_normal(out[name].shape)
        drawn = base * np.exp(spread * noise) if base else spread * noise
        out[name] = jnp.asarray(drawn.astype(out[name].dtype))
    for name, factor in factors.items():
        out[name] = (out[name] * factor).astype(out[name].dtype)
    return out
```

```python
from contextlib import ExitStack

import numpy as np

import concourse.bass as bass
from concourse import mybir

F32 = mybir.dt.float32
BF16 = mybir.dt.bfloat16
ALU = mybir.AluOpType
ACT = mybir.ActivationFunctionType
AX = mybir.AxisListType.X

P = 128
NB = 4
L = 1024
BANK = 512
NC2 = L // BANK
D = 128
HALVES = 2
DI = HALVES * P
NS = 64
TAPS = 4
RANK = D // 16
GRP = 32
NG = 2 * NS // GRP
LAYERS = 2
HEADS = 8
DH = 64
WIN = 64
NW = L // WIN
PAIRS = HEADS // 2
INNER = HEADS * DH
HID = int(D * 4 * 2 / 3)
FB = 3
FROWS = [min(P, HID - P * f) for f in range(FB)]
TOK = L // P
QKS = 2 * PAIRS * NC2
QUAD = 4
GROUPS = PAIRS * NW // QUAD
LAG = 3
EPS = 1e-5
EXP = "exp_and_others"
LOG = "natural_log"
LN2 = float(np.log(2.0))
NORM_SHIFT = 20
LN_SLACK = 2e-7


class Steps:

    def __init__(self, eng, sem):
        self.eng, self.sem, self.base, self.k, self.outer = eng, sem, 0, 0, []

    def done(self, inst):
        inst.then_inc(self.sem, 1)
        self.k += 1

    def wait(self):
        self.eng.wait_ge(self.sem, self.base + self.k)

    def enter(self, var, per):
        self.outer.append((self.base, self.k, per))
        self.base, self.k = self.base + self.k + var * per, 0

    def leave(self, times):
        base, k, per = self.outer.pop()
        assert self.k == per, (self.k, per)
        self.base, self.k = base, k + per * times


VECS = {"ln_w": 1, "ln_b": 1, "c": NB, "conv_b": HALVES, "b_dt": HALVES, "D": HALVES, "qk": 4 * LAYERS,
        "ln_g": LAYERS, "ln_b2": LAYERS, "b2": LAYERS, "b1": 2 * FB * LAYERS}


def adaln_block(nc, x, vecs, W_in, conv_w, W_xproj, W_dt, A_log, W_out, wqkv, wo, w1, w2, wmod,
                k_ident, k_ones, k_blocks, k_select, k_mask, k_tables, out):
    with ExitStack() as ctx:
        def sb(name, shape, dt=F32):
            return ctx.enter_context(nc.sbuf_tensor(name, shape, dt))

        def sem(name):
            return ctx.enter_context(nc.semaphore(name))

        ps = ctx.enter_context(nc.psum_tensor("ps", [P, 8, BANK], F32))

        def banks(first, n=NC2, rows=slice(0, P)):
            return ps[rows, first:first + n, :].rearrange("p a b -> p (a b)")

        ident = sb("ident", [P, P])
        mean_w = sb("mean_w", [P, P])
        xT = sb("xT", [P, NB, L])
        hf = sb("hf", [P, NB, L])
        lnA = sb("lnA", [P, L])
        lnB = sb("lnB", [P, L])
        lnC = sb("lnC", [P, L])
        mod = sb("mod", [P, 6, NB])
        gate = sb("gate", [P, 2, NB])
        gtmp = sb("gtmp", [P, 2, 2, NB])
        silu_c = sb("silu_c", [P, NB])
        vec_s = sb("vec_s", [P, sum(VECS.values())])
        at, col = {}, 0
        for name, width in VECS.items():
            at[name], col = vec_s[:, col:col + width], col + width
        qv = at["qk"].rearrange("p (l a) -> p l a", a=4)
        b1s = at["b1"].rearrange("p (l a f) -> p l a f", a=2, f=FB)
        epsv = sb("epsv", [P, 4])

        ARENA = 37500
        arena = sb("arena", [P, ARENA])
        used = [0]

        def carve(n):
            a = arena[:, used[0]:used[0] + n]
            used[0] += n
            assert used[0] <= ARENA, used[0]
            return a

        def carve3(a, n):
            return carve(a * n).rearrange("p (a n) -> p a n", a=a)

        select = carve(GRP * P // 2).bitcast(BF16).rearrange("p (a n) -> p a n", a=GRP)
        bcs = carve(NG * L // 2).bitcast(BF16).rearrange("p (g n) -> p g n", g=NG)
        u = carve3(HALVES, L)
        zs = carve3(HALVES, L)
        delta = carve3(HALVES, L)
        du = carve3(HALVES, L)
        dA = [carve3(HALVES, L) for _ in range(2)]
        dBu = [carve3(HALVES, L) for _ in range(2)]
        hst_both = carve(2 * HALVES * L)
        hst = [hst_both[:, i * HALVES * L:(i + 1) * HALVES * L].rearrange("p (a n) -> p a n", a=HALVES)
               for i in range(2)]
        hC = [carve3(HALVES, L) for _ in range(2)]
        Csb = [carve(L) for _ in range(2)]
        hres = carve(L)
        xn = carve(L + TAPS - 1)
        wmod_s = hC[0].rearrange("p a n -> p (a n)")[:, 0:6 * D]
        w_in = carve(2 * DI)
        convw = hC[1].rearrange("p a n -> p (a n)")[:, 0:DI * TAPS]
        w_taps = carve3(TAPS, DI)
        A = carve3(HALVES, NS)
        w_x = carve3(HALVES, RANK + 2 * NS)
        w_bc = carve(HALVES * NG * 3 * GRP).rearrange("p (m g r n) -> p m g r n", m=HALVES, g=NG, r=3)
        w_dt = carve(DI)
        w_out = carve3(HALVES, D)
        diagD = carve3(HALVES, P)
        dtr = lnB[0:RANK, :]
        spY, spL, spX, spT, r1 = dBu[0], dBu[1], hst[0], hst[1], hC[0]

        used[0] = 0
        w_qkv = carve(3 * INNER)
        w_rot = carve(2 * INNER)
        w_o = carve3(PAIRS, D)
        w_1 = carve(2 * HID)
        w_2 = carve3(FB, D)
        blocks = carve(P)
        mask = carve3(2, 2 * WIN)
        tables = carve3(4, L)
        hs_all = carve(WIN + L)
        hs = hs_all[:, WIN:]
        qT = carve3(PAIRS, L)
        kT = carve(PAIRS * (L + WIN)).rearrange("p (a n) -> p a n", a=PAIRS)
        vtok = carve3(NW, INNER)
        oT = carve3(PAIRS, L)
        qcos = carve3(2, BANK)
        qsin = carve3(2, BANK)
        qrot = carve3(2, BANK)
        qsq = carve3(2, BANK)
        qln = carve3(2, BANK)
        qinv = carve3(2, BANK)
        sc, ex, pr, pT = qcos, qsin, qrot, qsq
        smax = carve3(2, QUAD)
        ssum = carve3(2, QUAD)
        srec = carve3(2, QUAD)
        gl = qT[:, 0:2, :]
        ff = vtok.rearrange("p a n -> p (a n)")[:, 0:FB * L].rearrange("p (a n) -> p a n", a=FB)

        names = """consts_in mod_in mamba_in select_in silu_c mod_ps mod_sb consts_ok prep_ok a_ok
            x_in ln_mean ln_dev ln_sq ln_var ln_rstd hres_ok xn_ok xc_ps z_ps u_ok zs_ok
            dtr_ps dtr_ok bc_ps bc_hi bc_r1 bc_mid bc_ok dt_ps sp_ok du_ok
            b_ps dbu_ok c_ps c_ok da_ok h_ok hc_ok y_acc gated mix_ps x1_ok batch_ok
            layer_in weights_ok hs_ok v_ps v_ok qk_ps sq_ok ss_ps inv_ok rotated halves_ok qk_ok
            sim_ps masked max_ok shifted sum_ok exp_ok rsum_ok prob_ok pt_ps pt_ok o_ps o_ok wo_ps attn_ok
            ffin_ok ag_ps gelu_ok ff_ok w2_ps layer_ok fin_ok stored
            vec_step act_step marks""".split()
        s = {n: sem(n) for n in names}

        mod_loads = [(vec_s[:], vecs), (wmod_s, wmod), (mean_w[:], k_ones), (ident[:], k_ident)]
        mamba_loads = [(w_in, W_in),
                       (convw, conv_w.rearrange("d o k -> o (d k)").broadcast_to([P, DI * TAPS])),
                       (A, A_log.rearrange("(m p) n -> p m n", p=P)),
                       (w_x, W_xproj.rearrange("(m p) n -> p m n", p=P)),
                       (w_dt[0:RANK], W_dt),
                       (w_out, W_out.rearrange("(m p) n -> p m n", p=P))]
        phase_loads = [(blocks, k_blocks), (mask, k_mask)]

        def layer_loads(l):
            full = (FB - 1) * P

            def one(w):
                return w[bass.ds(l, 1)].rearrange("l a b -> (l a) b")

            return [(w_qkv, one(wqkv)),
                    (w_o, one(wo).rearrange("(a p) n -> p a n", p=P)),
                    (w_1, one(w1)),
                    (w_2[:, 0:FB - 1, :], w2[bass.ds(l, 1), 0:full].rearrange("l (a p) n -> p (l a) n", p=P)),
                    (w_2[0:FROWS[-1], FB - 1, :], w2[bass.ds(l, 1), full:HID].rearrange("l a n -> (l a) n")),
                    (tables, k_tables)]

        N_LAYER_LOADS = 6

        def passed(eng):
            eng.sem_inc(s["marks"], 1)

        def table(act, name):
            passed(act)
            act.preload_act_table_set(name)

        block = ctx.enter_context(nc.Block())

        N_LN_MAMBA = 3

        @block.sync
        def _(sp):
            for dst, src in mod_loads:
                sp.dma_start(dst, src).then_inc(s["mod_in"], 16)
            for b in range(NB):
                sp.dma_start(xT[:, b, :], x[:, b, :]).then_inc(s["x_in"], 16)
            for dst, src in mamba_loads:
                sp.dma_start(dst, src).then_inc(s["mamba_in"], 16)
            sp.wait_ge(s["batch_ok"], NB + 1)
            for dst, src in phase_loads:
                sp.dma_start(dst, src).then_inc(s["consts_in"], 16)
            with sp.Fori(0, LAYERS) as l:
                sp.wait_ge(s["layer_ok"], l * NB + 1)
                for dst, src in layer_loads(l):
                    sp.dma_start(dst, src).then_inc(s["layer_in"], 16)
            for b in range(NB):
                sp.wait_ge(s["fin_ok"], b + 1)
                sp.dma_start(out[:, b, :], xT[:, b, :]).then_inc(s["stored"], 16)
            sp.wait_ge(s["stored"], 16 * NB)

        @block.tensor
        def _(pe):
            def layer_norm(src, q):
                for ch in range(NC2):
                    mm = pe.matmul(ps[:, 6 + ch, :], mean_w[:], src(ch), start=True, stop=True)
                mm.then_inc(s["ln_mean"], 1)
                pe.wait_ge(s["ln_sq"], q + 1)
                for ch in range(NC2):
                    mm = pe.matmul(ps[:, 6 + ch, :], mean_w[:], lnB[:, ch * BANK:(ch + 1) * BANK],
                                   start=True, stop=True)
                mm.then_inc(s["ln_var"], 1)

            def chunk(ap, ch):
                return ap[:, ch * BANK:(ch + 1) * BANK]

            pe.wait_ge(s["silu_c"], 1)
            for j in range(6):
                mm = pe.matmul(ps[:, 7, j * NB:(j + 1) * NB], wmod_s[:, j * D:(j + 1) * D], silu_c[:],
                               start=True, stop=True)
            mm.then_inc(s["mod_ps"], 1)
            pe.wait_ge(s["x_in"], 16 * NB)
            for name in ("y_acc", "ss_ps", "pt_ps", "o_ps"):
                pe.sem_inc(s[name], 2)
            pe.wait_ge(s["select_in"], 16)
            pe.wait_ge(s["prep_ok"], 1)
            with pe.Fori(0, NB) as b:
                pe.wait_ge(s["batch_ok"], b + 1)
                layer_norm(lambda ch: xT[:, b, ch * BANK:(ch + 1) * BANK], b * N_LN_MAMBA)
                pe.wait_ge(s["hres_ok"], b + 1)
                layer_norm(lambda ch: chunk(hres, ch), b * N_LN_MAMBA + 1)
                pe.wait_ge(s["xn_ok"], b + 1)
                for m in range(HALVES):
                    for ch in range(NC2):
                        for k in range(TAPS):
                            mm = pe.matmul(ps[:, 2 * m + ch, :], w_taps[:, k, m * P:(m + 1) * P],
                                           xn[:, ch * BANK + k:ch * BANK + k + BANK],
                                           start=(k == 0), stop=(k == TAPS - 1))
                    mm.then_inc(s["xc_ps"], 1)
                for m in range(HALVES):
                    for ch in range(NC2):
                        o = ch * BANK + TAPS - 1
                        mm = pe.matmul(ps[:, 4 + 2 * m + ch, :], w_in[:, DI + m * P:DI + (m + 1) * P],
                                       xn[:, o:o + BANK], start=True, stop=True)
                    mm.then_inc(s["z_ps"], 1)
                pe.wait_ge(s["u_ok"], HALVES * b + HALVES)
                for ch in range(NC2):
                    for m in range(HALVES):
                        mm = pe.matmul(ps[0:RANK, ch, :], w_x[:, m, 0:RANK], chunk(u[:, m, :], ch),
                                       start=(m == 0), stop=(m == HALVES - 1))
                mm.then_inc(s["dtr_ps"], 1)

                def spread(g, first):
                    for ch in range(NC2):
                        for m in range(HALVES):
                            mm = pe.matmul(ps[0:3 * GRP, first + ch, :],
                                           w_bc[:, m, g, :, :].rearrange("p r n -> p (r n)"),
                                           chunk(u[:, m, :], ch), start=(m == 0), stop=(m == HALVES - 1))
                    mm.then_inc(s["bc_ps"], 1)

                def dt_proj(m, first):
                    for ch in range(NC2):
                        mm = pe.matmul(ps[:, first + ch, :], w_dt[0:RANK, m * P:(m + 1) * P],
                                       chunk(dtr, ch), start=True, stop=True)
                    mm.then_inc(s["dt_ps"], 1)

                spread(0, 2)
                pe.wait_ge(s["zs_ok"], HALVES * b + HALVES)
                spread(1, 4)
                spread(2, 6)
                pe.wait_ge(s["dtr_ok"], b + 1)
                dt_proj(0, 0)
                pe.wait_ge(s["bc_r1"], NG * b + 1)
                spread(3, 2)
                pe.wait_ge(s["bc_r1"], NG * b + 2)
                dt_proj(1, 4)
                pe.wait_ge(s["du_ok"], b + 1)
                for m in range(HALVES):
                    for ch in range(NC2):
                        pe.matmul(ps[:, 2 * m + ch, :], diagD[:, m, :], chunk(u[:, m, :], ch),
                                  start=True, stop=False, skip_group_check=True)

                def spread_b(n, par, G):
                    pe.wait_ge(s["dbu_ok"], G + 1)
                    for ch in range(NC2):
                        mm = pe.matmul(ps[:, 4 + ch, :], select[0:3 * GRP, n, :],
                                       bcs[0:3 * GRP, par, ch * BANK:(ch + 1) * BANK], start=True, stop=True)
                    mm.then_inc(s["b_ps"], 1)

                def spread_c(n, par, G):
                    pe.wait_ge(s["c_ok"], G + 1)
                    for ch in range(NC2):
                        mm = pe.matmul(ps[:, 6 + ch, :], select[0:3 * GRP, n, :],
                                       bcs[0:3 * GRP, 2 + par, ch * BANK:(ch + 1) * BANK], start=True, stop=True)
                    mm.then_inc(s["c_ps"], 1)

                def sum_states(par, G):
                    pe.wait_ge(s["hc_ok"], G + 3)
                    for m in range(HALVES):
                        for ch in range(NC2):
                            mm = pe.matmul(ps[:, 2 * m + ch, :], ident[:], chunk(hC[par][:, m, :], ch),
                                           start=False, stop=False, skip_group_check=True)
                    mm.then_inc(s["y_acc"], 1)

                for G in range(LAG):
                    spread_b(G // 2, G % 2, b * NS + G)
                    spread_c(G // 2, G % 2, b * NS + G)
                with pe.Fori(1, GRP - 1) as i:
                    G = b * NS + 2 * i + 1
                    spread_b(i, 1, G)
                    spread_c(i, 1, G)
                    sum_states(0, G - LAG)
                    spread_b(i + 1, 0, G + 1)
                    spread_c(i + 1, 0, G + 1)
                    sum_states(1, G + 1 - LAG)
                G = b * NS + NS - 1
                spread_b(GRP - 1, 1, G)
                spread_c(GRP - 1, 1, G)
                for k in range(LAG + 1):
                    sum_states((NS - 1 - LAG + k) % 2, G - LAG + k)
                pe.wait_ge(s["gated"], b + 1)
                for ch in range(NC2):
                    for m in range(HALVES):
                        mm = pe.matmul(ps[:, 4 + ch, :], w_out[:, m, :], chunk(zs[:, m, :], ch),
                                       start=(m == 0), stop=(m == HALVES - 1))
                mm.then_inc(s["mix_ps"], 1)
                pe.wait_ge(s["x1_ok"], b + 1)
                layer_norm(lambda ch: xT[:, b, ch * BANK:(ch + 1) * BANK], b * N_LN_MAMBA + 2)

            def attention(l, b, I):
                pe.wait_ge(s["hs_ok"], 2 * I + 1)

                def values(t):
                    pe.wait_ge(s["v_ok"], NW * I + t + 1)
                    pe.matmul(ps[:, 6 + t % 2, :], hs_all[:, t * WIN:t * WIN + P], w_qkv[:, 2 * INNER:],
                              start=True, stop=True).then_inc(s["v_ps"], 1)

                def project(st):
                    j, ch, base = st // 2, st % 2, 3 * (st % 2)
                    n = QKS * I + st
                    pe.wait_ge(s["halves_ok"], n + 1)
                    pe.wait_ge(s["sq_ok"], n + 1)
                    pe.matmul(ps[:, base, :], w_qkv[:, j * P:(j + 1) * P], chunk(hs, ch), start=True, stop=True)
                    pe.matmul(ps[:, base + 1, :], w_rot[:, j * P:(j + 1) * P], chunk(hs, ch),
                              start=True, stop=True).then_inc(s["qk_ps"], 1)

                def norms(st):
                    n = QKS * I + st
                    pe.wait_ge(s["sq_ok"], n + 3)
                    pe.wait_ge(s["inv_ok"], n + 1)
                    pe.matmul(ps[:, 3 * (st % 2) + 2, :], blocks, qsq[:, st % 2, :],
                              start=True, stop=True).then_inc(s["ss_ps"], 1)

                for st in range(QKS + 1):
                    if st < QKS:
                        project(st)
                    if st < NW:
                        values(st)
                    if st >= 1:
                        norms(st - 1)
                pe.wait_ge(s["qk_ok"], QKS * (I + 1) + 2)
                pe.wait_ge(s["v_ok"], NW * (I + 1) + 2)
                passed(pe)

                def scores(g):
                    hp, w0 = g // QUAD, QUAD * (g % QUAD)
                    pe.wait_ge(s["masked"], GROUPS * I + g + 1)
                    passed(pe)
                    for w in range(w0, w0 + QUAD):
                        for h in range(2):
                            rows = slice(DH * h, DH * h + DH)
                            keys = kT[rows, hp, w * WIN:(w + 2) * WIN]
                            mm = pe.matmul(ps[rows, g % 2, (w - w0) * P:(w - w0 + 1) * P],
                                           qT[rows, hp, w * WIN:(w + 1) * WIN], keys, start=True, stop=True)
                    mm.then_inc(s["sim_ps"], 1)

                def turn(g):
                    n = GROUPS * I + g
                    pe.wait_ge(s["prob_ok"], n + 3)
                    pe.wait_ge(s["pt_ok"], n + 1)
                    for w in range(QUAD):
                        mm = pe.transpose(ps[:, 2 + g % 2, w * P:(w + 1) * P], pr[:, g % 2, w * P:(w + 1) * P],
                                          ident[:])
                    mm.then_inc(s["pt_ps"], 1)

                def weigh(g):
                    hp, w0 = g // QUAD, QUAD * (g % QUAD)
                    n = GROUPS * I + g
                    pe.wait_ge(s["pt_ok"], n + 3)
                    pe.wait_ge(s["o_ok"], n + 1)
                    passed(pe)
                    for w in range(w0, w0 + QUAD):
                        for h in range(2):
                            dst = ps[DH * h:DH * h + DH, 4 + g % 2, (w - w0) * WIN:(w - w0 + 1) * WIN]
                            cols = slice((2 * hp + h) * DH, (2 * hp + h + 1) * DH)
                            pc = slice((w - w0) * P + h * WIN, (w - w0) * P + h * WIN + WIN)
                            mm = pe.matmul(dst, vtok[:, w, cols], pT[:, g % 2, pc], start=True, stop=True)
                    mm.then_inc(s["o_ps"], 1)

                for g in range(GROUPS + 3):
                    if g < GROUPS:
                        scores(g)
                    if 2 <= g < GROUPS + 2:
                        turn(g - 2)
                    if g >= 3:
                        weigh(g - 3)
                pe.wait_ge(s["o_ok"], GROUPS * (I + 1) + 2)
                for ch in range(NC2):
                    for hp in range(PAIRS):
                        mm = pe.matmul(ps[:, 6 + ch, :], w_o[:, hp, :], chunk(oT[:, hp, :], ch),
                                       start=(hp == 0), stop=(hp == PAIRS - 1))
                mm.then_inc(s["wo_ps"], 1)

            def feed_forward(l, b, I):
                pe.wait_ge(s["hs_ok"], 2 * I + 2)
                layer_norm(lambda ch: chunk(hs, ch), NB * N_LN_MAMBA + I)
                pe.wait_ge(s["ffin_ok"], I + 1)
                for f, rows in enumerate(FROWS):
                    if f == 2:
                        pe.wait_ge(s["ff_ok"], FB * I + 1)
                    for part in range(2):
                        for ch in range(NC2):
                            o = part * HID + f * P
                            mm = pe.matmul(ps[0:rows, 4 * (f % 2) + 2 * part + ch, :], w_1[:, o:o + rows],
                                           chunk(lnA, ch), start=True, stop=True)
                    mm.then_inc(s["ag_ps"], 1)
                pe.wait_ge(s["ff_ok"], FB * I + FB)
                for ch in range(NC2):
                    for f, rows in enumerate(FROWS):
                        mm = pe.matmul(ps[:, 4 + ch, :], w_2[0:rows, f, :], ff[0:rows, f, ch * BANK:(ch + 1) * BANK],
                                       start=(f == 0), stop=(f == FB - 1))
                mm.then_inc(s["w2_ps"], 1)

            with pe.Fori(0, LAYERS) as l:
                pe.wait_ge(s["weights_ok"], 6 * l + 6)
                passed(pe)
                with pe.Fori(0, NB) as b:
                    I = l * NB + b
                    attention(l, b, I)
                    feed_forward(l, b, I)
        @block.scalar
        def _(act):
            own = Steps(act, s["act_step"])

            def layer_norm(q):
                act.wait_ge(s["ln_dev"], q + 1)
                act.activation(lnB[:], lnA[:], ACT.Square).then_inc(s["ln_sq"], 1)
                act.wait_ge(s["ln_var"], q + 1)
                table(act, LOG)
                own.done(act.activation(lnC[:], banks(6), ACT.Ln, bias=epsv[:, 0:1]))
                table(act, EXP)
                own.wait()
                act.activation(lnC[:], lnC[:], ACT.Exp, scale=-0.5).then_inc(s["ln_rstd"], 1)

            act.sem_inc(s["c_ok"], 1)
            act.wait_ge(s["mod_in"], 16 * len(mod_loads))
            act.activation(silu_c[:], at["c"], ACT.Silu).then_inc(s["silu_c"], 1)
            act.wait_ge(s["mamba_in"], 16 * len(mamba_loads))
            table(act, EXP)
            own.done(act.activation(A, A, ACT.Exp))
            own.wait()
            act.mul(A, A, -1.0).then_inc(s["a_ok"], 1)
            act.wait_ge(s["consts_ok"], 1)
            act.wait_ge(s["a_ok"], 1)
            PER_BATCH = N_LN_MAMBA + 3 * HALVES
            with act.Fori(0, NB) as b:
                own.enter(b, PER_BATCH)
                layer_norm(b * N_LN_MAMBA)
                layer_norm(b * N_LN_MAMBA + 1)
                for m in range(HALVES):
                    act.wait_ge(s["xc_ps"], HALVES * b + m + 1)
                    act.activation(u[:, m, :], banks(2 * m), ACT.Silu, bias=at["conv_b"][:, m:m + 1]).then_inc(s["u_ok"], 1)
                for m in range(HALVES):
                    act.wait_ge(s["z_ps"], HALVES * b + m + 1)
                    act.activation(zs[:, m, :], banks(4 + 2 * m), ACT.Silu).then_inc(s["zs_ok"], 1)
                table(act, EXP)

                def parts(g):
                    act.wait_ge(s["bc_ps"], NG * b + g + 1)
                    act.copy(bcs[0:3 * GRP, g, :], banks([2, 4, 6, 2][g], rows=slice(0, 3 * GRP)))\
                        .then_inc(s["bc_hi"], 1)
                    act.wait_ge(s["bc_r1"], NG * b + g + 1)
                    act.copy(bcs[GRP:2 * GRP, g, :], r1[GRP:2 * GRP, g % 2, :])
                    act.copy(bcs[2 * GRP:3 * GRP, g, :], r1[2 * GRP:3 * GRP, g % 2, :]).then_inc(s["bc_mid"], 1)

                def softplus(m):
                    act.wait_ge(s["dt_ps"], HALVES * b + m + 1)
                    own.done(act.activation(spX[:, m, :], banks(4 * m), ACT.Identity, bias=at["b_dt"][:, m:m + 1]))
                    own.wait()
                    own.done(act.activation(spY[:, m, :], spX[:, m, :], ACT.Abs))
                    own.wait()
                    own.done(act.activation(spY[:, m, :], spY[:, m, :], ACT.Exp, scale=-1.0))
                    own.wait()


                parts(0)
                parts(1)
                softplus(0)
                parts(2)
                parts(3)
                softplus(1)
                table(act, LOG)
                act.activation(spL, spY, ACT.Ln, bias=epsv[:, 1:2]).then_inc(s["sp_ok"], 1)

                def state(n, par, G):
                    act.wait_ge(s["h_ok"], G + 1)
                    for m in range(HALVES):
                        e = act.activation(dA[par][:, m, 1:L], delta[:, m, 1:L], ACT.Exp, scale=n(m))
                    e.then_inc(s["da_ok"], 1)
                    act.wait_ge(s["c_ps"], G + 1)
                    act.wait_ge(s["hc_ok"], G + 1)
                    act.copy(Csb[par], banks(6)).then_inc(s["c_ok"], 1)

                act.wait_ge(s["du_ok"], b + 1)
                passed(act)
                table(act, EXP)
                with act.Fori(0, GRP) as i:
                    for par in range(2):
                        state(lambda m: A[:, m, bass.ds(i + par * GRP, 1)], par, b * NS + 2 * i + par)
                layer_norm(b * N_LN_MAMBA + 2)
                own.leave(NB)

            def attention(I):
                def squares(st):
                    n = QKS * I + st
                    act.wait_ge(s["qk_ps"], n + 1)
                    act.wait_ge(s["ss_ps"], n + 1)
                    act.activation(qsq[:, st % 2, :], ps[:, 3 * (st % 2), :], ACT.Square).then_inc(s["sq_ok"], 1)

                def log_norm(st):
                    act.wait_ge(s["ss_ps"], QKS * I + st + 3)
                    own.done(act.activation(qln[:, st % 2, :], ps[:, 3 * (st % 2) + 2, :], ACT.Ln,
                                            scale=float(2 ** NORM_SHIFT), bias=epsv[:, 2:3]))

                def inv_norm(st):
                    act.wait_ge(s["qk_ok"], QKS * I + st + 1)
                    act.activation(qinv[:, st % 2, :], qln[:, st % 2, :], ACT.Exp, scale=-0.5,
                                   bias=epsv[:, 3:4]).then_inc(s["inv_ok"], 1)

                def value_copy(t):
                    act.wait_ge(s["v_ps"], NW * I + t + 1)
                    act.copy(vtok[:, t, :], ps[:, 6 + t % 2, :]).then_inc(s["v_ok"], 1)

                for st in range(QKS + 1):
                    if st >= 1:
                        log_norm(st - 1)
                    if st < QKS:
                        squares(st)
                    if st < NW:
                        value_copy(st)
                    if st >= 1:
                        own.wait()
                        inv_norm(st - 1)

                def exps(g):
                    n = GROUPS * I + g
                    act.wait_ge(s["shifted"], n + 3)
                    act.wait_ge(s["prob_ok"], n + 1)
                    act.activation(ex[:, g % 2, :], sc[:, g % 2, :], ACT.Exp).then_inc(s["exp_ok"], 1)

                def turned(g):
                    n = GROUPS * I + g
                    act.wait_ge(s["pt_ps"], n + 3)
                    act.wait_ge(s["o_ps"], n + 1)
                    act.copy(pT[:, g % 2, :], ps[:, 2 + g % 2, :]).then_inc(s["pt_ok"], 1)

                def heads_out(g):
                    hp, w0 = g // QUAD, QUAD * (g % QUAD)
                    act.wait_ge(s["o_ps"], GROUPS * I + g + 3)
                    act.copy(oT[:, hp, w0 * WIN:(w0 + QUAD) * WIN], ps[:, 4 + g % 2, 0:QUAD * WIN])\
                        .then_inc(s["o_ok"], 1)

                table(act, EXP)
                for g in range(GROUPS + 3):
                    if g < GROUPS:
                        exps(g)
                    if 2 <= g < GROUPS + 2:
                        turned(g - 2)
                    if g >= 3:
                        heads_out(g - 3)

            act.sem_inc(s["v_ok"], 2)
            act.sem_inc(s["sq_ok"], 2)
            act.sem_inc(s["inv_ok"], 2)
            act.sem_inc(s["exp_ok"], 2)
            act.sem_inc(s["pt_ok"], 2)
            act.sem_inc(s["o_ok"], 2)
            PER_LB = QKS + 1
            with act.Fori(0, LAYERS) as l:
                own.enter(l, PER_LB * NB)
                with act.Fori(0, NB) as b:
                    own.enter(b, PER_LB)
                    I = l * NB + b
                    attention(I)
                    layer_norm(NB * N_LN_MAMBA + I)
                    for f, rows in enumerate(FROWS):
                        act.wait_ge(s["ag_ps"], FB * I + f + 1)
                        if f == 2:
                            act.wait_ge(s["ff_ok"], FB * I + 1)
                        act.activation(gl[0:rows, f % 2, :], banks(4 * (f % 2) + 2, rows=slice(0, rows)), ACT.Gelu,
                                       bias=b1s[0:rows, bass.ds(l, 1), 1, f])\
                            .then_inc(s["gelu_ok"], 1)
                    own.leave(NB)
                own.leave(LAYERS)

        @block.vector
        def _(dve):
            own = Steps(dve, s["vec_step"])

            def layer_norm(src, dst, scale, shift, q, inc):
                dve.wait_ge(s["ln_mean"], q + 1)
                dve.tensor_tensor(lnA[:], src, banks(6), ALU.subtract).then_inc(s["ln_dev"], 1)
                dve.wait_ge(s["ln_rstd"], q + 1)
                own.done(dve.tensor_tensor(lnA[:], lnA[:], lnC[:], ALU.mult))
                own.wait()
                dve.tensor_scalar(dst, lnA[:], scale, shift, ALU.mult, ALU.add).then_inc(s[inc], 1)

            dve.sem_inc(s["batch_ok"], 1)
            dve.sem_inc(s["dbu_ok"], 1)
            dve.sem_inc(s["h_ok"], 2)
            dve.memset(epsv[:, 0:1], EPS)
            dve.memset(epsv[:, 1:2], 1.0)
            dve.memset(epsv[:, 2:3], 2.0 ** -63)
            dve.memset(epsv[:, 3:4], NORM_SHIFT / 2 * LN2)
            for par in range(2):
                dve.memset(dA[par][:, :, 0:1], 0.0)
            dve.memset(xn[:, 0:TAPS - 1], 0.0).then_inc(s["consts_ok"], 1)

            dve.wait_ge(s["mod_ps"], 1)
            dve.tensor_copy(mod[:].rearrange("p a b -> p (a b)"), ps[:, 7, 0:6 * NB]).then_inc(s["mod_sb"], 1)
            dve.wait_ge(s["mod_sb"], 1)
            for j in range(2):
                g = mod[:, 2 + 3 * j, :]
                own.done(dve.tensor_scalar(mod[:, 1 + 3 * j, :], mod[:, 1 + 3 * j, :], 1.0, None, ALU.add))
                own.done(dve.tensor_scalar(gtmp[:, j, 0, :], g, -1.0, None, ALU.mult))
                own.wait()
                own.done(dve.tensor_tensor(gtmp[:, j, 0, :], gtmp[:, j, 0, :], g, ALU.max))
                own.done(dve.tensor_scalar(gtmp[:, j, 1, :], g, 0.0, 2.0, ALU.is_ge, ALU.mult))
                own.wait()
                own.done(dve.tensor_scalar(gtmp[:, j, 0, :], gtmp[:, j, 0, :], 0.25, None, ALU.max))
                own.wait()
                own.done(dve.scalar_tensor_tensor(gate[:, j, :], gtmp[:, j, 1, :], -1.0, gtmp[:, j, 0, :],
                                                  ALU.add, ALU.mult))
            own.wait()
            dve.wait_ge(s["mamba_in"], 16 * len(mamba_loads))
            dve.wait_ge(s["mod_in"], 16 * len(mod_loads))
            cw = convw.rearrange("p (d k) -> p k d", k=TAPS)
            for k in range(TAPS):
                dve.tensor_tensor(w_taps[:, k, :], w_in[:, 0:DI], cw[:, k, :], ALU.mult)
            for m in range(HALVES):
                for r in range(3):
                    dve.tensor_copy(w_bc[:, m, :, r, :],
                                    w_x[:, m, RANK:].rearrange("p (g n) -> p g n", n=GRP))
                own.done(dve.tensor_scalar(diagD[:, m, :], ident[:], at["D"][:, m:m + 1], None, ALU.mult))
            own.wait()
            dve.sem_inc(s["prep_ok"], 1)

            dve.wait_ge(s["x_in"], 16 * NB)
            PER_BATCH = N_LN_MAMBA + 6 + 1
            with dve.Fori(0, NB) as b:
                own.enter(b, PER_BATCH)
                bb = bass.ds(b, 1)
                layer_norm(xT[:, b, :], hres, mod[:, 1, bb], mod[:, 0, bb], b * N_LN_MAMBA, "hres_ok")
                dve.wait_ge(s["hres_ok"], b + 1)
                layer_norm(hres, xn[:, TAPS - 1:], at["ln_w"], at["ln_b"], b * N_LN_MAMBA + 1, "xn_ok")
                dve.wait_ge(s["dtr_ps"], b + 1)
                dve.tensor_copy(dtr, banks(0, rows=slice(0, RANK))).then_inc(s["dtr_ok"], 1)

                def rest(g):
                    dve.wait_ge(s["bc_hi"], NG * b + g + 1)
                    dve.tensor_tensor(r1[0:3 * GRP, g % 2, :], banks([2, 4, 6, 2][g], rows=slice(0, 3 * GRP)),
                                      bcs[0:3 * GRP, g, :], ALU.subtract).then_inc(s["bc_r1"], 1)
                    dve.wait_ge(s["bc_mid"], NG * b + g + 1)
                    dve.tensor_tensor(bcs[2 * GRP:3 * GRP, g, :], r1[2 * GRP:3 * GRP, g % 2, :],
                                      bcs[2 * GRP:3 * GRP, g, :], ALU.subtract).then_inc(s["bc_ok"], 1)

                for g in range(NG):
                    rest(g)
                dve.wait_ge(s["sp_ok"], b + 1)
                own.done(dve.tensor_scalar(spT, spY, -0.25, 1.0 / 3.0, ALU.mult, ALU.add))
                own.wait()
                own.done(dve.tensor_tensor(spT, spT, spY, ALU.mult))
                own.wait()
                own.done(dve.scalar_tensor_tensor(spT, spT, -0.5, spY, ALU.add, ALU.mult))
                own.wait()
                own.done(dve.scalar_tensor_tensor(spT, spT, 1.0, spY, ALU.add, ALU.mult))
                own.wait()
                own.done(dve.scalar_tensor_tensor(spT, spL, -LN_SLACK, spT, ALU.add, ALU.max))
                own.wait()
                own.done(dve.scalar_tensor_tensor(delta, spX, 0.0, spT, ALU.max, ALU.add))
                own.wait()
                dve.tensor_tensor(du, delta, u, ALU.mult).then_inc(s["du_ok"], 1)
                dve.wait_ge(s["du_ok"], b + 1)

                def inject(par, G):
                    dve.wait_ge(s["b_ps"], G + 1)
                    dve.wait_ge(s["h_ok"], G + 1)
                    bb2 = banks(4).unsqueeze(1).broadcast_to([P, HALVES, L])
                    dve.tensor_tensor(dBu[par], du, bb2, ALU.mult).then_inc(s["dbu_ok"], 1)

                def scan(par, G):
                    dve.wait_ge(s["dbu_ok"], G + 2)
                    dve.wait_ge(s["da_ok"], G + 1)
                    dve.wait_ge(s["hc_ok"], G + 1)
                    flat = [t[par].rearrange("p a n -> p (a n)") for t in (hst, dA, dBu)]
                    dve.tensor_tensor_scan(flat[0], flat[1], flat[2], 0.0, ALU.mult, ALU.add)\
                        .then_inc(s["h_ok"], 1)

                inject(0, b * NS)
                with dve.Fori(0, GRP - 1) as i:
                    G = b * NS + 2 * i
                    inject(1, G + 1)
                    scan(0, G)
                    inject(0, G + 2)
                    scan(1, G + 1)
                G = b * NS + NS - 2
                inject(1, G + 1)
                scan(0, G)
                scan(1, G + 1)
                dve.wait_ge(s["y_acc"], NS * b + NS + 2)
                dve.tensor_tensor(zs, ps[:, 0:4, :].rearrange("p (a c) n -> p a (c n)", a=HALVES), zs, ALU.mult)\
                    .then_inc(s["gated"], 1)
                dve.wait_ge(s["mix_ps"], b + 1)
                own.done(dve.tensor_tensor(lnA[:], banks(4), hres, ALU.add))
                own.wait()
                dve.scalar_tensor_tensor(xT[:, b, :], lnA[:], gate[:, 0, bb], xT[:, b, :], ALU.mult, ALU.add)\
                    .then_inc(s["x1_ok"], 1)
                dve.wait_ge(s["x1_ok"], b + 1)
                layer_norm(xT[:, b, :], hf[:, b, :], mod[:, 4, bb], mod[:, 3, bb], b * N_LN_MAMBA + 2, "batch_ok")
                own.leave(NB)

            for name in ("masked", "halves_ok", "shifted", "qk_ok"):
                dve.sem_inc(s[name], 2)
            dve.sem_inc(s["layer_ok"], 1)
            dve.wait_ge(s["batch_ok"], NB + 1)
            dve.memset(hs_all[:, 0:WIN], 0.0)
            dve.memset(hs[DH:P, 0:1], 0.0)
            dve.memset(kT[:, :, 0:WIN], 0.0)

            def moved(b, I, nth):
                dve.tensor_copy(hs[0:DH, :], hf[0:DH, b, :])
                dve.tensor_copy(hs[DH:P, 1:L], hf[DH:P, b, 0:L - 1]).then_inc(s["hs_ok"], 1)

            def attention(I):
                def halves(st):
                    j, ch = st // 2, st % 2
                    n = QKS * I + st
                    t = 0 if j < PAIRS else 2
                    cols = slice(ch * BANK, (ch + 1) * BANK)
                    dve.wait_ge(s["sq_ok"], n + 3)
                    dve.wait_ge(s["rotated"], n + 1)
                    dve.tensor_tensor(qcos[:, st % 2, :], ps[:, 3 * (st % 2), :], tables[:, t, cols], ALU.mult)
                    dve.tensor_tensor(qsin[:, st % 2, :], ps[:, 3 * (st % 2) + 1, :], tables[:, t + 1, cols], ALU.mult)\
                        .then_inc(s["halves_ok"], 1)

                def normed(st):
                    j, ch = st // 2, st % 2
                    n = QKS * I + st
                    o = ch * BANK + (WIN if j >= PAIRS else 0)
                    dst = (kT if j >= PAIRS else qT)[:, j % PAIRS, o:o + BANK]
                    dve.wait_ge(s["rotated"], n + 3)
                    dve.wait_ge(s["inv_ok"], n + 3)
                    dve.scalar_tensor_tensor(dst, qinv[:, st % 2, :], 1e12, qrot[:, st % 2, :], ALU.min, ALU.mult)\
                        .then_inc(s["qk_ok"], 1)

                for st in range(QKS + 1):
                    if st < QKS:
                        halves(st)
                    if st >= 1:
                        normed(st - 1)

                def mask_in(g):
                    n = GROUPS * I + g
                    dve.wait_ge(s["sim_ps"], n + 1)
                    dve.wait_ge(s["exp_ok"], n + 1)
                    s3 = sc[:, g % 2, :].rearrange("p (w j) -> p w j", j=P)
                    p3 = ps[:, g % 2, :].rearrange("p (w j) -> p w j", j=P)
                    if g % QUAD == 0:
                        dve.tensor_tensor(s3[:, 0, :], p3[:, 0, :], mask[:, 1, :], ALU.add)
                    a = int(g % QUAD == 0)
                    dve.tensor_tensor(s3[:, a:, :], p3[:, a:, :],
                                      mask[:, 0:1, :].broadcast_to([P, QUAD - a, P]), ALU.add)\
                        .then_inc(s["masked"], 1)

                def row_max(g):
                    n = GROUPS * I + g
                    dve.wait_ge(s["masked"], n + 3)
                    dve.tensor_reduce(smax[:, g % 2, :], sc[:, g % 2, :].rearrange("p (w j) -> p w j", j=P),
                                      AX, ALU.max).then_inc(s["max_ok"], 1)

                def shift_in(g):
                    n = GROUPS * I + g
                    dve.wait_ge(s["max_ok"], n + 1)
                    s3 = sc[:, g % 2, :].rearrange("p (w j) -> p w j", j=P)
                    dve.tensor_tensor(s3, s3, smax[:, g % 2, :].unsqueeze(2).broadcast_to([P, QUAD, P]),
                                      ALU.subtract).then_inc(s["shifted"], 1)

                def row_sum(g):
                    n = GROUPS * I + g
                    dve.wait_ge(s["exp_ok"], n + 3)
                    dve.tensor_reduce(ssum[:, g % 2, :], ex[:, g % 2, :].rearrange("p (w j) -> p w j", j=P),
                                      AX, ALU.add).then_inc(s["sum_ok"], 1)

                def row_rec(g):
                    n = GROUPS * I + g
                    dve.wait_ge(s["sum_ok"], n + 1)
                    dve.wait_ge(s["prob_ok"], n + 1)
                    dve.reciprocal(srec[:, g % 2, :], ssum[:, g % 2, :]).then_inc(s["rsum_ok"], 1)

                for g in range(GROUPS + 1):
                    if g < GROUPS:
                        mask_in(g)
                        row_max(g)
                    if g >= 1:
                        row_sum(g - 1)
                    if g < GROUPS:
                        shift_in(g)
                    if g >= 1:
                        row_rec(g - 1)

            def feed_forward(l, b, I):
                ll = bass.ds(l, 1)
                layer_norm(hs, lnA[:], at["ln_g"][:, ll], at["ln_b2"][:, ll], NB * N_LN_MAMBA + I, "ffin_ok")
                for f, rows in enumerate(FROWS):
                    dve.wait_ge(s["gelu_ok"], FB * I + f + 1)
                    dve.scalar_tensor_tensor(ff[0:rows, f, :], banks(4 * (f % 2), rows=slice(0, rows)),
                                             b1s[0:rows, ll, 0, f],
                                             gl[0:rows, f % 2, :], ALU.add, ALU.mult).then_inc(s["ff_ok"], 1)
                dve.wait_ge(s["w2_ps"], I + 1)
                dve.scalar_tensor_tensor(hf[:, b, :], banks(4), at["b2"][:, ll], hf[:, b, :], ALU.add, ALU.add)\
                    .then_inc(s["layer_ok"], 1)

            PER_LB = 1
            with dve.Fori(0, LAYERS) as l:
                own.enter(l, PER_LB * NB)
                dve.wait_ge(s["layer_in"], 16 * N_LAYER_LOADS * (l + 1))
                dve.wait_ge(s["consts_in"], 16 * len(phase_loads))
                for t in range(4):
                    dve.tensor_scalar(tables[:, t, :], tables[:, t, :], qv[:, bass.ds(l, 1), t], None, ALU.mult)\
                        .then_inc(s["weights_ok"], 1)
                dve.wait_ge(s["weights_ok"], 6 * l + 6)
                passed(dve)
                with dve.Fori(0, NB) as b:
                    own.enter(b, PER_LB)
                    I = l * NB + b
                    dve.wait_ge(s["layer_ok"], I + 1)
                    passed(dve)
                    moved(b, I, 0)
                    attention(I)
                    dve.wait_ge(s["wo_ps"], I + 1)
                    dve.tensor_tensor(hf[:, b, :], hf[:, b, :], banks(6), ALU.add).then_inc(s["attn_ok"], 1)
                    dve.wait_ge(s["attn_ok"], I + 1)
                    passed(dve)
                    moved(b, I, 1)
                    dve.wait_ge(s["hs_ok"], 2 * I + 2)
                    feed_forward(l, b, I)
                    own.leave(NB)
                own.leave(LAYERS)
            dve.wait_ge(s["layer_ok"], LAYERS * NB + 1)
            for b in range(NB):
                dve.scalar_tensor_tensor(xT[:, b, :], hf[:, b, :], gate[:, 1, b:b + 1], xT[:, b, :],
                                         ALU.mult, ALU.add).then_inc(s["fin_ok"], 1)

        @block.gpsimd
        def _(pool):
            pool.sem_inc(s["hc_ok"], 2)
            pool.dma_start(select[0:3 * GRP], k_select).then_inc(s["select_in"], 16)
            with pool.Fori(0, NB) as b:
                with pool.Fori(0, GRP) as i:
                    for par in range(2):
                        G = b * NS + 2 * i + par
                        pool.wait_ge(s["h_ok"], G + 3)
                        pool.wait_ge(s["c_ok"], G + 2)
                        pool.wait_ge(s["y_acc"], G + 1)
                        pool.tensor_tensor(hC[par], hst[par], Csb[par].unsqueeze(1).broadcast_to([P, HALVES, L]),
                                           ALU.mult).then_inc(s["hc_ok"], 1)
            pool.sem_inc(s["rotated"], 2)
            pool.sem_inc(s["prob_ok"], 2)
            with pool.Fori(0, LAYERS) as l:
                pool.wait_ge(s["layer_in"], 16 * N_LAYER_LOADS * (l + 1))
                passed(pool)
                w4 = w_qkv[:, 0:2 * INNER].rearrange("p (h a d) -> p h a d", a=2, d=DH // 2)
                r4 = w_rot.rearrange("p (h a d) -> p h a d", a=2, d=DH // 2)
                for a in range(2):
                    pool.tensor_copy(r4[:, :, a, :], w4[:, :, 1 - a, :]).then_inc(s["weights_ok"], 1)
                with pool.Fori(0, NB) as b:
                    I = l * NB + b
                    for st in range(QKS):
                        n = QKS * I + st
                        pool.wait_ge(s["halves_ok"], n + 3)
                        pool.wait_ge(s["qk_ok"], n + 1)
                        pool.tensor_tensor(qrot[:, st % 2, :], qcos[:, st % 2, :], qsin[:, st % 2, :], ALU.add)\
                            .then_inc(s["rotated"], 1)
                    for g in range(GROUPS):
                        n = GROUPS * I + g
                        pool.wait_ge(s["rsum_ok"], n + 1)
                        pool.wait_ge(s["pt_ps"], n + 1)
                        pool.tensor_tensor(pr[:, g % 2, :].rearrange("p (w j) -> p w j", j=P),
                                           ex[:, g % 2, :].rearrange("p (w j) -> p w j", j=P),
                                           srec[:, g % 2, :].unsqueeze(2).broadcast_to([P, QUAD, P]),
                                           ALU.mult).then_inc(s["prob_ok"], 1)


def columns(v):
    return np.ascontiguousarray(v.reshape(-1, P).T)


def packed_vectors(a):
    half = DH // 2
    qk = []
    for l in range(LAYERS):
        for name in ("L0_ffn_q_scale", "L0_ffn_k_scale"):
            v = a[name][l]
            qk += [np.tile(v, 2), np.tile(np.concatenate([v[half:], v[:half]]), 2)]
    b1 = np.zeros((LAYERS, 2, FB, P), np.float32)
    for part in range(2):
        for f, rows in enumerate(FROWS):
            b1[:, part, f, :rows] = a["L0_ffn_b1"][:, part * HID + f * P:part * HID + f * P + rows]
    named = {"ln_w": a["L0_attn_ln_w"], "ln_b": a["L0_attn_ln_b"], "c": a["L0_c"], "conv_b": a["L0_attn_conv_b"],
             "b_dt": a["L0_attn_b_dt"], "D": a["L0_attn_D"], "qk": np.stack(qk), "ln_g": a["L0_ffn_ln_g"],
             "ln_b2": a["L0_ffn_ln_b"], "b2": a["L0_ffn_b2"], "b1": b1}
    return np.concatenate([columns(named[n]) for n in VECS], 1)


def constants():
    ident = np.eye(P, dtype=np.float32)
    ones = np.full((P, P), 1.0 / P, np.float32)
    blocks = np.kron(np.eye(2), np.ones((DH, DH))).astype(np.float32)
    select = np.zeros((3 * GRP, GRP, P), np.float32)
    for r in range(3 * GRP):
        select[r, r % GRP] = 1.0
    no = np.float32(-3.0e38)
    i, j = np.arange(WIN)[:, None], np.arange(WIN)[None, :]
    own = np.where(j <= i, np.float32(0), no)
    prev = np.where(j >= i, np.float32(0), no)
    mask = np.stack([np.concatenate([prev, own], 1), np.concatenate([np.full_like(own, no), own], 1)], 1)
    mask = np.concatenate([mask, mask], 0).astype(np.float32)
    half = np.arange(0, DH, 2, dtype=np.float32)
    freq = np.float32(1.0) / np.float32(10000.0) ** (half / np.float32(DH))
    t = np.arange(L, dtype=np.float32)
    angle = t[:, None] * freq[None, :]
    base = (half + np.float32(0.4 * DH)) / np.float32(1.4 * DH)
    power = (t - L // 2) / np.float32(WIN // 2)
    scale = base[None, :] ** power[:, None]
    angle, scale = (np.concatenate([a, a], 1).T for a in (angle, scale))
    sign = np.where(np.arange(DH) < DH // 2, -1.0, 1.0).astype(np.float32)[:, None]
    cos, sin = np.cos(angle), np.sin(angle) * sign
    tables = np.stack([cos * scale * 8, sin * scale * 8, cos / scale, sin / scale], 1)
    tables = np.concatenate([tables, tables], 0).astype(np.float32)
    return {"k_ident": ident, "k_ones": ones, "k_blocks": blocks, "k_select": select, "k_mask": mask,
            "k_tables": tables}


def kernel(**inputs):
    import concourse.bacc as bacc
    from concourse.bass_utils import run_bass_kernel_spmd

    nc = bacc.Bacc("TRN2", target_bir_lowering=False, num_devices=1)
    a = {n: np.asarray(v) for n, v in inputs.items()}
    arrays = {"x": np.ascontiguousarray(a["L0_attn_x"].transpose(2, 0, 1)), "vecs": packed_vectors(a)}
    for n in ("attn_W_in", "attn_conv_w", "attn_W_xproj", "attn_W_dt", "attn_A_log", "attn_W_out",
              "ffn_wqkv", "ffn_wo", "ffn_w1", "ffn_w2", "wmod"):
        arrays[n] = np.ascontiguousarray(a["L0_" + n])
    arrays.update(constants())
    args = [nc.dram_tensor("in_" + n, a.shape, mybir.dt.from_np(a.dtype), kind="ExternalInput").ap()
            for n, a in arrays.items()]
    y = nc.dram_tensor("out_y", (D, NB, L), F32, kind="ExternalOutput").ap()
    adaln_block(nc, *args, y)
    r = run_bass_kernel_spmd(nc, [{"in_" + n: a for n, a in arrays.items()}], core_ids=[0])
    return np.ascontiguousarray(r.results[0]["out_y"].transpose(1, 2, 0))
```

```python
from contextlib import ExitStack

import numpy as np

import concourse.bass as bass
from concourse import mybir

F32 = mybir.dt.float32
BF16 = mybir.dt.bfloat16
ALU = mybir.AluOpType
ACT = mybir.ActivationFunctionType
AX = mybir.AxisListType.X

P = 128
NB = 4
L = 1024
BANK = 512
NC2 = L // BANK
D = 128
HALVES = 2
DI = HALVES * P
NS = 64
TAPS = 4
RANK = D // 16
GRP = 32
NG = 2 * NS // GRP
LAYERS = 2
HEADS = 8
DH = 64
WIN = 64
NW = L // WIN
PAIRS = HEADS // 2
INNER = HEADS * DH
HID = int(D * 4 * 2 / 3)
FB = 3
FROWS = [min(P, HID - P * f) for f in range(FB)]
TOK = L // P
BLOCKS = 2 * PAIRS
STEPS = NC2 * BLOCKS
QUAD = 4
GROUPS = PAIRS * NW // QUAD
CQ = NW // NC2
TILES = BANK // P
LAG = 3
EPS = 1e-5
GELU = "gelu_and_others"
EXP = "exp_and_others"
LOG = "natural_log"
LN2 = float(np.log(2.0))
NORM_SHIFT = 20
LN_SLACK = 2e-7


class Steps:

    def __init__(self, eng, sem):
        self.eng, self.sem, self.base, self.k, self.outer = eng, sem, 0, 0, []

    def done(self, inst):
        inst.then_inc(self.sem, 1)
        self.k += 1

    def wait(self):
        self.eng.wait_ge(self.sem, self.base + self.k)

    def enter(self, var, per):
        self.outer.append((self.base, self.k, per))
        self.base, self.k = self.base + self.k + var * per, 0

    def leave(self, times):
        base, k, per = self.outer.pop()
        assert self.k == per, (self.k, per)
        self.base, self.k = base, k + per * times


FFN_AT = {0: ("dev", 0, 0), 1: ("var", 0, 0), 2: ("norm", 0, 0), 3: ("ag", 0, 0), 4: ("ag", 0, 1),
          5: ("ag", 0, 2), 6: ("dev", 1, 0), 7: ("var", 1, 0), 8: ("norm", 1, 0), 9: ("w2", 0, 0),
          10: ("ag", 1, 0), 11: ("ag", 1, 1), 12: ("ag", 1, 2), 15: ("w2", 1, 0)}
GELU_AT = {6: 0, 13: 1}
WO_AT = 11
NORM_AT = (8, 10, 11)
INV_AT = (13, 14, 15, 16)
FINAL_AT = {3: (0,), 4: (1, 2), 5: (3,), 6: (4,), 7: (5,), 8: (6,), 9: (7,)}

VECS = {"ln_w": 1, "ln_b": 1, "c": NB, "conv_b": HALVES, "b_dt": HALVES, "D": HALVES, "qk": 4 * LAYERS,
        "ln_g": LAYERS, "ln_b2": LAYERS, "b2": LAYERS, "b1": 2 * FB * LAYERS}


def adaln_block(nc, x, vecs, W_in, conv_w, W_xproj, W_dt, A_log, W_out, wqkv, wo, w1, w2, wmod,
                k_ident, k_centre, k_heads, k_spread, k_select, k_mask, k_tables, out):
    with ExitStack() as ctx:
        def sb(name, shape, dt=F32):
            return ctx.enter_context(nc.sbuf_tensor(name, shape, dt))

        def sem(name):
            return ctx.enter_context(nc.semaphore(name))

        ps = ctx.enter_context(nc.psum_tensor("ps", [P, 8, BANK], F32))

        def banks(first, n=NC2, rows=slice(0, P)):
            return ps[rows, first:first + n, :].rearrange("p a b -> p (a b)")

        ident = sb("ident", [P, P])
        centre = sb("centre", [P, P])
        mean_col = sb("mean_col", [P, 1])
        ln_var = sb("ln_var", [P, NC2, TILES])
        rstd = sb("rstd", [P, NC2, TILES])
        minus_half = sb("minus_half", [P, 1])
        hf = sb("hf", [P, NB, L])
        lnA = sb("lnA", [P, L])
        lnB = sb("lnB", [P, L])
        lnC = sb("lnC", [P, L])
        mod = sb("mod", [P, 6, NB])
        gate = sb("gate", [P, 2, NB])
        gtmp = sb("gtmp", [P, 2, 2, NB])
        silu_c = sb("silu_c", [P, NB])
        vec_s = sb("vec_s", [P, sum(VECS.values())])
        at, col = {}, 0
        for name, width in VECS.items():
            at[name], col = vec_s[:, col:col + width], col + width
        qv = at["qk"].rearrange("p (l a) -> p l a", a=4)
        b1s = at["b1"].rearrange("p (l a f) -> p l a f", a=2, f=FB)
        epsv = sb("epsv", [P, 4])

        ARENA = 44100
        arena = sb("arena", [P, ARENA])
        used = [0]

        def carve(n):
            a = arena[:, used[0]:used[0] + n]
            used[0] += n
            assert used[0] <= ARENA, used[0]
            return a

        def carve3(a, n):
            return carve(a * n).rearrange("p (a n) -> p a n", a=a)

        select = carve(GRP * P // 2).bitcast(BF16).rearrange("p (a n) -> p a n", a=GRP)
        bcs = carve(NG * L // 2).bitcast(BF16).rearrange("p (g n) -> p g n", g=NG)
        u = carve3(HALVES, L)
        zs = carve3(HALVES, L)
        delta = carve3(HALVES, L)
        du = carve3(HALVES, L)
        dA = [carve3(HALVES, L) for _ in range(2)]
        dBu = [carve3(HALVES, L) for _ in range(2)]
        hst = [carve3(HALVES, L) for _ in range(2)]
        hC = [carve3(HALVES, L) for _ in range(2)]
        Csb = [carve(L) for _ in range(2)]
        hres = carve(L)
        xn = carve(L + TAPS - 1)
        xT = carve3(NB, L)
        wmod_s = hC[0].rearrange("p a n -> p (a n)")[:, 0:6 * D]
        w_in = carve(2 * DI)
        convw = hC[1].rearrange("p a n -> p (a n)")[:, 0:DI * TAPS]
        w_taps = carve3(TAPS, DI)
        A = carve3(HALVES, NS)
        w_x = carve3(HALVES, RANK + 2 * NS)
        w_bc = carve(HALVES * NG * 3 * GRP).rearrange("p (m g r n) -> p m g r n", m=HALVES, g=NG, r=3)
        w_dt = carve(DI)
        w_out = carve3(HALVES, D)
        diagD = carve3(HALVES, P)
        dtr = lnB[0:RANK, :]
        spY, spL, spX, spT, r1 = dBu[0], dBu[1], hst[0], hst[1], hC[0]

        used[0] = 0
        w_qkv = carve(3 * INNER)
        w_rot = carve(2 * INNER)
        w_o = carve3(PAIRS, D)
        w_1 = carve(2 * HID)
        w_2 = carve3(FB, D)
        heads = carve3(BLOCKS, 3 * GRP)
        unhead = carve(BLOCKS * P // 2).bitcast(BF16).rearrange("p (a n) -> p a n", a=BLOCKS)
        mask = carve3(2, 2 * WIN)
        tables = carve3(4, L)
        gbuf = carve(FB * BANK)
        hs_all = gbuf[:, 0:WIN + L]
        hs = hs_all[:, WIN:]
        abuf = carve(PAIRS * BANK)
        qraw = [t.rearrange("p (a n) -> p a n", a=PAIRS) for t in (abuf, carve(PAIRS * BANK))]
        qbd = carve(PAIRS * NW * P).rearrange("p (a w n) -> p a w n", a=PAIRS, w=NW)
        kT = carve(PAIRS * (L + WIN)).rearrange("p (a n) -> p a n", a=PAIRS)
        vtok = carve3(NW, INNER)
        oT = carve3(PAIRS, BANK)
        qcos = carve3(2, BANK)
        qsin = carve3(2, BANK)
        qsq = carve3(2, BANK)
        sc, ex, pT = qcos, qsin, qsq
        pr = carve3(2, BANK)
        nlog = carve(BANK)
        ninv = carve(BANK)
        nrest = nlog
        nparts = carve(BANK // 2).bitcast(BF16)
        smax = carve3(2, QUAD)
        ssum = carve3(2, QUAD)
        srec = carve3(2, QUAD)
        xend = qbd.rearrange("p a w n -> p (a w n)")[:, 0:NB * L].rearrange("p (b n) -> p b n", b=NB)
        fs = lnA
        fdev, fsq = lnB[:, 0:BANK], lnB[:, BANK:]
        fnorm, fin = lnC[:, 0:BANK], lnC[:, BANK:]
        x1_dram = nc.dram_tensor("x1_parked", (P, NB, L), F32, kind="Internal").ap()

        names = """consts_in mod_in mamba_in select_in silu_c mod_ps mod_sb consts_ok prep_ok a_ok
            x_in ln_dev ln_sq ln_var_ps ln_eps ln_rstd ln_bc hres_ok xn_ok xc_ps z_ps u_ok zs_ok
            dtr_ps dtr_ok bc_ps bc_hi bc_r1 bc_mid bc_ok dt_ps sp_ok du_ok
            b_ps dbu_ok c_ps c_ok da_ok h_ok hc_ok y_acc gated mix_ps x1_ok batch_ok
            attn_in ffn_in weights_ok hs_ok v_ps v_ok qk_ps sq_ok ss_ps halves_ok raw_ok
            norm_log norm_exp norm_min norm_hi norm_rest norm_mid norm_ok inv_ps qk_ok
            sim_ps masked max_ok shifted exp_ok sum_ok rsum_ok prob_ok pt_ps pt_ok o_ps o_ok wo_ps attn_ok fs_ok
            f_dev f_sq f_kept f_var f_eps f_rstd f_bc f_norm f_in ag_ps av_ok g_ok gelu_ok ff_ok w2_ps f_out
            parked x1_back end_ok stored
            vec_step act_step pool_step marks""".split()
        s = {n: sem(n) for n in names}

        mod_loads = [(vec_s[:], vecs), (wmod_s, wmod), (centre[:], k_centre), (ident[:], k_ident)]
        mamba_loads = [(w_in, W_in),
                       (convw, conv_w.rearrange("d o k -> o (d k)").broadcast_to([P, DI * TAPS])),
                       (A, A_log.rearrange("(m p) n -> p m n", p=P)),
                       (w_x, W_xproj.rearrange("(m p) n -> p m n", p=P)),
                       (w_dt[0:RANK], W_dt),
                       (w_out, W_out.rearrange("(m p) n -> p m n", p=P))]
        phase_loads = [(heads, k_heads), (mask, k_mask)]

        def attn_loads(l):
            return [(w_qkv, wqkv[l]), (tables, k_tables)]

        def ffn_loads(l):
            full = (FB - 1) * P
            return [(w_o, wo[l].rearrange("(a p) n -> p a n", p=P)),
                    (w_1, w1[l]),
                    (w_2[:, 0:FB - 1, :], w2[l, 0:full].rearrange("(a p) n -> p a n", p=P)),
                    (w_2[0:FROWS[-1], FB - 1, :], w2[l, full:HID])]

        N_ATTN, N_FFN = len(attn_loads(0)), len(ffn_loads(0))

        def passed(eng):
            eng.sem_inc(s["marks"], 1)

        def table(act, name):
            passed(act)
            act.preload_act_table_set(name)

        block = ctx.enter_context(nc.Block())

        N_LN_MAMBA = 3

        @block.sync
        def _(sp):
            for dst, src in mod_loads:
                sp.dma_start(dst, src).then_inc(s["mod_in"], 16)
            for b in range(NB):
                sp.dma_start(xT[:, b, :], x[:, b, :]).then_inc(s["x_in"], 16)
            for dst, src in mamba_loads:
                sp.dma_start(dst, src).then_inc(s["mamba_in"], 16)
            for b in range(NB):
                sp.wait_ge(s["x1_ok"], b + 1)
                sp.dma_start(x1_dram[:, b, :], xT[:, b, :]).then_inc(s["parked"], 16)
            sp.wait_ge(s["batch_ok"], NC2 * NB + 1)
            sp.wait_ge(s["parked"], 16 * NB)
            for dst, src in phase_loads:
                sp.dma_start(dst, src).then_inc(s["consts_in"], 16)
            for l in range(LAYERS):
                if l:
                    sp.wait_ge(s["ss_ps"], STEPS * NB * l + 2)
                    sp.wait_ge(s["halves_ok"], STEPS * NB * l + 2)
                    sp.wait_ge(s["v_ps"], NW * NB * l)
                for dst, src in attn_loads(l):
                    sp.dma_start(dst, src).then_inc(s["attn_in"], 16)
                if l:
                    sp.wait_ge(s["f_out"], NC2 * NB * l + 1)
                for dst, src in ffn_loads(l):
                    sp.dma_start(dst, src).then_inc(s["ffn_in"], 16)
            sp.wait_ge(s["attn_ok"], NC2 * LAYERS * NB)
            sp.dma_start(xend, x1_dram).then_inc(s["x1_back"], 16)
            for b in range(NB):
                sp.wait_ge(s["end_ok"], b + 1)
                sp.dma_start(out[:, b, :], xend[:, b, :]).then_inc(s["stored"], 16)
            sp.wait_ge(s["stored"], 16 * NB)

        @block.tensor
        def _(pe):
            def variances(bank, squares, t0):
                for t in range(TILES):
                    mm = pe.matmul(ps[:, bank, t:t + 1], squares[:, t0 + t * P:t0 + (t + 1) * P], mean_col[:],
                                   start=True, stop=True)
                return mm

            def on_all_rows(bank, ch):
                for t in range(TILES):
                    mm = pe.matmul(ps[:, bank, t * P:(t + 1) * P], rstd[:, ch, t:t + 1].broadcast_to([P, P]),
                                   ident[:], start=True, stop=True)
                return mm

            def layer_norm(src, q, ready=None):
                for ch in range(NC2):
                    if ready is not None:
                        pe.wait_ge(s["hres_ok"], ready + ch)
                    pe.matmul(ps[:, 4 + ch, :], centre[:], src(ch), start=True, stop=True)\
                        .then_inc(s["ln_dev"], 1)
                for ch in range(NC2):
                    pe.wait_ge(s["ln_sq"], NC2 * q + ch + 1)
                    variances(6 + ch, lnB, ch * BANK).then_inc(s["ln_var_ps"], 1)
                for ch in range(NC2):
                    pe.wait_ge(s["ln_rstd"], NC2 * q + ch + 1)
                    on_all_rows(6 + ch, ch).then_inc(s["ln_bc"], 1)

            def chunk(ap, ch):
                return ap[:, ch * BANK:(ch + 1) * BANK]

            pe.wait_ge(s["silu_c"], 1)
            for j in range(6):
                mm = pe.matmul(ps[:, 7, j * NB:(j + 1) * NB], wmod_s[:, j * D:(j + 1) * D], silu_c[:],
                               start=True, stop=True)
            mm.then_inc(s["mod_ps"], 1)
            pe.wait_ge(s["x_in"], 16 * NB)
            for name in ("y_acc", "ss_ps", "pt_ps", "o_ps"):
                pe.sem_inc(s[name], 2)
            pe.wait_ge(s["select_in"], 16)
            pe.wait_ge(s["prep_ok"], 1)
            with pe.Fori(0, NB) as b:
                pe.wait_ge(s["batch_ok"], NC2 * b + 1)
                layer_norm(lambda ch: xT[:, b, ch * BANK:(ch + 1) * BANK], b * N_LN_MAMBA)
                layer_norm(lambda ch: chunk(hres, ch), b * N_LN_MAMBA + 1, NC2 * b + 1)
                pe.wait_ge(s["xn_ok"], NC2 * (b + 1))
                for m in range(HALVES):
                    for ch in range(NC2):
                        for k in range(TAPS):
                            mm = pe.matmul(ps[:, 2 * m + ch, :], w_taps[:, k, m * P:(m + 1) * P],
                                           xn[:, ch * BANK + k:ch * BANK + k + BANK],
                                           start=(k == 0), stop=(k == TAPS - 1))
                    mm.then_inc(s["xc_ps"], 1)
                for m in range(HALVES):
                    for ch in range(NC2):
                        o = ch * BANK + TAPS - 1
                        mm = pe.matmul(ps[:, 4 + 2 * m + ch, :], w_in[:, DI + m * P:DI + (m + 1) * P],
                                       xn[:, o:o + BANK], start=True, stop=True)
                    mm.then_inc(s["z_ps"], 1)
                pe.wait_ge(s["u_ok"], HALVES * b + HALVES)
                for ch in range(NC2):
                    for m in range(HALVES):
                        mm = pe.matmul(ps[0:RANK, ch, :], w_x[:, m, 0:RANK], chunk(u[:, m, :], ch),
                                       start=(m == 0), stop=(m == HALVES - 1))
                mm.then_inc(s["dtr_ps"], 1)

                def spread(g, first):
                    for ch in range(NC2):
                        for m in range(HALVES):
                            mm = pe.matmul(ps[0:3 * GRP, first + ch, :],
                                           w_bc[:, m, g, :, :].rearrange("p r n -> p (r n)"),
                                           chunk(u[:, m, :], ch), start=(m == 0), stop=(m == HALVES - 1))
                    mm.then_inc(s["bc_ps"], 1)

                def dt_proj(m, first):
                    for ch in range(NC2):
                        mm = pe.matmul(ps[:, first + ch, :], w_dt[0:RANK, m * P:(m + 1) * P],
                                       chunk(dtr, ch), start=True, stop=True)
                    mm.then_inc(s["dt_ps"], 1)

                spread(0, 2)
                pe.wait_ge(s["zs_ok"], HALVES * b + HALVES)
                spread(1, 4)
                spread(2, 6)
                pe.wait_ge(s["dtr_ok"], b + 1)
                dt_proj(0, 0)
                pe.wait_ge(s["bc_r1"], NG * b + 1)
                spread(3, 2)
                pe.wait_ge(s["bc_r1"], NG * b + 2)
                dt_proj(1, 4)
                pe.wait_ge(s["du_ok"], b + 1)
                for m in range(HALVES):
                    for ch in range(NC2):
                        pe.matmul(ps[:, 2 * m + ch, :], diagD[:, m, :], chunk(u[:, m, :], ch),
                                  start=True, stop=False, skip_group_check=True)

                def spread_b(n, par, G):
                    pe.wait_ge(s["dbu_ok"], G + 1)
                    for ch in range(NC2):
                        mm = pe.matmul(ps[:, 4 + ch, :], select[0:3 * GRP, n, :],
                                       bcs[0:3 * GRP, par, ch * BANK:(ch + 1) * BANK], start=True, stop=True)
                    mm.then_inc(s["b_ps"], 1)

                def spread_c(n, par, G):
                    pe.wait_ge(s["c_ok"], G + 1)
                    for ch in range(NC2):
                        mm = pe.matmul(ps[:, 6 + ch, :], select[0:3 * GRP, n, :],
                                       bcs[0:3 * GRP, 2 + par, ch * BANK:(ch + 1) * BANK], start=True, stop=True)
                    mm.then_inc(s["c_ps"], 1)

                def sum_states(par, G):
                    pe.wait_ge(s["hc_ok"], G + 3)
                    for m in range(HALVES):
                        for ch in range(NC2):
                            mm = pe.matmul(ps[:, 2 * m + ch, :], ident[:], chunk(hC[par][:, m, :], ch),
                                           start=False, stop=False, skip_group_check=True)
                    mm.then_inc(s["y_acc"], 1)

                for G in range(LAG):
                    spread_b(G // 2, G % 2, b * NS + G)
                    spread_c(G // 2, G % 2, b * NS + G)
                with pe.Fori(1, GRP - 1) as i:
                    G = b * NS + 2 * i + 1
                    spread_b(i, 1, G)
                    spread_c(i, 1, G)
                    sum_states(0, G - LAG)
                    spread_b(i + 1, 0, G + 1)
                    spread_c(i + 1, 0, G + 1)
                    sum_states(1, G + 1 - LAG)
                G = b * NS + NS - 1
                spread_b(GRP - 1, 1, G)
                spread_c(GRP - 1, 1, G)
                for k in range(LAG + 1):
                    sum_states((NS - 1 - LAG + k) % 2, G - LAG + k)
                pe.wait_ge(s["gated"], b + 1)
                for ch in range(NC2):
                    for m in range(HALVES):
                        mm = pe.matmul(ps[:, 4 + ch, :], w_out[:, m, :], chunk(zs[:, m, :], ch),
                                       start=(m == 0), stop=(m == HALVES - 1))
                mm.then_inc(s["mix_ps"], 1)
                pe.wait_ge(s["x1_ok"], b + 1)
                layer_norm(lambda ch: xT[:, b, ch * BANK:(ch + 1) * BANK], b * N_LN_MAMBA + 2)

            def project(I, st):
                ch, j = st // BLOCKS, st % BLOCKS
                col = (j % 2) * INNER + (j // 2) * P
                pe.wait_ge(s["halves_ok"], STEPS * I + st + 1)
                pe.matmul(ps[:, st % 2, :], w_qkv[:, col:col + P], chunk(hs, ch), start=True, stop=True)
                pe.matmul(ps[:, 2 + st % 2, :], w_rot[:, col:col + P], chunk(hs, ch),
                          start=True, stop=True).then_inc(s["qk_ps"], 1)

            def values(I, t):
                pe.wait_ge(s["v_ok"], NW * I + t + 1)
                pe.matmul(ps[:, 6 + t % 2, :], hs_all[:, t * WIN:t * WIN + P], w_qkv[:, 2 * INNER:],
                          start=True, stop=True).then_inc(s["v_ps"], 1)

            def norms(I, st):
                ch, j = st // BLOCKS, st % BLOCKS
                if j == 0 and ch:
                    pe.wait_ge(s["norm_log"], NC2 * I + ch)
                pe.wait_ge(s["sq_ok"], STEPS * I + st + 3)
                pe.matmul(ps[0:3 * GRP, 4, :], heads[:, j, :], qsq[:, st % 2, :],
                          start=(j == 0), stop=(j == BLOCKS - 1)).then_inc(s["ss_ps"], 1)

            def inverse(I, f):
                ch, j = f // BLOCKS, f % BLOCKS
                pe.wait_ge(s["norm_ok"], NC2 * I + ch + 1)
                pe.wait_ge(s["qk_ok"], STEPS * I + f + 1)
                pe.matmul(ps[:, 5, :], unhead[0:3 * GRP, j, :], nparts[0:3 * GRP, :],
                          start=True, stop=True).then_inc(s["inv_ps"], 1)

            def scores(I, g):
                quad, hp = g // PAIRS, g % PAIRS
                ch = quad * QUAD // CQ
                pe.wait_ge(s["masked"], GROUPS * I + g + 1)
                pe.wait_ge(s["qk_ok"], STEPS * I + ch * BLOCKS + 2 * hp + 3)
                for i in range(QUAD):
                    w = quad * QUAD + i
                    mm = pe.matmul(ps[:, g % 2, i * P:(i + 1) * P], qbd[:, hp, w, :],
                                   kT[:, hp, w * WIN:(w + 2) * WIN], start=True, stop=True)
                mm.then_inc(s["sim_ps"], 1)

            def turn(I, g):
                n = GROUPS * I + g
                pe.wait_ge(s["prob_ok"], n + 3)
                pe.wait_ge(s["pt_ok"], n + 1)
                for i in range(QUAD):
                    mm = pe.transpose(ps[:, 2 + g % 2, i * P:(i + 1) * P], pr[:, g % 2, i * P:(i + 1) * P],
                                      ident[:])
                mm.then_inc(s["pt_ps"], 1)

            def weigh(I, g):
                quad, hp = g // PAIRS, g % PAIRS
                n = GROUPS * I + g
                pe.wait_ge(s["pt_ok"], n + 3)
                pe.wait_ge(s["o_ok"], n + 1)
                for i in range(QUAD):
                    mm = pe.matmul(ps[:, 4, i * P:(i + 1) * P], vtok[:, quad * QUAD + i, hp * P:(hp + 1) * P],
                                   pT[:, g % 2, i * P:(i + 1) * P], start=True, stop=True)
                mm.then_inc(s["o_ps"], 1)

            def out_proj(I, ch, bank):
                pe.wait_ge(s["o_ok"], GROUPS * I + (ch + 1) * GROUPS // NC2 + 1)
                for hp in range(PAIRS):
                    mm = pe.matmul(ps[:, bank, :], w_o[:, hp, :], oT[:, hp, :],
                                   start=(hp == 0), stop=(hp == PAIRS - 1))
                mm.then_inc(s["wo_ps"], 1)

            def ffn_piece(J, step):
                if step not in FFN_AT:
                    return
                what, ch, f = FFN_AT[step]
                K = NC2 * J + ch
                if what == "dev":
                    pe.wait_ge(s["fs_ok"], J + 1)
                    if ch:
                        pe.wait_ge(s["av_ok"], FB * K)
                    pe.matmul(ps[:, 6, :], centre[:], chunk(fs, ch), start=True, stop=True).then_inc(s["f_dev"], 1)
                if what == "var":
                    if ch:
                        pe.wait_ge(s["g_ok"], FB * K)
                    pe.wait_ge(s["f_sq"], K + 1)
                    variances(7, fsq, 0).then_inc(s["f_var"], 1)
                if what == "norm":
                    pe.wait_ge(s["f_rstd"], K + 1)
                    on_all_rows(7, ch).then_inc(s["f_bc"], 1)
                if what == "ag":
                    rows, o = FROWS[f], f * P
                    pe.wait_ge(s["f_in"], K + 1)
                    if f:
                        pe.wait_ge(s["av_ok"], FB * K + f)
                        pe.wait_ge(s["g_ok"], FB * K + f)
                    elif ch:
                        pe.wait_ge(s["f_out"], K + 1)
                    pe.matmul(ps[0:rows, 6, :], w_1[:, o:o + rows], fin, start=True, stop=True)
                    pe.matmul(ps[0:rows, 7, :], w_1[:, HID + o:HID + o + rows], fin,
                              start=True, stop=True).then_inc(s["ag_ps"], 1)
                if what == "w2":
                    pe.wait_ge(s["ff_ok"], K + 2)
                    if not ch:
                        pe.wait_ge(s["f_in"], K + 2)
                    for f, rows in enumerate(FROWS):
                        mm = pe.matmul(ps[:, 6, :], w_2[0:rows, f, :], abuf[0:rows, f * BANK:(f + 1) * BANK],
                                       start=(f == 0), stop=(f == FB - 1))
                    mm.then_inc(s["w2_ps"], 1)

            def body(I, J):
                pe.wait_ge(s["hs_ok"], I + 1)
                pe.wait_ge(s["pt_ok"], GROUPS * I + 2)
                for st in range(STEPS + 1):
                    if st < STEPS:
                        project(I, st)
                    if st == 1 and J is not None:
                        pe.wait_ge(s["attn_ok"], NC2 * J + 1)
                        out_proj(J, 1, 5)
                    if st in INV_AT:
                        if st == min(INV_AT) and J is not None:
                            pe.wait_ge(s["attn_ok"], NC2 * J + 2)
                        inverse(I, 2 * (st - min(INV_AT)))
                    if st < NW:
                        values(I, st)
                    if st >= 1:
                        norms(I, st - 1)
                    if st in INV_AT:
                        inverse(I, 2 * (st - min(INV_AT)) + 1)
                pe.wait_ge(s["v_ok"], NW * (I + 1) + 2)
                scores(I, 0)
                for g in range(GROUPS + 3):
                    for j in FINAL_AT.get(g, ())[:1]:
                        inverse(I, BLOCKS + j)
                    if g + 1 < GROUPS:
                        scores(I, g + 1)
                    if g == WO_AT:
                        pe.wait_ge(s["qk_ok"], STEPS * (I + 1) + 1)
                        out_proj(I, 0, 5)
                    if 2 <= g < GROUPS + 2:
                        turn(I, g - 2)
                    if g >= 3:
                        weigh(I, g - 3)
                    for j in FINAL_AT.get(g, ())[1:]:
                        inverse(I, BLOCKS + j)
                    if J is not None:
                        ffn_piece(J, g)

            pe.wait_ge(s["select_in"], 32)
            with pe.Fori(0, LAYERS) as l:
                pe.wait_ge(s["weights_ok"], 6 * l + 6)
                pe.wait_ge(s["ffn_in"], 16 * N_FFN * (l + 1))
                body(l * NB, None)
                passed(pe)
                with pe.Fori(1, NB) as b:
                    body(l * NB + b, l * NB + b - 1)
                J = l * NB + NB - 1
                pe.wait_ge(s["attn_ok"], NC2 * J + 1)
                out_proj(J, 1, 5)
                for step in range(GROUPS):
                    ffn_piece(J, step)

        @block.scalar
        def _(act):
            own = Steps(act, s["act_step"])

            def layer_norm(q):
                for ch in range(NC2):
                    act.wait_ge(s["ln_dev"], NC2 * q + ch + 1)
                    act.activation(lnB[:, ch * BANK:(ch + 1) * BANK], ps[:, 4 + ch, :], ACT.Square)\
                        .then_inc(s["ln_sq"], 1)
                for ch in range(NC2):
                    act.wait_ge(s["ln_var_ps"], NC2 * q + ch + 1)
                    act.activation(ln_var[:, ch, :], ps[:, 6 + ch, 0:TILES], ACT.Identity, bias=epsv[:, 0:1])\
                        .then_inc(s["ln_eps"], 1)

            act.sem_inc(s["c_ok"], 1)
            act.wait_ge(s["mod_in"], 16 * len(mod_loads))
            act.activation(silu_c[:], at["c"], ACT.Silu).then_inc(s["silu_c"], 1)
            act.wait_ge(s["mamba_in"], 16 * len(mamba_loads))
            table(act, EXP)
            own.done(act.activation(A, A, ACT.Exp))
            own.wait()
            act.mul(A, A, -1.0).then_inc(s["a_ok"], 1)
            act.wait_ge(s["consts_ok"], 1)
            act.wait_ge(s["a_ok"], 1)
            PER_BATCH = 3 * HALVES
            with act.Fori(0, NB) as b:
                own.enter(b, PER_BATCH)
                layer_norm(b * N_LN_MAMBA)
                layer_norm(b * N_LN_MAMBA + 1)
                for m in range(HALVES):
                    act.wait_ge(s["xc_ps"], HALVES * b + m + 1)
                    act.activation(u[:, m, :], banks(2 * m), ACT.Silu, bias=at["conv_b"][:, m:m + 1]).then_inc(s["u_ok"], 1)
                for m in range(HALVES):
                    act.wait_ge(s["z_ps"], HALVES * b + m + 1)
                    act.activation(zs[:, m, :], banks(4 + 2 * m), ACT.Silu).then_inc(s["zs_ok"], 1)
                table(act, EXP)

                def parts(g):
                    act.wait_ge(s["bc_ps"], NG * b + g + 1)
                    act.copy(bcs[0:3 * GRP, g, :], banks([2, 4, 6, 2][g], rows=slice(0, 3 * GRP)))\
                        .then_inc(s["bc_hi"], 1)
                    act.wait_ge(s["bc_r1"], NG * b + g + 1)
                    act.copy(bcs[GRP:2 * GRP, g, :], r1[GRP:2 * GRP, g % 2, :])
                    act.copy(bcs[2 * GRP:3 * GRP, g, :], r1[2 * GRP:3 * GRP, g % 2, :]).then_inc(s["bc_mid"], 1)

                def softplus(m):
                    act.wait_ge(s["dt_ps"], HALVES * b + m + 1)
                    own.done(act.activation(spX[:, m, :], banks(4 * m), ACT.Identity, bias=at["b_dt"][:, m:m + 1]))
                    own.wait()
                    own.done(act.activation(spY[:, m, :], spX[:, m, :], ACT.Abs))
                    own.wait()
                    own.done(act.activation(spY[:, m, :], spY[:, m, :], ACT.Exp, scale=-1.0))
                    own.wait()


                parts(0)
                parts(1)
                softplus(0)
                parts(2)
                parts(3)
                softplus(1)
                table(act, LOG)
                act.activation(spL, spY, ACT.Ln, bias=epsv[:, 1:2]).then_inc(s["sp_ok"], 1)

                def state(n, par, G):
                    act.wait_ge(s["h_ok"], G + 1)
                    for m in range(HALVES):
                        e = act.activation(dA[par][:, m, 1:L], delta[:, m, 1:L], ACT.Exp, scale=n(m))
                    e.then_inc(s["da_ok"], 1)
                    act.wait_ge(s["c_ps"], G + 1)
                    act.wait_ge(s["hc_ok"], G + 1)
                    act.copy(Csb[par], banks(6)).then_inc(s["c_ok"], 1)

                act.wait_ge(s["du_ok"], b + 1)
                passed(act)
                table(act, EXP)
                with act.Fori(0, GRP) as i:
                    for par in range(2):
                        state(lambda m: A[:, m, bass.ds(i + par * GRP, 1)], par, b * NS + 2 * i + par)
                layer_norm(b * N_LN_MAMBA + 2)
                own.leave(NB)

            def squares(I, st):
                n = STEPS * I + st
                act.wait_ge(s["qk_ps"], n + 1)
                act.wait_ge(s["ss_ps"], n + 1)
                act.activation(qsq[:, st % 2, :], ps[:, st % 2, :], ACT.Square).then_inc(s["sq_ok"], 1)

            def value_copy(I, t):
                act.wait_ge(s["v_ps"], NW * I + t + 1)
                act.copy(vtok[:, t, :], ps[:, 6 + t % 2, :]).then_inc(s["v_ok"], 1)

            def norm_piece(I, ch, k):
                K = NC2 * I + ch
                rows = slice(0, 3 * GRP)
                if k == 0:
                    act.wait_ge(s["ss_ps"], STEPS * I + BLOCKS * (ch + 1) + 2)
                    if ch:
                        act.wait_ge(s["norm_ok"], K)
                    table(act, LOG)
                    act.activation(nlog[rows, :], ps[rows, 4, :], ACT.Ln, scale=float(2 ** NORM_SHIFT),
                                   bias=epsv[rows, 2:3]).then_inc(s["norm_log"], 1)
                    table(act, EXP)
                    act.wait_ge(s["norm_log"], K + 1)
                    act.activation(ninv[rows, :], nlog[rows, :], ACT.Exp, scale=-0.5,
                                   bias=epsv[rows, 3:4]).then_inc(s["norm_exp"], 1)
                if k == 1:
                    act.wait_ge(s["norm_min"], K + 1)
                    if ch:
                        act.wait_ge(s["inv_ps"], STEPS * I + BLOCKS)
                    act.copy(nparts[rows, :], ninv[rows, :]).then_inc(s["norm_hi"], 1)
                if k == 2:
                    act.wait_ge(s["norm_rest"], K + 1)
                    act.copy(nparts[GRP:2 * GRP, :], nrest[GRP:2 * GRP, :])
                    act.copy(nparts[2 * GRP:3 * GRP, :], nrest[2 * GRP:3 * GRP, :]).then_inc(s["norm_mid"], 1)

            def exps(I, g):
                n = GROUPS * I + g
                act.wait_ge(s["shifted"], n + 3)
                act.wait_ge(s["prob_ok"], n + 1)
                act.activation(ex[:, g % 2, :], sc[:, g % 2, :], ACT.Exp).then_inc(s["exp_ok"], 1)

            def turned(I, g):
                n = GROUPS * I + g
                act.wait_ge(s["pt_ps"], n + 3)
                act.wait_ge(s["o_ps"], n + 1)
                act.copy(pT[:, g % 2, :], ps[:, 2 + g % 2, :]).then_inc(s["pt_ok"], 1)

            def heads_out(I, g):
                quad, hp = g // PAIRS, g % PAIRS
                act.wait_ge(s["o_ps"], GROUPS * I + g + 3)
                if g == GROUPS // NC2:
                    act.wait_ge(s["wo_ps"], NC2 * I + 1)
                for h in range(2):
                    rows = slice(h * DH, (h + 1) * DH)
                    o = (quad * QUAD % CQ) * WIN
                    cp = act.copy(oT[rows, hp, o:o + QUAD * WIN].rearrange("p (w i) -> p w i", i=WIN),
                                  ps[rows, 4, :].rearrange("p (w i) -> p w i", i=P)[:, :, h * WIN:(h + 1) * WIN])
                cp.then_inc(s["o_ok"], 1)

            def ffn_piece(l, J, step):
                if step in GELU_AT:
                    K = NC2 * J + GELU_AT[step]
                    act.wait_ge(s["g_ok"], FB * K + FB)
                    table(act, GELU)
                    act.activation(gbuf, gbuf, ACT.Gelu).then_inc(s["gelu_ok"], 1)
                    table(act, EXP)
                if step not in FFN_AT:
                    return
                what, ch, f = FFN_AT[step]
                K = NC2 * J + ch
                if what == "dev":
                    act.wait_ge(s["f_dev"], K + 1)
                    act.activation(fsq, ps[:, 6, :], ACT.Square).then_inc(s["f_sq"], 1)
                if what == "var":
                    act.wait_ge(s["f_var"], K + 1)
                    act.activation(ln_var[:, ch, :], ps[:, 7, 0:TILES], ACT.Identity, bias=epsv[:, 0:1])\
                        .then_inc(s["f_eps"], 1)
                if what == "ag":
                    rows = FROWS[f]
                    act.wait_ge(s["ag_ps"], FB * K + f + 1)
                    if f == 0:
                        act.wait_ge(s["ff_ok"], K + 1)
                    passed(act)
                    act.activation(gbuf[0:rows, f * BANK:(f + 1) * BANK], ps[0:rows, 7, :], ACT.Identity,
                                   bias=b1s[0:rows, bass.ds(l, 1), 1, f]).then_inc(s["g_ok"], 1)

            def body(l, I, J):
                act.wait_ge(s["o_ps"], GROUPS * I + 2)
                for st in range(STEPS + 1):
                    if st < STEPS:
                        squares(I, st)
                    if st < NW:
                        value_copy(I, st)
                    if st in NORM_AT:
                        norm_piece(I, 0, NORM_AT.index(st))
                    if st == STEPS:
                        norm_piece(I, 1, 0)
                for g in range(GROUPS + 3):
                    if g < GROUPS:
                        exps(I, g)
                    if 2 <= g < GROUPS + 2:
                        turned(I, g - 2)
                    if g >= 3:
                        heads_out(I, g - 3)
                    if g < 2:
                        norm_piece(I, 1, g + 1)
                    if J is not None:
                        ffn_piece(l, J, g)

            for name in ("v_ok", "sq_ok", "exp_ok", "pt_ok"):
                act.sem_inc(s[name], 2)
            act.sem_inc(s["o_ok"], 1)
            with act.Fori(0, LAYERS) as l:
                body(l, l * NB, None)
                passed(act)
                with act.Fori(1, NB) as b:
                    body(l, l * NB + b, l * NB + b - 1)
                for step in range(GROUPS):
                    ffn_piece(l, l * NB + NB - 1, step)

        @block.vector
        def _(dve):
            own = Steps(dve, s["vec_step"])

            def layer_norm(dst, scale, shift, q, inc):
                for ch in range(NC2):
                    dve.wait_ge(s["ln_dev"], NC2 * q + ch + 1)
                    dve.wait_ge(s["ln_sq"], NC2 * q + ch + 1)
                    own.done(dve.tensor_copy(lnA[:, ch * BANK:(ch + 1) * BANK], ps[:, 4 + ch, :]))
                own.wait()
                for ch in range(NC2):
                    cols = slice(ch * BANK, (ch + 1) * BANK)
                    dve.wait_ge(s["ln_bc"], NC2 * q + ch + 1)
                    own.done(dve.tensor_tensor(lnA[:, cols], lnA[:, cols], ps[:, 6 + ch, :], ALU.mult))
                    own.wait()
                    dve.tensor_scalar(dst[:, cols], lnA[:, cols], scale, shift, ALU.mult, ALU.add)\
                        .then_inc(s[inc], 1)

            dve.sem_inc(s["batch_ok"], 1)
            dve.sem_inc(s["dbu_ok"], 1)
            dve.sem_inc(s["h_ok"], 2)
            dve.memset(epsv[:, 0:1], EPS)
            dve.memset(mean_col[:], 1.0 / P)
            dve.memset(epsv[:, 1:2], 1.0)
            dve.memset(epsv[:, 2:3], 2.0 ** -63)
            dve.memset(epsv[:, 3:4], NORM_SHIFT / 2 * LN2)
            for par in range(2):
                dve.memset(dA[par][:, :, 0:1], 0.0)
            dve.memset(xn[:, 0:TAPS - 1], 0.0).then_inc(s["consts_ok"], 1)

            dve.wait_ge(s["mod_ps"], 1)
            dve.tensor_copy(mod[:].rearrange("p a b -> p (a b)"), ps[:, 7, 0:6 * NB]).then_inc(s["mod_sb"], 1)
            dve.wait_ge(s["mod_sb"], 1)
            for j in range(2):
                g = mod[:, 2 + 3 * j, :]
                own.done(dve.tensor_scalar(mod[:, 1 + 3 * j, :], mod[:, 1 + 3 * j, :], 1.0, None, ALU.add))
                own.done(dve.tensor_scalar(gtmp[:, j, 0, :], g, -1.0, None, ALU.mult))
                own.wait()
                own.done(dve.tensor_tensor(gtmp[:, j, 0, :], gtmp[:, j, 0, :], g, ALU.max))
                own.done(dve.tensor_scalar(gtmp[:, j, 1, :], g, 0.0, 2.0, ALU.is_ge, ALU.mult))
                own.wait()
                own.done(dve.tensor_scalar(gtmp[:, j, 0, :], gtmp[:, j, 0, :], 0.25, None, ALU.max))
                own.wait()
                own.done(dve.scalar_tensor_tensor(gate[:, j, :], gtmp[:, j, 1, :], -1.0, gtmp[:, j, 0, :],
                                                  ALU.add, ALU.mult))
            own.wait()
            dve.wait_ge(s["mamba_in"], 16 * len(mamba_loads))
            dve.wait_ge(s["mod_in"], 16 * len(mod_loads))
            cw = convw.rearrange("p (d k) -> p k d", k=TAPS)
            for k in range(TAPS):
                dve.tensor_tensor(w_taps[:, k, :], w_in[:, 0:DI], cw[:, k, :], ALU.mult)
            for m in range(HALVES):
                for r in range(3):
                    dve.tensor_copy(w_bc[:, m, :, r, :],
                                    w_x[:, m, RANK:].rearrange("p (g n) -> p g n", n=GRP))
                own.done(dve.tensor_scalar(diagD[:, m, :], ident[:], at["D"][:, m:m + 1], None, ALU.mult))
            own.wait()
            dve.sem_inc(s["prep_ok"], 1)

            dve.wait_ge(s["x_in"], 16 * NB)
            PER_BATCH = N_LN_MAMBA * NC2 * 2 + 6 + 1
            with dve.Fori(0, NB) as b:
                own.enter(b, PER_BATCH)
                bb = bass.ds(b, 1)
                layer_norm(hres, mod[:, 1, bb], mod[:, 0, bb], b * N_LN_MAMBA, "hres_ok")
                layer_norm(xn[:, TAPS - 1:], at["ln_w"], at["ln_b"], b * N_LN_MAMBA + 1, "xn_ok")
                dve.wait_ge(s["dtr_ps"], b + 1)
                dve.tensor_copy(dtr, banks(0, rows=slice(0, RANK))).then_inc(s["dtr_ok"], 1)

                def rest(g):
                    dve.wait_ge(s["bc_hi"], NG * b + g + 1)
                    dve.tensor_tensor(r1[0:3 * GRP, g % 2, :], banks([2, 4, 6, 2][g], rows=slice(0, 3 * GRP)),
                                      bcs[0:3 * GRP, g, :], ALU.subtract).then_inc(s["bc_r1"], 1)
                    dve.wait_ge(s["bc_mid"], NG * b + g + 1)
                    dve.tensor_tensor(bcs[2 * GRP:3 * GRP, g, :], r1[2 * GRP:3 * GRP, g % 2, :],
                                      bcs[2 * GRP:3 * GRP, g, :], ALU.subtract).then_inc(s["bc_ok"], 1)

                for g in range(NG):
                    rest(g)
                dve.wait_ge(s["sp_ok"], b + 1)
                own.done(dve.tensor_scalar(spT, spY, -0.25, 1.0 / 3.0, ALU.mult, ALU.add))
                own.wait()
                own.done(dve.tensor_tensor(spT, spT, spY, ALU.mult))
                own.wait()
                own.done(dve.scalar_tensor_tensor(spT, spT, -0.5, spY, ALU.add, ALU.mult))
                own.wait()
                own.done(dve.scalar_tensor_tensor(spT, spT, 1.0, spY, ALU.add, ALU.mult))
                own.wait()
                own.done(dve.scalar_tensor_tensor(spT, spL, -LN_SLACK, spT, ALU.add, ALU.max))
                own.wait()
                own.done(dve.scalar_tensor_tensor(delta, spX, 0.0, spT, ALU.max, ALU.add))
                own.wait()
                dve.tensor_tensor(du, delta, u, ALU.mult).then_inc(s["du_ok"], 1)
                dve.wait_ge(s["du_ok"], b + 1)

                def inject(par, G):
                    dve.wait_ge(s["b_ps"], G + 1)
                    dve.wait_ge(s["h_ok"], G + 1)
                    bb2 = banks(4).unsqueeze(1).broadcast_to([P, HALVES, L])
                    dve.tensor_tensor(dBu[par], du, bb2, ALU.mult).then_inc(s["dbu_ok"], 1)

                def scan(par, G):
                    dve.wait_ge(s["dbu_ok"], G + 2)
                    dve.wait_ge(s["da_ok"], G + 1)
                    dve.wait_ge(s["hc_ok"], G + 1)
                    flat = [t[par].rearrange("p a n -> p (a n)") for t in (hst, dA, dBu)]
                    dve.tensor_tensor_scan(flat[0], flat[1], flat[2], 0.0, ALU.mult, ALU.add)\
                        .then_inc(s["h_ok"], 1)

                inject(0, b * NS)
                with dve.Fori(0, GRP - 1) as i:
                    G = b * NS + 2 * i
                    inject(1, G + 1)
                    scan(0, G)
                    inject(0, G + 2)
                    scan(1, G + 1)
                G = b * NS + NS - 2
                inject(1, G + 1)
                scan(0, G)
                scan(1, G + 1)
                dve.wait_ge(s["y_acc"], NS * b + NS + 2)
                dve.tensor_tensor(zs, ps[:, 0:4, :].rearrange("p (a c) n -> p a (c n)", a=HALVES), zs, ALU.mult)\
                    .then_inc(s["gated"], 1)
                dve.wait_ge(s["mix_ps"], b + 1)
                own.done(dve.tensor_tensor(lnA[:], banks(4), hres, ALU.add))
                own.wait()
                dve.scalar_tensor_tensor(xT[:, b, :], lnA[:], gate[:, 0, bb], xT[:, b, :], ALU.mult, ALU.add)\
                    .then_inc(s["x1_ok"], 1)
                layer_norm(hf[:, b, :], mod[:, 4, bb], mod[:, 3, bb], b * N_LN_MAMBA + 2, "batch_ok")
                own.leave(NB)

            for name in ("masked", "halves_ok", "shifted"):
                dve.sem_inc(s[name], 2)
            for name in ("qk_ok", "f_out"):
                dve.sem_inc(s[name], 1)
            dve.wait_ge(s["batch_ok"], NC2 * NB + 1)
            dve.wait_ge(s["parked"], 16 * NB)
            dve.memset(kT[:, :, 0:WIN], 0.0)
            dve.memset(qbd, 0.0)
            dve.memset(gbuf, 0.0)

            def shift_to(dst, b):
                dve.tensor_copy(dst[0:DH, :], hf[0:DH, b, :])
                return dve.tensor_copy(dst[DH:P, 1:L], hf[DH:P, b, 0:L - 1])

            def halves(I, st):
                ch, j = st // BLOCKS, st % BLOCKS
                n = STEPS * I + st
                t = 2 * (j % 2)
                cols = slice(ch * BANK, (ch + 1) * BANK)
                dve.wait_ge(s["sq_ok"], n + 3)
                dve.wait_ge(s["raw_ok"], n + 1)
                dve.tensor_tensor(qcos[:, st % 2, :], ps[:, st % 2, :], tables[:, t, cols], ALU.mult)
                dve.tensor_tensor(qsin[:, st % 2, :], ps[:, 2 + st % 2, :], tables[:, t + 1, cols], ALU.mult)\
                    .then_inc(s["halves_ok"], 1)

            def norm_piece(I, ch, k):
                K = NC2 * I + ch
                rows = slice(0, 3 * GRP)
                if k == 0:
                    dve.wait_ge(s["norm_exp"], K + 1)
                    dve.tensor_scalar(ninv[rows, :], ninv[rows, :], 1e12, None, ALU.min).then_inc(s["norm_min"], 1)
                if k == 1:
                    dve.wait_ge(s["norm_hi"], K + 1)
                    dve.tensor_tensor(nrest[rows, :], ninv[rows, :], nparts[rows, :], ALU.subtract)\
                        .then_inc(s["norm_rest"], 1)
                if k == 2:
                    dve.wait_ge(s["norm_mid"], K + 1)
                    third = slice(2 * GRP, 3 * GRP)
                    dve.tensor_tensor(nparts[third, :], nrest[third, :], nparts[third, :], ALU.subtract)\
                        .then_inc(s["norm_ok"], 1)

            def scaled(I, f):
                ch, j = f // BLOCKS, f % BLOCKS
                hp, n = j // 2, STEPS * I + f
                dve.wait_ge(s["inv_ps"], n + 1)
                dve.wait_ge(s["raw_ok"], n + 3)
                if j % 2:
                    kk = kT[:, hp, WIN + ch * BANK:WIN + (ch + 1) * BANK]
                    dve.tensor_tensor(kk, kk, ps[:, 5, :], ALU.mult).then_inc(s["qk_ok"], 1)
                else:
                    for h in range(2):
                        rows = slice(h * DH, (h + 1) * DH)
                        win = "p (w i) -> p w i"
                        tt = dve.tensor_tensor(qbd[rows, hp, ch * CQ:(ch + 1) * CQ, h * WIN:(h + 1) * WIN],
                                               qraw[ch][rows, hp, :].rearrange(win, i=WIN),
                                               ps[rows, 5, :].rearrange(win, i=WIN), ALU.mult)
                    tt.then_inc(s["qk_ok"], 1)

            def mask_in(I, g):
                n = GROUPS * I + g
                dve.wait_ge(s["sim_ps"], n + 1)
                dve.wait_ge(s["exp_ok"], n + 1)
                s3 = sc[:, g % 2, :].rearrange("p (w j) -> p w j", j=P)
                p3 = ps[:, g % 2, :].rearrange("p (w j) -> p w j", j=P)
                a = int(g < PAIRS)
                if a:
                    dve.tensor_tensor(s3[:, 0, :], p3[:, 0, :], mask[:, 1, :], ALU.add)
                dve.tensor_tensor(s3[:, a:, :], p3[:, a:, :], mask[:, 0:1, :].broadcast_to([P, QUAD - a, P]),
                                  ALU.add).then_inc(s["masked"], 1)

            def row_max(I, g):
                dve.wait_ge(s["masked"], GROUPS * I + g + 3)
                dve.tensor_reduce(smax[:, g % 2, :], sc[:, g % 2, :].rearrange("p (w j) -> p w j", j=P),
                                  AX, ALU.max).then_inc(s["max_ok"], 1)

            def shift_in(I, g):
                dve.wait_ge(s["max_ok"], GROUPS * I + g + 1)
                s3 = sc[:, g % 2, :].rearrange("p (w j) -> p w j", j=P)
                dve.tensor_tensor(s3, s3, smax[:, g % 2, :].unsqueeze(2).broadcast_to([P, QUAD, P]),
                                  ALU.subtract).then_inc(s["shifted"], 1)

            def row_sum(I, g):
                dve.wait_ge(s["exp_ok"], GROUPS * I + g + 3)
                dve.tensor_reduce(ssum[:, g % 2, :], ex[:, g % 2, :].rearrange("p (w j) -> p w j", j=P),
                                  AX, ALU.add).then_inc(s["sum_ok"], 1)

            def row_rec(I, g):
                n = GROUPS * I + g
                dve.wait_ge(s["sum_ok"], n + 1)
                dve.wait_ge(s["prob_ok"], n + 1)
                dve.reciprocal(srec[:, g % 2, :], ssum[:, g % 2, :]).then_inc(s["rsum_ok"], 1)

            def attn_add(I, b, ch, bank):
                cols = slice(ch * BANK, (ch + 1) * BANK)
                dve.wait_ge(s["wo_ps"], NC2 * I + ch + 1)
                dve.tensor_tensor(hf[:, b, cols], hf[:, b, cols], ps[:, bank, :], ALU.add).then_inc(s["attn_ok"], 1)

            def close(J, b):
                attn_add(J, b, 1, 5)
                dve.wait_ge(s["attn_ok"], NC2 * J + 2)
                passed(dve)
                dve.memset(fs[DH:P, 0:1], 0.0)
                shift_to(fs, b).then_inc(s["fs_ok"], 1)

            def ffn_piece(l, J, b, step):
                ll = bass.ds(l, 1)
                if step not in FFN_AT:
                    return
                what, ch, f = FFN_AT[step]
                K = NC2 * J + ch
                if what == "dev":
                    dve.wait_ge(s["f_sq"], K + 1)
                    dve.tensor_copy(fdev, ps[:, 6, :]).then_inc(s["f_kept"], 1)
                if what == "norm":
                    dve.wait_ge(s["f_kept"], K + 1)
                    dve.wait_ge(s["f_bc"], K + 1)
                    dve.tensor_tensor(fnorm, fdev, ps[:, 7, :], ALU.mult).then_inc(s["f_norm"], 1)
                    dve.wait_ge(s["f_norm"], K + 1)
                    dve.tensor_scalar(fin, fnorm, at["ln_g"][:, ll], at["ln_b2"][:, ll], ALU.mult, ALU.add)\
                        .then_inc(s["f_in"], 1)
                if what == "ag":
                    rows = FROWS[f]
                    dve.wait_ge(s["ag_ps"], FB * K + f + 1)
                    dve.tensor_scalar(abuf[0:rows, f * BANK:(f + 1) * BANK], ps[0:rows, 6, :],
                                      b1s[0:rows, ll, 0, f], None, ALU.add).then_inc(s["av_ok"], 1)
                if what == "w2":
                    cols = slice(ch * BANK, (ch + 1) * BANK)
                    dve.wait_ge(s["w2_ps"], K + 1)
                    dve.scalar_tensor_tensor(hf[:, b, cols], ps[:, 6, :], at["b2"][:, ll], hf[:, b, cols],
                                             ALU.add, ALU.add).then_inc(s["f_out"], 1)

            def body(l, b, I, J):
                dve.wait_ge(s["f_out"], NC2 * NB * l + 1)
                passed(dve)
                dve.memset(hs_all[:, 0:WIN], 0.0)
                dve.memset(hs[DH:P, 0:1], 0.0)
                shift_to(hs, b).then_inc(s["hs_ok"], 1)
                dve.wait_ge(s["prob_ok"], GROUPS * I + 2)
                for st in range(STEPS + 1):
                    if st < STEPS:
                        halves(I, st)
                    if st == 1 and J is not None:
                        close(J, b - 1)
                    if st - 1 in NORM_AT:
                        norm_piece(I, 0, NORM_AT.index(st - 1))
                    if st in INV_AT:
                        for k in range(2):
                            scaled(I, 2 * (st - min(INV_AT)) + k)
                dve.wait_ge(s["raw_ok"], STEPS * (I + 1) + 2)
                for g in range(GROUPS + 3):
                    if g < GROUPS:
                        mask_in(I, g)
                        row_max(I, g)
                    if 1 <= g <= GROUPS:
                        row_sum(I, g - 1)
                    if g < GROUPS:
                        shift_in(I, g)
                    if 1 <= g <= GROUPS:
                        row_rec(I, g - 1)
                    if g < 3:
                        norm_piece(I, 1, g)
                    for j in FINAL_AT.get(g, ()):
                        scaled(I, BLOCKS + j)
                    if J is not None:
                        ffn_piece(l, J, b - 1, g)
                    if g == WO_AT:
                        attn_add(I, b, 0, 5)

            with dve.Fori(0, LAYERS) as l:
                dve.wait_ge(s["attn_in"], 16 * N_ATTN * (l + 1))
                dve.wait_ge(s["consts_in"], 16 * len(phase_loads))
                for t in range(4):
                    dve.tensor_scalar(tables[:, t, :], tables[:, t, :], qv[:, bass.ds(l, 1), t], None, ALU.mult)\
                        .then_inc(s["weights_ok"], 1)
                dve.wait_ge(s["weights_ok"], 6 * l + 6)
                body(l, 0, l * NB, None)
                passed(dve)
                with dve.Fori(1, NB) as b:
                    body(l, b, l * NB + b, l * NB + b - 1)
                J = l * NB + NB - 1
                close(J, NB - 1)
                for step in range(GROUPS):
                    ffn_piece(l, J, NB - 1, step)
            dve.wait_ge(s["f_out"], NC2 * LAYERS * NB + 1)
            dve.wait_ge(s["x1_back"], 16)
            for b in range(NB):
                dve.scalar_tensor_tensor(xend[:, b, :], hf[:, b, :], gate[:, 1, b:b + 1], xend[:, b, :],
                                         ALU.mult, ALU.add).then_inc(s["end_ok"], 1)

        @block.gpsimd
        def _(pool):
            def inverse_root(ch, var_ready, n, done):
                pool.wait_ge(s[var_ready], n)
                pool.tensor_tensor(rstd[:, ch, :], ln_var[:, ch, :], minus_half[:, 0:1].broadcast_to([P, TILES]),
                                   ALU.pow).then_inc(s[done], 1)

            def layer_norm(q):
                for ch in range(NC2):
                    inverse_root(ch, "ln_eps", NC2 * q + ch + 1, "ln_rstd")

            pool.sem_inc(s["hc_ok"], 2)
            pool.memset(minus_half[:], -0.5).then_inc(s["pool_step"], 1)
            pool.wait_ge(s["pool_step"], 1)
            pool.dma_start(select[0:3 * GRP], k_select).then_inc(s["select_in"], 16)
            with pool.Fori(0, NB) as b:
                layer_norm(b * N_LN_MAMBA)
                layer_norm(b * N_LN_MAMBA + 1)
                passed(pool)
                with pool.Fori(0, GRP) as i:
                    for par in range(2):
                        G = b * NS + 2 * i + par
                        pool.wait_ge(s["h_ok"], G + 3)
                        pool.wait_ge(s["c_ok"], G + 2)
                        pool.wait_ge(s["y_acc"], G + 1)
                        pool.tensor_tensor(hC[par], hst[par], Csb[par].unsqueeze(1).broadcast_to([P, HALVES, L]),
                                           ALU.mult).then_inc(s["hc_ok"], 1)
                layer_norm(b * N_LN_MAMBA + 2)
            pool.sem_inc(s["raw_ok"], 2)
            pool.sem_inc(s["prob_ok"], 2)
            pool.sem_inc(s["ff_ok"], 1)
            pool.wait_ge(s["batch_ok"], NC2 * NB + 1)
            pool.wait_ge(s["parked"], 16 * NB)
            pool.dma_start(unhead[0:3 * GRP], k_spread).then_inc(s["select_in"], 16)

            def raw(I, st):
                ch, j = st // BLOCKS, st % BLOCKS
                hp, n = j // 2, STEPS * I + st
                dst = kT[:, hp, WIN + ch * BANK:WIN + (ch + 1) * BANK] if j % 2 else qraw[ch][:, hp, :]
                pool.wait_ge(s["halves_ok"], n + 3)
                pool.tensor_tensor(dst, qcos[:, st % 2, :], qsin[:, st % 2, :], ALU.add).then_inc(s["raw_ok"], 1)

            def probs(I, g):
                n = GROUPS * I + g
                pool.wait_ge(s["rsum_ok"], n + 1)
                pool.wait_ge(s["pt_ps"], n + 1)
                pool.tensor_tensor(pr[:, g % 2, :].rearrange("p (w j) -> p w j", j=P),
                                   ex[:, g % 2, :].rearrange("p (w j) -> p w j", j=P),
                                   srec[:, g % 2, :].unsqueeze(2).broadcast_to([P, QUAD, P]),
                                   ALU.mult).then_inc(s["prob_ok"], 1)

            def ffn_norm(J, step):
                if step in FFN_AT and FFN_AT[step][0] == "var":
                    ch = FFN_AT[step][1]
                    inverse_root(ch, "f_eps", NC2 * J + ch + 1, "f_rstd")

            def ffn_piece(J, step):
                for at_step, ch in GELU_AT.items():
                    K = NC2 * J + ch
                    for f in {0: (0,), 1: (1, 2)}.get(step - at_step, ()):
                        pool.wait_ge(s["gelu_ok"], K + 1)
                        pool.wait_ge(s["av_ok"], FB * K + FB)
                        rows, cols = FROWS[f], slice(f * BANK, (f + 1) * BANK)
                        tt = pool.tensor_tensor(abuf[0:rows, cols], abuf[0:rows, cols], gbuf[0:rows, cols], ALU.mult)
                        if f == FB - 1:
                            tt.then_inc(s["ff_ok"], 1)

            def body(I, J):
                for st in range(STEPS):
                    raw(I, st)
                for g in range(GROUPS):
                    if J is not None:
                        ffn_norm(J, g)
                    probs(I, g)
                    if J is not None:
                        ffn_piece(J, g)

            with pool.Fori(0, LAYERS) as l:
                pool.wait_ge(s["attn_in"], 16 * N_ATTN * (l + 1))
                passed(pool)
                w4 = w_qkv[:, 0:2 * INNER].rearrange("p (h a d) -> p h a d", a=2, d=DH // 2)
                r4 = w_rot.rearrange("p (h a d) -> p h a d", a=2, d=DH // 2)
                for a in range(2):
                    pool.tensor_copy(r4[:, :, a, :], w4[:, :, 1 - a, :]).then_inc(s["weights_ok"], 1)
                body(l * NB, None)
                passed(pool)
                with pool.Fori(1, NB) as b:
                    body(l * NB + b, l * NB + b - 1)
                for step in range(GROUPS):
                    ffn_norm(l * NB + NB - 1, step)
                    ffn_piece(l * NB + NB - 1, step)


def columns(v):
    return np.ascontiguousarray(v.reshape(-1, P).T)


def packed_vectors(a):
    half = DH // 2
    qk = []
    for l in range(LAYERS):
        for name in ("L0_ffn_q_scale", "L0_ffn_k_scale"):
            v = a[name][l]
            qk += [np.tile(v, 2), np.tile(np.concatenate([v[half:], v[:half]]), 2)]
    b1 = np.zeros((LAYERS, 2, FB, P), np.float32)
    for part in range(2):
        for f, rows in enumerate(FROWS):
            b1[:, part, f, :rows] = a["L0_ffn_b1"][:, part * HID + f * P:part * HID + f * P + rows]
    named = {"ln_w": a["L0_attn_ln_w"], "ln_b": a["L0_attn_ln_b"], "c": a["L0_c"], "conv_b": a["L0_attn_conv_b"],
             "b_dt": a["L0_attn_b_dt"], "D": a["L0_attn_D"], "qk": np.stack(qk), "ln_g": a["L0_ffn_ln_g"],
             "ln_b2": a["L0_ffn_ln_b"], "b2": a["L0_ffn_b2"], "b1": b1}
    return np.concatenate([columns(named[n]) for n in VECS], 1)


def constants():
    ident = np.eye(P, dtype=np.float32)
    centre = ident - np.float32(1.0 / P)
    heads = np.zeros((P, BLOCKS, 3 * GRP), np.float32)
    for j in range(BLOCKS):
        for h in range(2):
            for r in range(3):
                heads[h * DH:(h + 1) * DH, j, r * GRP + 2 * j + h] = 1.0
    spread = np.ascontiguousarray(heads.transpose(2, 1, 0))
    select = np.zeros((3 * GRP, GRP, P), np.float32)
    for r in range(3 * GRP):
        select[r, r % GRP] = 1.0
    no = np.float32(-3.0e38)
    i, j = np.arange(WIN)[:, None], np.arange(WIN)[None, :]
    own = np.where(j <= i, np.float32(0), no)
    prev = np.where(j >= i, np.float32(0), no)
    mask = np.stack([np.concatenate([prev, own], 1), np.concatenate([np.full_like(own, no), own], 1)], 1)
    mask = np.concatenate([mask, mask], 0).astype(np.float32)
    half = np.arange(0, DH, 2, dtype=np.float32)
    freq = np.float32(1.0) / np.float32(10000.0) ** (half / np.float32(DH))
    t = np.arange(L, dtype=np.float32)
    angle = t[:, None] * freq[None, :]
    base = (half + np.float32(0.4 * DH)) / np.float32(1.4 * DH)
    power = (t - L // 2) / np.float32(WIN // 2)
    scale = base[None, :] ** power[:, None]
    angle, scale = (np.concatenate([a, a], 1).T for a in (angle, scale))
    sign = np.where(np.arange(DH) < DH // 2, -1.0, 1.0).astype(np.float32)[:, None]
    cos, sin = np.cos(angle), np.sin(angle) * sign
    tables = np.stack([cos * scale * 8, sin * scale * 8, cos / scale, sin / scale], 1)
    tables = np.concatenate([tables, tables], 0).astype(np.float32)
    return {"k_ident": ident, "k_centre": centre, "k_heads": heads, "k_spread": spread, "k_select": select, "k_mask": mask,
            "k_tables": tables}


def kernel(**inputs):
    import concourse.bacc as bacc
    from concourse.bass_utils import run_bass_kernel_spmd

    nc = bacc.Bacc("TRN2", target_bir_lowering=False, num_devices=1)
    a = {n: np.asarray(v) for n, v in inputs.items()}
    arrays = {"x": np.ascontiguousarray(a["L0_attn_x"].transpose(2, 0, 1)), "vecs": packed_vectors(a)}
    for n in ("attn_W_in", "attn_conv_w", "attn_W_xproj", "attn_W_dt", "attn_A_log", "attn_W_out",
              "ffn_wqkv", "ffn_wo", "ffn_w1", "ffn_w2", "wmod"):
        arrays[n] = np.ascontiguousarray(a["L0_" + n])
    arrays.update(constants())
    args = [nc.dram_tensor("in_" + n, a.shape, mybir.dt.from_np(a.dtype), kind="ExternalInput").ap()
            for n, a in arrays.items()]
    y = nc.dram_tensor("out_y", (D, NB, L), F32, kind="ExternalOutput").ap()
    adaln_block(nc, *args, y)
    r = run_bass_kernel_spmd(nc, [{"in_" + n: a for n, a in arrays.items()}], core_ids=[0])
    return np.ascontiguousarray(r.results[0]["out_y"].transpose(1, 2, 0))
```

```python
from contextlib import ExitStack

import numpy as np

import concourse.bass as bass
from concourse import mybir

F32 = mybir.dt.float32
BF16 = mybir.dt.bfloat16
ALU = mybir.AluOpType
ACT = mybir.ActivationFunctionType
AX = mybir.AxisListType.X

P = 128
NB = 4
L = 1024
BANK = 512
NC2 = L // BANK
D = 128
HALVES = 2
DI = HALVES * P
NS = 64
TAPS = 4
RANK = D // 16
GRP = 32
NG = 2 * NS // GRP
LAYERS = 2
HEADS = 8
DH = 64
WIN = 64
NW = L // WIN
PAIRS = HEADS // 2
INNER = HEADS * DH
HID = int(D * 4 * 2 / 3)
FB = 3
FROWS = [min(P, HID - P * f) for f in range(FB)]
TOK = L // P
BLOCKS = 2 * PAIRS
STEPS = NC2 * BLOCKS
QUAD = 4
GROUPS = PAIRS * NW // QUAD
CQ = NW // NC2
TILES = BANK // P
LAG = 3
EPS = 1e-5
GELU = "gelu_and_others"
EXP = "exp_and_others"
LOG = "natural_log"
LN2 = float(np.log(2.0))
NORM_SHIFT = 20
LN_SLACK = 2e-7


class Steps:

    def __init__(self, eng, sem):
        self.eng, self.sem, self.base, self.k, self.outer = eng, sem, 0, 0, []

    def done(self, inst):
        inst.then_inc(self.sem, 1)
        self.k += 1

    def wait(self):
        self.eng.wait_ge(self.sem, self.base + self.k)

    def enter(self, var, per):
        self.outer.append((self.base, self.k, per))
        self.base, self.k = self.base + self.k + var * per, 0

    def leave(self, times):
        base, k, per = self.outer.pop()
        assert self.k == per, (self.k, per)
        self.base, self.k = base, k + per * times


def row_banks(f, alone):
    return (0, 1) if alone and f == 1 else (6, 7)


def inv_bank(f):
    return 5 if f >= BLOCKS else 6 + f % 2


LN_AT = {3: ("dev", 0), 5: ("var", 0), 7: ("norm", 0), 8: ("dev", 1), 10: ("var", 1), 12: ("norm", 1)}
FFN_AT = {1: ("ag", 0, 0), 2: ("ag", 0, 1), 3: ("ag", 0, 2), 7: ("w2", 0, 0),
          8: ("ag", 1, 0), 9: ("ag", 1, 1), 10: ("ag", 1, 2), 16: ("w2", 1, 0)}
GELU_AT = {4: 0, 12: 1}
WO_AT = 11
NORM_AT = (8, 10, 11)
INV_AT = (13, 14, 15, 16)
FINAL_AT = {3: (0,), 4: (1, 2), 5: (3,), 6: (4,), 7: (5,), 8: (6,), 9: (7,)}

VECS = {"ln_w": 1, "ln_b": 1, "c": NB, "conv_b": HALVES, "b_dt": HALVES, "D": HALVES, "qk": 4 * LAYERS,
        "ln_g": LAYERS, "ln_b2": LAYERS, "b2": LAYERS, "b1": 2 * FB * LAYERS}


def adaln_block(nc, x, vecs, W_in, conv_w, W_xproj, W_dt, A_log, W_out, wqkv, wo, w1, w2, wmod,
                k_ident, k_centre, k_heads, k_spread, k_select, k_mask, k_tables, out):
    with ExitStack() as ctx:
        def sb(name, shape, dt=F32):
            return ctx.enter_context(nc.sbuf_tensor(name, shape, dt))

        def sem(name):
            return ctx.enter_context(nc.semaphore(name))

        ps = ctx.enter_context(nc.psum_tensor("ps", [P, 8, BANK], F32))

        def banks(first, n=NC2, rows=slice(0, P)):
            return ps[rows, first:first + n, :].rearrange("p a b -> p (a b)")

        ident = sb("ident", [P, P])
        ident16 = sb("ident16", [P, P], BF16)
        centre = sb("centre", [P, P])
        mean_col = sb("mean_col", [P, 1])
        ln_var = sb("ln_var", [P, NC2, TILES])
        rstd = sb("rstd", [P, NC2, TILES])
        minus_half = sb("minus_half", [P, 1])
        hf = sb("hf", [P, NB, L])
        lnA = sb("lnA", [P, L])
        lnB = sb("lnB", [P, L])
        lnC = sb("lnC", [P, L])
        mod = sb("mod", [P, 6, NB])
        gate = sb("gate", [P, 2, NB])
        gtmp = sb("gtmp", [P, 2, 2, NB])
        silu_c = sb("silu_c", [P, NB])
        vec_s = sb("vec_s", [P, sum(VECS.values())])
        at, col = {}, 0
        for name, width in VECS.items():
            at[name], col = vec_s[:, col:col + width], col + width
        qv = at["qk"].rearrange("p (l a) -> p l a", a=4)
        b1s = at["b1"].rearrange("p (l a f) -> p l a f", a=2, f=FB)
        epsv = sb("epsv", [P, 4])

        ARENA = 44100
        arena = sb("arena", [P, ARENA])
        used = [0]

        def carve(n):
            a = arena[:, used[0]:used[0] + n]
            used[0] += n
            assert used[0] <= ARENA, used[0]
            return a

        def carve3(a, n):
            return carve(a * n).rearrange("p (a n) -> p a n", a=a)

        select = carve(GRP * P // 2).bitcast(BF16).rearrange("p (a n) -> p a n", a=GRP)
        bcs = carve(NG * L // 2).bitcast(BF16).rearrange("p (g n) -> p g n", g=NG)
        u = carve3(HALVES, L)
        zs = carve3(HALVES, L)
        delta = carve3(HALVES, L)
        du = carve3(HALVES, L)
        dA = [carve3(HALVES, L) for _ in range(2)]
        dBu = [carve3(HALVES, L) for _ in range(2)]
        hst = [carve3(HALVES, L) for _ in range(2)]
        hC = [carve3(HALVES, L) for _ in range(2)]
        Csb = [carve(L) for _ in range(2)]
        xn = carve(L + TAPS - 1)
        xT = carve3(NB, L)
        wmod_s = hC[0].rearrange("p a n -> p (a n)")[:, 0:6 * D]
        w_in = carve(2 * DI)
        convw = hC[1].rearrange("p a n -> p (a n)")[:, 0:DI * TAPS]
        w_taps = carve3(TAPS, DI)
        A = carve3(HALVES, NS)
        w_x = carve3(HALVES, RANK + 2 * NS)
        w_bc = carve(HALVES * NG * 3 * GRP).rearrange("p (m g r n) -> p m g r n", m=HALVES, g=NG, r=3)
        w_dt = carve(DI)
        w_out = carve3(HALVES, D)
        diagD = carve3(HALVES, P)
        dtr = lnB[0:RANK, :]
        spY, spL, spX, spT = dBu[0], dBu[1], hst[0], hst[1]
        BC_BANKS = (4, 6, 2, 0)

        def left(g, rows):
            return hC[g // 2][rows, g % 2, :]

        used[0] = 0
        w_qkv = carve(3 * INNER)
        w_rot = carve(2 * INNER)
        w_o = carve3(PAIRS, D)
        w_1 = carve(2 * HID)
        w_2 = carve3(FB, D)
        heads = carve3(BLOCKS, 3 * GRP)
        unhead = carve(BLOCKS * P // 2).bitcast(BF16).rearrange("p (a n) -> p a n", a=BLOCKS)
        mask = carve(BANK).bitcast(BF16).rearrange("p (a n) -> p a n", a=2)
        tables = carve3(4, L)
        gbuf = carve(FB * BANK)
        hs = gbuf[:, 0:L]
        abuf = carve(PAIRS * BANK)
        qraw = [t.rearrange("p (a n) -> p a n", a=PAIRS) for t in (abuf, carve(PAIRS * BANK))]
        qbd = carve(PAIRS * NW * P).rearrange("p (a w n) -> p a w n", a=PAIRS, w=NW)
        kT = carve(PAIRS * (L + WIN)).rearrange("p (a n) -> p a n", a=PAIRS)
        vtok = carve3(NW, INNER)
        oT = carve3(PAIRS, BANK)
        qcos = carve3(2, BANK)
        qsin = carve3(2, BANK)
        qsq = carve3(2, BANK)
        sc, ex, pT = qcos, qsin, qsq
        pr = carve3(2, BANK)
        nlog = carve(BANK)
        ninv = carve(BANK)
        nrest = nlog
        nparts = carve(BANK // 2).bitcast(BF16)
        smax = carve3(2, QUAD)
        ssum = carve3(2, QUAD)
        srec = carve3(2, QUAD)
        xend = qbd.rearrange("p a w n -> p (a w n)")[:, 0:NB * L].rearrange("p (b n) -> p b n", b=NB)
        fs = lnA
        fdev, fsq = lnB[:, 0:BANK], lnB[:, BANK:]
        fin = lnC[:]
        x1_dram = nc.dram_tensor("x1_parked", (P, NB, L), F32, kind="Internal").ap()

        names = """consts_in mod_in mamba_in select_in silu_c mod_ps mod_sb consts_ok prep_ok a_ok
            x_in ln_dev ln_sq ln_var_ps ln_eps ln_rstd ln_bc ln_kept hres_ok xn_ok xc_ps z_ps u_ok zs_ok
            dtr_ps dtr_ok bc_ps bc_hi bc_r1 bc_mid bc_ok dt_ps sp_abs sp_x sp_y sp_ok du_ok
            b_ps dbu_ok c_ps c_ok da_ok h_ok hc_ok hc_last y_acc gated mix_ps x1_ok batch_ok
            ident16_ok qbd_ok attn_in wo_in ffn_in weights_ok hs_ok v_ps v_ok v_moved0 v_moved1 qk_ps sq_ok ss_ps halves_ok raw_ok
            norm_log norm_exp norm_min norm_hi norm_rest norm_mid norm_ok inv_ps qk_ok
            sim_ps max_ok shifted exp_ok sum_ok rsum_ok prob_ok pt_ps pt_ok o_ps o_ok wo_ps attn_ok fs_ok
            f_dev f_sq f_kept f_var f_eps f_rstd f_bc f_norm f_in ag_ps av_ok g_ok gelu_ok ff_ok w2_ps f_out
            parked x1_back end_ok stored
            vec_step act_step pool_step marks""".split()
        s = {n: sem(n) for n in names}

        mod_loads = [(vec_s[:], vecs), (wmod_s, wmod), (centre[:], k_centre), (ident[:], k_ident)]
        mamba_loads = [(w_in, W_in),
                       (convw, conv_w.rearrange("d o k -> o (d k)").broadcast_to([P, DI * TAPS])),
                       (A, A_log.rearrange("(m p) n -> p m n", p=P)),
                       (w_x, W_xproj.rearrange("(m p) n -> p m n", p=P)),
                       (w_dt[0:RANK], W_dt),
                       (w_out, W_out.rearrange("(m p) n -> p m n", p=P))]
        phase_loads = [(heads, k_heads)]

        def attn_loads(l):
            return [(w_qkv, wqkv[l]), (tables, k_tables)]

        def ffn_loads(l):
            full = (FB - 1) * P
            return [(w_1, w1[l]),
                    (w_2[:, 0:FB - 1, :], w2[l, 0:full].rearrange("(a p) n -> p a n", p=P)),
                    (w_2[0:FROWS[-1], FB - 1, :], w2[l, full:HID])]

        end_pieces = [(b, slice(0, L)) for b in range(NB - 1)] +\
            [(NB - 1, slice(ch * BANK, (ch + 1) * BANK)) for ch in range(NC2)]
        N_ATTN, N_FFN = len(attn_loads(0)), len(ffn_loads(0))

        def passed(eng):
            eng.sem_inc(s["marks"], 1)

        def table(act, name):
            passed(act)
            act.preload_act_table_set(name)

        block = ctx.enter_context(nc.Block())

        N_LN_MAMBA = 3
        N_FIRST = 2

        @block.sync
        def _(sp):
            for dst, src in mod_loads:
                sp.dma_start(dst, src).then_inc(s["mod_in"], 16)
            for b in range(NB):
                sp.dma_start(xT[:, b, :], x[:, b, :]).then_inc(s["x_in"], 16)
            for dst, src in mamba_loads:
                sp.dma_start(dst, src).then_inc(s["mamba_in"], 16)
            def park(b):
                sp.wait_ge(s["x1_ok"], NC2 * (b + 1))
                sp.dma_start(x1_dram[:, b, :], xT[:, b, :]).then_inc(s["parked"], 16)

            for b in range(NB - 1):
                park(b)
            sp.wait_ge(s["mix_ps"], NC2 * NB)
            (first_dst, first_src), (second_dst, second_src) = attn_loads(0)
            sp.dma_start(first_dst, first_src).then_inc(s["attn_in"], 16)
            park(NB - 1)
            sp.dma_start(second_dst, second_src).then_inc(s["attn_in"], 16)
            for dst, src in phase_loads:
                sp.dma_start(dst, src).then_inc(s["consts_in"], 16)

            def move_values(I):
                for half in range(2):
                    sp.wait_ge(s["v_ok"], TOK * I + (half + 1) * TOK // 2 + 2)
                    w, end = half * CQ, (half + 1) * CQ
                    skip = 2 * (w == 0)
                    sp.dma_start(vtok[0:WIN, w + skip:end:2, :], vtok[WIN:P, w + skip - 1:end - 1:2, :])\
                        .then_inc(s[f"v_moved{half}"], 16)
                    sp.dma_start(vtok[WIN:P, w:end:2, :], vtok[0:WIN, w + 1:end:2, :]).then_inc(s[f"v_moved{half}"], 16)

            for l in range(LAYERS):
                if l:
                    sp.wait_ge(s["ss_ps"], STEPS * NB * l + 2)
                    sp.wait_ge(s["halves_ok"], STEPS * NB * l + 2)
                    sp.wait_ge(s["v_ps"], TOK * NB * l)
                    for dst, src in attn_loads(l):
                        sp.dma_start(dst, src).then_inc(s["attn_in"], 16)
                if l:
                    sp.wait_ge(s["wo_ps"], NC2 * NB * l)
                sp.dma_start(w_o, wo[l].rearrange("(a p) n -> p a n", p=P)).then_inc(s["wo_in"], 16)
                move_values(l * NB)
                if l:
                    sp.wait_ge(s["w2_ps"], NC2 * NB * l)
                for dst, src in ffn_loads(l):
                    sp.dma_start(dst, src).then_inc(s["ffn_in"], 16)
                for b in range(1, NB):
                    move_values(l * NB + b)
            sp.wait_ge(s["shifted"], GROUPS * LAYERS * NB + 2)
            sp.dma_start(xend, x1_dram).then_inc(s["x1_back"], 16)
            for n, (b, cols) in enumerate(end_pieces):
                sp.wait_ge(s["end_ok"], n + 1)
                sp.dma_start(out[:, b, cols], xend[:, b, cols]).then_inc(s["stored"], 16)
            sp.wait_ge(s["stored"], 16 * len(end_pieces))

        @block.tensor
        def _(pe):
            def variances(bank, squares, t0):
                for t in range(TILES):
                    mm = pe.matmul(ps[:, bank, t:t + 1], squares[:, t0 + t * P:t0 + (t + 1) * P], mean_col[:],
                                   start=True, stop=True)
                return mm

            def on_all_rows(bank, ch):
                for t in range(TILES):
                    mm = pe.matmul(ps[:, bank, t * P:(t + 1) * P], rstd[:, ch, t:t + 1].broadcast_to([P, P]),
                                   ident[:], start=True, stop=True)
                return mm

            def deviations(src, ready, n):
                for ch in range(NC2):
                    pe.wait_ge(s[ready], n + (ch if ready != "x_in" else 0))
                    pe.matmul(ps[:, 4 + ch, :], centre[:], src(ch), start=True, stop=True)\
                        .then_inc(s["ln_dev"], 1)

            def ln_variances(q):
                for ch in range(NC2):
                    pe.wait_ge(s["ln_sq"], NC2 * q + ch + 1)
                    variances(6 + ch, lnB, ch * BANK).then_inc(s["ln_var_ps"], 1)

            def ln_roots(q):
                for ch in range(NC2):
                    pe.wait_ge(s["ln_rstd"], NC2 * q + ch + 1)
                    on_all_rows(6 + ch, ch).then_inc(s["ln_bc"], 1)

            def chunk(ap, ch):
                return ap[:, ch * BANK:(ch + 1) * BANK]

            pe.wait_ge(s["silu_c"], 1)
            for j in range(6):
                mm = pe.matmul(ps[:, 7, j * NB:(j + 1) * NB], wmod_s[:, j * D:(j + 1) * D], silu_c[:],
                               start=True, stop=True)
            mm.then_inc(s["mod_ps"], 1)
            pe.wait_ge(s["x_in"], 16 * NB)
            pe.sem_inc(s["y_acc"], 2 * HALVES)
            for name in ("ss_ps", "pt_ps", "o_ps"):
                pe.sem_inc(s[name], 2)
            pe.wait_ge(s["select_in"], 16)
            pe.wait_ge(s["prep_ok"], 1)
            def prepare(b, norm):
                pe.wait_ge(s["xn_ok"], NC2 * (b + 1))
                for m in range(HALVES):
                    for ch in range(NC2):
                        for k in range(TAPS):
                            mm = pe.matmul(ps[:, 2 * m + ch, :], w_taps[:, k, m * P:(m + 1) * P],
                                           xn[:, ch * BANK + k:ch * BANK + k + BANK],
                                           start=(k == 0), stop=(k == TAPS - 1))
                    mm.then_inc(s["xc_ps"], 1)
                    if m == 0 and norm is not None:
                        deviations(lambda ch: xT[:, b - 1, ch * BANK:(ch + 1) * BANK], "x1_ok", NC2 * (b - 1) + 1)
                if norm is not None:
                    ln_variances(norm)

                def z_proj(m):
                    for ch in range(NC2):
                        o = ch * BANK + TAPS - 1
                        mm = pe.matmul(ps[:, 4 + 2 * m + ch, :], w_in[:, DI + m * P:DI + (m + 1) * P],
                                       xn[:, o:o + BANK], start=True, stop=True)
                    mm.then_inc(s["z_ps"], 1)

                if norm is None:
                    pe.wait_ge(s["ln_kept"], NC2 * N_FIRST)
                else:
                    pe.wait_ge(s["ln_kept"], NC2 * (norm + 1))
                z_proj(0)
                if norm is not None:
                    ln_roots(norm)
                pe.wait_ge(s["u_ok"], HALVES * b + HALVES)
                for ch in range(NC2):
                    for m in range(HALVES):
                        mm = pe.matmul(ps[0:RANK, ch, :], w_x[:, m, 0:RANK], chunk(u[:, m, :], ch),
                                       start=(m == 0), stop=(m == HALVES - 1))
                mm.then_inc(s["dtr_ps"], 1)
                if norm is not None:
                    pe.wait_ge(s["batch_ok"], NC2 * b + 1)
                z_proj(1)

                def dt_proj(m, first):
                    for ch in range(NC2):
                        mm = pe.matmul(ps[:, first + ch, :], w_dt[0:RANK, m * P:(m + 1) * P],
                                       chunk(dtr, ch), start=True, stop=True)
                    mm.then_inc(s["dt_ps"], 1)

                def bc_rows(g, first):
                    for ch in range(NC2):
                        for m in range(HALVES):
                            mm = pe.matmul(ps[0:3 * GRP, first + ch, :],
                                           w_bc[:, m, g, :, :].rearrange("p r n -> p (r n)"),
                                           chunk(u[:, m, :], ch), start=(m == 0), stop=(m == HALVES - 1))
                    mm.then_inc(s["bc_ps"], 1)

                pe.wait_ge(s["dtr_ok"], b + 1)
                dt_proj(0, 2)
                dt_proj(1, 0)
                for g in range(NG):
                    if g < HALVES:
                        pe.wait_ge(s["zs_ok"], HALVES * b + g + 1)
                    else:
                        pe.wait_ge(s["sp_x"], HALVES * b + g - 1)
                    bc_rows(g, BC_BANKS[g])

            def states(b, q, norms):
                pe.wait_ge(s["bc_r1"], NG * (b + 1))
                for m in range(HALVES):
                    for ch in range(NC2):
                        pe.matmul(ps[:, 2 * m + ch, :], diagD[:, m, :], chunk(u[:, m, :], ch),
                                  start=True, stop=False, skip_group_check=True)
                pe.wait_ge(s["bc_ok"], NG * (b + 1))
                def spread_b(n, par, G):
                    pe.wait_ge(s["dbu_ok"], G + 1)
                    for ch in range(NC2):
                        mm = pe.matmul(ps[:, 4 + ch, :], select[0:3 * GRP, n, :],
                                       bcs[0:3 * GRP, par, ch * BANK:(ch + 1) * BANK], start=True, stop=True)
                    mm.then_inc(s["b_ps"], 1)

                def spread_c(n, par, G):
                    pe.wait_ge(s["c_ok"], G + 1)
                    for ch in range(NC2):
                        mm = pe.matmul(ps[:, 6 + ch, :], select[0:3 * GRP, n, :],
                                       bcs[0:3 * GRP, 2 + par, ch * BANK:(ch + 1) * BANK], start=True, stop=True)
                    mm.then_inc(s["c_ps"], 1)

                def sum_half(par, G, m):
                    pe.wait_ge(s["hc_ok"], HALVES * (G + 2) + m + 1)
                    for ch in range(NC2):
                        mm = pe.matmul(ps[:, 2 * m + ch, :], ident[:], chunk(hC[par][:, m, :], ch),
                                       start=False, stop=False, skip_group_check=True)
                    mm.then_inc(s["y_acc"], 1)

                for G in range(LAG):
                    spread_b(G // 2, G % 2, b * NS + G)
                    spread_c(G // 2, G % 2, b * NS + G)
                spread_b(LAG // 2, LAG % 2, b * NS + LAG)
                with pe.Fori(1, GRP - 1) as i:
                    G = b * NS + 2 * i + 1
                    spread_c(i, 1, G)
                    sum_half(0, G - LAG, 0)
                    spread_b(i + 1, 0, G + 1)
                    sum_half(0, G - LAG, 1)
                    spread_c(i + 1, 0, G + 1)
                    sum_half(1, G + 1 - LAG, 0)
                    spread_b(i + 1, 1, G + 2)
                    sum_half(1, G + 1 - LAG, 1)
                G = b * NS + NS - 1
                spread_c(GRP - 1, 1, G)
                halves = [(k, m) for k in range(LAG + 1) for m in range(HALVES)]

                def last_sums(first, end):
                    for k, m in halves[first:end]:
                        sum_half((NS - 1 - LAG + k) % 2, G - LAG + k, m)

                if norms:
                    pe.wait_ge(s["dbu_ok"], G + 2)
                    deviations(lambda ch: xT[:, b + 1, ch * BANK:(ch + 1) * BANK], "x_in", 16 * NB)
                    last_sums(0, 1)
                    pe.wait_ge(s["c_ok"], G + 2)
                    ln_variances(q)
                    last_sums(1, 5)
                    ln_roots(q)
                    last_sums(5, 7)
                    deviations(lambda ch: hf[:, b + 1, ch * BANK:(ch + 1) * BANK], "hres_ok", NC2 * (b + 1) + 1)
                    last_sums(7, 8)
                    ln_variances(q + 1)
                    ln_roots(q + 1)
                    pe.wait_ge(s["ln_kept"], NC2 * (q + 2))
                else:
                    last_sums(0, 8)
                for ch in range(NC2):
                    pe.wait_ge(s["gated"], NC2 * b + ch + 1)
                    for m in range(HALVES):
                        mm = pe.matmul(ps[:, 4 + ch, :], w_out[:, m, :], chunk(zs[:, m, :], ch),
                                       start=(m == 0), stop=(m == HALVES - 1))
                    mm.then_inc(s["mix_ps"], 1)

            deviations(lambda ch: xT[:, 0, ch * BANK:(ch + 1) * BANK], "x_in", 16 * NB)
            ln_variances(0)
            ln_roots(0)
            deviations(lambda ch: hf[:, 0, ch * BANK:(ch + 1) * BANK], "hres_ok", 1)
            ln_variances(1)
            ln_roots(1)
            prepare(0, None)
            with pe.Fori(0, NB - 1) as b:
                q = N_FIRST + N_LN_MAMBA * b
                states(b, q, True)
                prepare(b + 1, q + 2)
            states(NB - 1, None, False)
            q = N_LN_MAMBA * NB - 1
            deviations(lambda ch: xT[:, NB - 1, ch * BANK:(ch + 1) * BANK], "x1_ok", NC2 * (NB - 1) + 1)
            ln_variances(q)
            ln_roots(q)

            def project(I, st):
                ch, j = st // BLOCKS, st % BLOCKS
                col = (j % 2) * INNER + (j // 2) * P
                pe.wait_ge(s["halves_ok"], STEPS * I + st + 1)
                pe.matmul(ps[:, st % 2, :], w_qkv[:, col:col + P], chunk(hs, ch), start=True, stop=True)
                pe.matmul(ps[:, 2 + st % 2, :], w_rot[:, col:col + P], chunk(hs, ch),
                          start=True, stop=True).then_inc(s["qk_ps"], 1)

            def values(I, t):
                pe.wait_ge(s["v_ok"], TOK * I + t + 1)
                pe.matmul(ps[:, 6 + t % 2, :], hs[:, t * P:(t + 1) * P], w_qkv[:, 2 * INNER:],
                          start=True, stop=True).then_inc(s["v_ps"], 1)

            def norms(I, st):
                ch, j = st // BLOCKS, st % BLOCKS
                if j == 0 and ch:
                    pe.wait_ge(s["norm_log"], NC2 * I + ch)
                pe.wait_ge(s["sq_ok"], STEPS * I + st + 3)
                pe.matmul(ps[0:3 * GRP, 4, :], heads[:, j, :], qsq[:, st % 2, :],
                          start=(j == 0), stop=(j == BLOCKS - 1)).then_inc(s["ss_ps"], 1)

            def inverse(I, f):
                ch, j = f // BLOCKS, f % BLOCKS
                pe.wait_ge(s["norm_ok"], NC2 * I + ch + 1)
                if ch:
                    pe.wait_ge(s["qk_ok"], STEPS * I + f + 1)
                elif j > 1:
                    pe.wait_ge(s["qk_ok"], STEPS * I + f)
                else:
                    pe.wait_ge(s["v_ok"], TOK * (I + 1) + 2)
                pe.matmul(ps[:, inv_bank(f), :], unhead[0:3 * GRP, j, :], nparts[0:3 * GRP, :],
                          start=True, stop=True).then_inc(s["inv_ps"], 1)

            def scores(I, g):
                quad, hp = g // PAIRS, g % PAIRS
                ch = quad * QUAD // CQ
                pe.wait_ge(s["shifted"], GROUPS * I + g + 1)
                pe.wait_ge(s["qk_ok"], STEPS * I + ch * BLOCKS + 2 * hp + 3)
                pe.matmul(ps[:, g % 2, :], ident16[:], mask[:, min(quad, 1), :], start=True, stop=False,
                          skip_group_check=True)
                for i in range(QUAD):
                    w = quad * QUAD + i
                    mm = pe.matmul(ps[:, g % 2, i * P:(i + 1) * P], qbd[:, hp, w, :],
                                   kT[:, hp, w * WIN:(w + 2) * WIN], start=False, stop=True,
                                   skip_group_check=True)
                mm.then_inc(s["sim_ps"], 1)

            def turn(I, g):
                n = GROUPS * I + g
                pe.wait_ge(s["prob_ok"], n + 3)
                pe.wait_ge(s["pt_ok"], n + 1)
                for i in range(QUAD):
                    mm = pe.transpose(ps[:, 2 + g % 2, i * P:(i + 1) * P], pr[:, g % 2, i * P:(i + 1) * P],
                                      ident[:])
                mm.then_inc(s["pt_ps"], 1)

            def weigh(I, g):
                quad, hp = g // PAIRS, g % PAIRS
                n = GROUPS * I + g
                pe.wait_ge(s["pt_ok"], n + 3)
                pe.wait_ge(s[f"v_moved{quad * QUAD // CQ}"], 32 * (I + 1))
                pe.wait_ge(s["o_ok"], n + 1)
                for i in range(QUAD):
                    mm = pe.matmul(ps[:, 4, i * P:(i + 1) * P], vtok[:, quad * QUAD + i, hp * P:(hp + 1) * P],
                                   pT[:, g % 2, i * P:(i + 1) * P], start=True, stop=True)
                mm.then_inc(s["o_ps"], 1)

            def out_proj(l, I, ch, bank):
                pe.wait_ge(s["wo_in"], 16 * (l + 1))
                pe.wait_ge(s["o_ok"], GROUPS * I + (ch + 1) * GROUPS // NC2 + 1)
                for hp in range(PAIRS):
                    mm = pe.matmul(ps[:, bank, :], w_o[:, hp, :], oT[:, hp, :],
                                   start=(hp == 0), stop=(hp == PAIRS - 1))
                mm.then_inc(s["wo_ps"], 1)

            def ffn_norm(J, step):
                if step not in LN_AT:
                    return
                what, ch = LN_AT[step]
                K = NC2 * J + ch
                if what == "dev":
                    pe.wait_ge(s["fs_ok"], J + 1)
                    if ch:
                        pe.wait_ge(s["f_in"], K)
                    pe.matmul(ps[:, 5, :], centre[:], chunk(fs, ch), start=True, stop=True).then_inc(s["f_dev"], 1)
                if what == "var":
                    pe.wait_ge(s["f_kept"], K + 1)
                    variances(5, fsq, 0).then_inc(s["f_var"], 1)
                if what == "norm":
                    pe.wait_ge(s["f_rstd"], K + 1)
                    on_all_rows(5, ch).then_inc(s["f_bc"], 1)

            def ffn_piece(l, J, step, alone=False):
                if step not in FFN_AT:
                    return
                what, ch, f = FFN_AT[step]
                K = NC2 * J + ch
                if what == "ag":
                    rows, o = FROWS[f], f * P
                    pe.wait_ge(s["ffn_in"], 16 * N_FFN * (l + 1))
                    pe.wait_ge(s["f_in"], K + 1)
                    a_bank, g_bank = row_banks(f, alone)
                    before = f - 1 if alone else f
                    if f and before:
                        pe.wait_ge(s["av_ok"], FB * K + before)
                        pe.wait_ge(s["g_ok"], FB * K + before)
                    elif ch and not f:
                        pe.wait_ge(s["f_out"], K + 1)
                    pe.matmul(ps[0:rows, a_bank, :], w_1[:, o:o + rows], chunk(fin, ch), start=True, stop=True)
                    pe.matmul(ps[0:rows, g_bank, :], w_1[:, HID + o:HID + o + rows], chunk(fin, ch),
                              start=True, stop=True).then_inc(s["ag_ps"], 1)
                if what == "w2":
                    pe.wait_ge(s["ff_ok"], K + 2)
                    for f, rows in enumerate(FROWS):
                        mm = pe.matmul(ps[:, 6, :], w_2[0:rows, f, :], abuf[0:rows, f * BANK:(f + 1) * BANK],
                                       start=(f == 0), stop=(f == FB - 1))
                    mm.then_inc(s["w2_ps"], 1)

            def body(l, I, lj, J):
                pe.wait_ge(s["hs_ok"], I + 1)
                pe.wait_ge(s["pt_ok"], GROUPS * I + 2)
                for st in range(STEPS + 1):
                    if st < STEPS:
                        project(I, st)
                    if st == 1 and J is not None:
                        pe.wait_ge(s["attn_ok"], NC2 * J + 1)
                        out_proj(lj, J, 1, 5)
                    if st in INV_AT:
                        inverse(I, 2 * (st - min(INV_AT)))
                    if st < TOK:
                        values(I, st)
                    if st in INV_AT:
                        inverse(I, 2 * (st - min(INV_AT)) + 1)
                    if st >= 1:
                        norms(I, st - 1)
                    if J is not None:
                        ffn_norm(J, st)
                pe.wait_ge(s["qk_ok"], STEPS * I + BLOCKS + 1)
                if J is not None:
                    pe.wait_ge(s["f_in"], NC2 * (J + 1))
                scores(I, 0)
                for g in range(GROUPS + 3):
                    for j in FINAL_AT.get(g, ())[:1]:
                        inverse(I, BLOCKS + j)
                    if g + 1 < GROUPS:
                        scores(I, g + 1)
                    if g == WO_AT:
                        pe.wait_ge(s["qk_ok"], STEPS * (I + 1) + 1)
                        out_proj(l, I, 0, 5)
                    if 2 <= g < GROUPS + 2:
                        turn(I, g - 2)
                    if g >= 3:
                        weigh(I, g - 3)
                    for j in FINAL_AT.get(g, ())[1:]:
                        inverse(I, BLOCKS + j)
                    if J is not None:
                        ffn_piece(lj, J, g)

            pe.wait_ge(s["select_in"], 48)
            pe.wait_ge(s["ident16_ok"], 1)
            for l in range(LAYERS):
                pe.wait_ge(s["weights_ok"], 6 * (l + 1))
                first = l * NB
                body(l, first, l - 1, first - 1 if l else None)
                passed(pe)
                with pe.Fori(1, NB) as b:
                    body(l, first + b, l, first + b - 1)
            J = LAYERS * NB - 1
            pe.wait_ge(s["attn_ok"], NC2 * J + 1)
            out_proj(LAYERS - 1, J, 1, 5)
            for step in LN_AT:
                ffn_norm(J, step)
            for step in FFN_AT:
                ffn_piece(LAYERS - 1, J, step, alone=True)

        @block.scalar
        def _(act):
            own = Steps(act, s["act_step"])

            def ln_squares(q):
                for ch in range(NC2):
                    act.wait_ge(s["ln_dev"], NC2 * q + ch + 1)
                    act.activation(lnB[:, ch * BANK:(ch + 1) * BANK], ps[:, 4 + ch, :], ACT.Square)\
                        .then_inc(s["ln_sq"], 1)

            def ln_eps(q):
                for ch in range(NC2):
                    act.wait_ge(s["ln_var_ps"], NC2 * q + ch + 1)
                    act.activation(ln_var[:, ch, :], ps[:, 6 + ch, 0:TILES], ACT.Identity, bias=epsv[:, 0:1])\
                        .then_inc(s["ln_eps"], 1)

            act.sem_inc(s["c_ok"], 1)
            act.wait_ge(s["mod_in"], 16 * len(mod_loads))
            act.activation(silu_c[:], at["c"], ACT.Silu).then_inc(s["silu_c"], 1)
            act.wait_ge(s["mamba_in"], 16 * len(mamba_loads))
            table(act, EXP)
            own.done(act.activation(A, A, ACT.Exp))
            own.wait()
            act.mul(A, A, -1.0).then_inc(s["a_ok"], 1)
            act.wait_ge(s["consts_ok"], 1)
            act.wait_ge(s["a_ok"], 1)

            def prepare(b, norm):
                for m in range(HALVES):
                    act.wait_ge(s["xc_ps"], HALVES * b + m + 1)
                    act.activation(u[:, m, :], banks(2 * m), ACT.Silu, bias=at["conv_b"][:, m:m + 1])\
                        .then_inc(s["u_ok"], 1)
                    if norm is not None:
                        [ln_squares, ln_eps][m](norm)
                for m in range(HALVES):
                    act.wait_ge(s["z_ps"], HALVES * b + m + 1)
                    act.activation(zs[:, m, :], banks(4 + 2 * m), ACT.Silu).then_inc(s["zs_ok"], 1)
                table(act, EXP)
                for m in range(HALVES):
                    act.wait_ge(s["dt_ps"], HALVES * b + m + 1)
                    act.activation(spY[:, m, :], banks(2 - 2 * m), ACT.Abs, bias=at["b_dt"][:, m:m + 1])\
                        .then_inc(s["sp_abs"], 1)
                    act.activation(spX[:, m, :], banks(2 - 2 * m), ACT.Relu, bias=at["b_dt"][:, m:m + 1])\
                        .then_inc(s["sp_x"], 1)
                    act.wait_ge(s["sp_abs"], HALVES * b + m + 1)
                    act.activation(spY[:, m, :], spY[:, m, :], ACT.Exp, scale=-1.0).then_inc(s["sp_y"], 1)

                def first_part(g):
                    act.wait_ge(s["bc_ps"], NG * b + g + 1)
                    act.copy(bcs[0:3 * GRP, g, :], banks(BC_BANKS[g], rows=slice(0, 3 * GRP))).then_inc(s["bc_hi"], 1)

                def second_part(g):
                    rows = slice(0, 2 * GRP)
                    act.wait_ge(s["bc_r1"], NG * b + g + 1)
                    act.copy(bcs[rows, g, :], left(g, rows)).then_inc(s["bc_mid"], 1)

                first_part(0)
                first_part(1)
                act.wait_ge(s["sp_y"], HALVES * (b + 1))
                table(act, LOG)
                act.activation(spL, spY, ACT.Ln, bias=epsv[:, 1:2]).then_inc(s["sp_ok"], 1)
                second_part(0)
                first_part(2)
                second_part(1)
                first_part(3)
                second_part(2)
                second_part(3)

            def states(b):
                def state(n, par, G):
                    act.wait_ge(s["h_ok"], G + 1)
                    for m in range(HALVES):
                        e = act.activation(dA[par][:, m, 1:L], delta[:, m, 1:L], ACT.Exp, scale=n(m))
                    e.then_inc(s["da_ok"], 1)
                    act.wait_ge(s["c_ps"], G + 1)
                    act.wait_ge(s["hc_ok"], HALVES * (G + 1))
                    act.copy(Csb[par], banks(6)).then_inc(s["c_ok"], 1)

                act.wait_ge(s["sp_ok"], b + 1)
                table(act, EXP)
                act.wait_ge(s["du_ok"], HALVES * (b + 1))
                passed(act)
                with act.Fori(0, GRP) as i:
                    for par in range(2):
                        state(lambda m: A[:, m, bass.ds(i + par * GRP, 1)], par, b * NS + 2 * i + par)

            for q in range(N_FIRST):
                ln_squares(q)
                ln_eps(q)
            prepare(0, None)
            passed(act)
            with act.Fori(0, NB - 1) as b:
                q = N_FIRST + N_LN_MAMBA * b
                states(b)
                for k in range(N_FIRST):
                    ln_squares(q + k)
                    ln_eps(q + k)
                prepare(b + 1, q + 2)
            states(NB - 1)
            ln_squares(N_LN_MAMBA * NB - 1)
            ln_eps(N_LN_MAMBA * NB - 1)

            def squares(I, st):
                n = STEPS * I + st
                act.wait_ge(s["qk_ps"], n + 1)
                act.wait_ge(s["ss_ps"], n + 1)
                act.activation(qsq[:, st % 2, :], ps[:, st % 2, :], ACT.Square).then_inc(s["sq_ok"], 1)

            def value_copy(I, t):
                act.wait_ge(s["v_ps"], TOK * I + t + 1)
                act.copy(vtok[:, 2 * t + 1, :], ps[:, 6 + t % 2, :]).then_inc(s["v_ok"], 1)

            def norm_piece(I, ch, k):
                K = NC2 * I + ch
                rows = slice(0, 3 * GRP)
                if k == 0:
                    act.wait_ge(s["ss_ps"], STEPS * I + BLOCKS * (ch + 1) + 2)
                    if ch:
                        act.wait_ge(s["norm_ok"], K)
                    table(act, LOG)
                    act.activation(nlog[rows, :], ps[rows, 4, :], ACT.Ln, scale=float(2 ** NORM_SHIFT),
                                   bias=epsv[rows, 2:3]).then_inc(s["norm_log"], 1)
                    table(act, EXP)
                    act.wait_ge(s["norm_log"], K + 1)
                    act.activation(ninv[rows, :], nlog[rows, :], ACT.Exp, scale=-0.5,
                                   bias=epsv[rows, 3:4]).then_inc(s["norm_exp"], 1)
                if k == 1:
                    act.wait_ge(s["norm_min"], K + 1)
                    if ch:
                        act.wait_ge(s["inv_ps"], STEPS * I + BLOCKS)
                    act.copy(nparts[rows, :], ninv[rows, :]).then_inc(s["norm_hi"], 1)
                if k == 2:
                    act.wait_ge(s["norm_rest"], K + 1)
                    rows = slice(0, 2 * GRP)
                    act.copy(nparts[rows, :], nrest[rows, :]).then_inc(s["norm_mid"], 1)

            def exps(I, g):
                n = GROUPS * I + g
                act.wait_ge(s["shifted"], n + 3)
                act.wait_ge(s["prob_ok"], n + 1)
                act.activation(ex[:, g % 2, :], sc[:, g % 2, :], ACT.Exp).then_inc(s["exp_ok"], 1)

            def turned(I, g):
                n = GROUPS * I + g
                act.wait_ge(s["pt_ps"], n + 3)
                act.wait_ge(s["o_ps"], n + 1)
                act.copy(pT[:, g % 2, :], ps[:, 2 + g % 2, :]).then_inc(s["pt_ok"], 1)

            def heads_out(I, g):
                quad, hp = g // PAIRS, g % PAIRS
                act.wait_ge(s["o_ps"], GROUPS * I + g + 3)
                if g == GROUPS // NC2:
                    act.wait_ge(s["wo_ps"], NC2 * I + 1)
                for h in range(2):
                    rows = slice(h * DH, (h + 1) * DH)
                    o = (quad * QUAD % CQ) * WIN
                    cp = act.copy(oT[rows, hp, o:o + QUAD * WIN].rearrange("p (w i) -> p w i", i=WIN),
                                  ps[rows, 4, :].rearrange("p (w i) -> p w i", i=P)[:, :, h * WIN:(h + 1) * WIN])
                cp.then_inc(s["o_ok"], 1)

            def ffn_norm(J, step):
                if step not in LN_AT:
                    return
                what, ch = LN_AT[step]
                K = NC2 * J + ch
                if what == "dev":
                    act.wait_ge(s["f_dev"], K + 1)
                    act.activation(fsq, ps[:, 5, :], ACT.Square).then_inc(s["f_sq"], 1)
                if what == "var":
                    act.wait_ge(s["f_var"], K + 1)
                    act.activation(ln_var[:, ch, :], ps[:, 5, 0:TILES], ACT.Identity, bias=epsv[:, 0:1])\
                        .then_inc(s["f_eps"], 1)

            def ffn_piece(l, J, step):
                if step in FFN_AT:
                    what, ch, f = FFN_AT[step]
                    K = NC2 * J + ch
                    if what == "ag":
                        rows = FROWS[f]
                        act.wait_ge(s["ag_ps"], FB * K + f + 1)
                        if f == 0:
                            act.wait_ge(s["ff_ok"], K + 1)
                        passed(act)
                        act.activation(gbuf[0:rows, f * BANK:(f + 1) * BANK], ps[0:rows, 7, :], ACT.Identity,
                                       bias=b1s[0:rows, bass.ds(l, 1), 1, f]).then_inc(s["g_ok"], 1)
                if step in GELU_AT:
                    K = NC2 * J + GELU_AT[step]
                    act.wait_ge(s["g_ok"], FB * K + FB)
                    table(act, GELU)
                    act.activation(gbuf, gbuf, ACT.Gelu).then_inc(s["gelu_ok"], 1)
                    table(act, EXP)

            def body(I, lj, J):
                act.wait_ge(s["o_ps"], GROUPS * I + 2)
                for st in range(STEPS + 1):
                    if st < STEPS:
                        squares(I, st)
                    if st < TOK:
                        value_copy(I, st)
                    if st in NORM_AT:
                        norm_piece(I, 0, NORM_AT.index(st))
                    if st == STEPS:
                        norm_piece(I, 1, 0)
                    if J is not None:
                        ffn_norm(J, st)
                for g in range(GROUPS + 3):
                    if g < GROUPS:
                        exps(I, g)
                    if 2 <= g < GROUPS + 2:
                        turned(I, g - 2)
                    if g >= 3:
                        heads_out(I, g - 3)
                    if g < 2:
                        norm_piece(I, 1, g + 1)
                    if J is not None:
                        ffn_piece(lj, J, g)

            for name in ("v_ok", "sq_ok", "exp_ok", "pt_ok"):
                act.sem_inc(s[name], 2)
            act.sem_inc(s["o_ok"], 1)
            for l in range(LAYERS):
                first = l * NB
                body(first, l - 1, first - 1 if l else None)
                passed(act)
                with act.Fori(1, NB) as b:
                    body(first + b, l, first + b - 1)
            for step in LN_AT:
                ffn_norm(LAYERS * NB - 1, step)
            table(act, GELU)
            for what, ch, f in FFN_AT.values():
                if what == "ag":
                    K, rows = NC2 * (LAYERS * NB - 1) + ch, FROWS[f]
                    act.wait_ge(s["ag_ps"], FB * K + f + 1)
                    if f == 0:
                        act.wait_ge(s["ff_ok"], K + 1)
                    act.activation(gbuf[0:rows, f * BANK:(f + 1) * BANK],
                                   ps[0:rows, row_banks(f, True)[1], :], ACT.Gelu,
                                   bias=b1s[0:rows, LAYERS - 1, 1, f:f + 1]).then_inc(s["g_ok"], 1)

        @block.vector
        def _(dve):
            own = Steps(dve, s["vec_step"])

            def ln_keep(q):
                for ch in range(NC2):
                    dve.wait_ge(s["ln_sq"], NC2 * q + ch + 1)
                    dve.tensor_copy(lnA[:, ch * BANK:(ch + 1) * BANK], ps[:, 4 + ch, :]).then_inc(s["ln_kept"], 1)

            def ln_end(dst, scale, shift, q, inc):
                for ch in range(NC2):
                    cols = slice(ch * BANK, (ch + 1) * BANK)
                    dve.wait_ge(s["ln_kept"], NC2 * q + ch + 1)
                    dve.wait_ge(s["ln_bc"], NC2 * q + ch + 1)
                    own.done(dve.tensor_tensor(lnA[:, cols], lnA[:, cols], ps[:, 6 + ch, :], ALU.mult))
                    own.wait()
                    dve.tensor_scalar(dst[:, cols], lnA[:, cols], scale, shift, ALU.mult, ALU.add)\
                        .then_inc(s[inc], 1)

            dve.sem_inc(s["batch_ok"], 1)
            dve.sem_inc(s["dbu_ok"], 1)
            dve.sem_inc(s["h_ok"], 2)
            dve.memset(epsv[:, 0:1], EPS)
            dve.memset(mean_col[:], 1.0 / P)
            dve.memset(epsv[:, 1:2], 1.0)
            dve.memset(epsv[:, 2:3], 2.0 ** -63)
            dve.memset(epsv[:, 3:4], NORM_SHIFT / 2 * LN2)
            for par in range(2):
                dve.memset(dA[par][:, :, 0:1], 0.0)
            dve.memset(xn[:, 0:TAPS - 1], 0.0).then_inc(s["consts_ok"], 1)

            dve.wait_ge(s["mod_ps"], 1)
            dve.tensor_copy(mod[:].rearrange("p a b -> p (a b)"), ps[:, 7, 0:6 * NB]).then_inc(s["mod_sb"], 1)
            dve.wait_ge(s["mod_sb"], 1)
            for j in range(2):
                g = mod[:, 2 + 3 * j, :]
                own.done(dve.tensor_scalar(mod[:, 1 + 3 * j, :], mod[:, 1 + 3 * j, :], 1.0, None, ALU.add))
                own.done(dve.tensor_scalar(gtmp[:, j, 0, :], g, -1.0, None, ALU.mult))
                own.wait()
                own.done(dve.tensor_tensor(gtmp[:, j, 0, :], gtmp[:, j, 0, :], g, ALU.max))
                own.done(dve.tensor_scalar(gtmp[:, j, 1, :], g, 0.0, 2.0, ALU.is_ge, ALU.mult))
                own.wait()
                own.done(dve.tensor_scalar(gtmp[:, j, 0, :], gtmp[:, j, 0, :], 0.25, None, ALU.max))
                own.wait()
                own.done(dve.scalar_tensor_tensor(gate[:, j, :], gtmp[:, j, 1, :], -1.0, gtmp[:, j, 0, :],
                                                  ALU.add, ALU.mult))
            own.wait()
            dve.wait_ge(s["mamba_in"], 16 * len(mamba_loads))
            dve.wait_ge(s["mod_in"], 16 * len(mod_loads))
            cw = convw.rearrange("p (d k) -> p k d", k=TAPS)
            for k in range(TAPS):
                dve.tensor_tensor(w_taps[:, k, :], w_in[:, 0:DI], cw[:, k, :], ALU.mult)
            for m in range(HALVES):
                for r in range(3):
                    dve.tensor_copy(w_bc[:, m, :, r, :],
                                    w_x[:, m, RANK:].rearrange("p (g n) -> p g n", n=GRP))
                own.done(dve.tensor_scalar(diagD[:, m, :], ident[:], at["D"][:, m:m + 1], None, ALU.mult))
            own.wait()
            dve.sem_inc(s["prep_ok"], 1)

            dve.wait_ge(s["x_in"], 16 * NB)

            def hres_end(b, q):
                ln_end(hf[:, b, :], mod[:, 1, bass.ds(b, 1)], mod[:, 0, bass.ds(b, 1)], q, "hres_ok")

            def xn_end(q):
                ln_end(xn[:, TAPS - 1:], at["ln_w"], at["ln_b"], q, "xn_ok")

            def prepare(b, norm):
                if norm is not None:
                    ln_keep(norm)
                    ln_end(hf[:, b - 1, :], mod[:, 4, bass.ds(b - 1, 1)], mod[:, 3, bass.ds(b - 1, 1)], norm,
                           "batch_ok")
                dve.wait_ge(s["dtr_ps"], b + 1)
                dve.tensor_copy(dtr, banks(0, rows=slice(0, RANK))).then_inc(s["dtr_ok"], 1)
                def rest(g):
                    rows = slice(0, 2 * GRP)
                    dve.wait_ge(s["bc_hi"], NG * b + g + 1)
                    dve.tensor_tensor(left(g, rows), banks(BC_BANKS[g], rows=rows), bcs[rows, g, :], ALU.subtract)\
                        .then_inc(s["bc_r1"], 1)

                def series(m):
                    y, t = spY[:, m, :], spT[:, m, :]
                    dve.wait_ge(s["sp_y"], HALVES * b + m + 1)
                    own.done(dve.tensor_scalar(t, y, -0.25, 1.0 / 3.0, ALU.mult, ALU.add))
                    own.wait()
                    own.done(dve.tensor_tensor(t, t, y, ALU.mult))
                    own.wait()
                    own.done(dve.scalar_tensor_tensor(t, t, -0.5, y, ALU.add, ALU.mult))
                    own.wait()
                    own.done(dve.scalar_tensor_tensor(t, t, 1.0, y, ALU.add, ALU.mult))

                def softplus_end(m):
                    t, d = spT[:, m, :], delta[:, m, :]
                    dve.wait_ge(s["sp_ok"], b + 1)
                    own.done(dve.scalar_tensor_tensor(t, spL[:, m, :], -LN_SLACK, t, ALU.add, ALU.max))
                    own.wait()
                    dve.wait_ge(s["sp_x"], HALVES * (b + 1))
                    own.done(dve.tensor_tensor(d, spX[:, m, :], t, ALU.add))
                    own.wait()
                    dve.tensor_tensor(du[:, m, :], d, u[:, m, :], ALU.mult).then_inc(s["du_ok"], 1)

                series(0)
                rest(0)
                series(1)
                for g in range(1, NG):
                    rest(g)
                own.wait()
                for m in range(HALVES):
                    softplus_end(m)

            def states(b):
                dve.wait_ge(s["du_ok"], HALVES * (b + 1))

                def inject(par, G):
                    dve.wait_ge(s["b_ps"], G + 1)
                    dve.wait_ge(s["h_ok"], G + 1)
                    bb2 = banks(4).unsqueeze(1).broadcast_to([P, HALVES, L])
                    dve.tensor_tensor(dBu[par], du, bb2, ALU.mult).then_inc(s["dbu_ok"], 1)

                def scan(par, G):
                    dve.wait_ge(s["dbu_ok"], G + 2)
                    dve.wait_ge(s["da_ok"], G + 1)
                    dve.wait_ge(s["hc_ok"], HALVES * (G + 1))
                    flat = [t[par].rearrange("p a n -> p (a n)") for t in (hst, dA, dBu)]
                    dve.tensor_tensor_scan(flat[0], flat[1], flat[2], 0.0, ALU.mult, ALU.add)\
                        .then_inc(s["h_ok"], 1)

                inject(0, b * NS)
                with dve.Fori(0, GRP - 1) as i:
                    G = b * NS + 2 * i
                    inject(1, G + 1)
                    scan(0, G)
                    inject(0, G + 2)
                    scan(1, G + 1)
                G = b * NS + NS - 2
                inject(1, G + 1)
                scan(0, G)
                scan(1, G + 1)

            def finish(b, q, norms):
                if norms:
                    ln_keep(q)
                G = b * NS + NS - 1
                dve.wait_ge(s["h_ok"], G + 3)
                dve.wait_ge(s["c_ok"], G + 2)
                for m in range(HALVES):
                    dve.wait_ge(s["y_acc"], HALVES * G + m + 1)
                    dve.tensor_tensor(hC[1][:, m, :], hst[1][:, m, :], Csb[1], ALU.mult).then_inc(s["hc_last"], 1)
                if norms:
                    hres_end(b + 1, q)
                    ln_keep(q + 1)
                dve.wait_ge(s["y_acc"], HALVES * (NS * b + NS + 2))
                y = ps[:, 0:4, :].rearrange("p (a c) n -> p a c n", a=HALVES)
                for ch in range(NC2):
                    z = zs[:, :, ch * BANK:(ch + 1) * BANK]
                    dve.tensor_tensor(z, y[:, :, ch, :], z, ALU.mult).then_inc(s["gated"], 1)
                if norms:
                    xn_end(q + 1)
                for ch in range(NC2):
                    cols = slice(ch * BANK, (ch + 1) * BANK)
                    dve.wait_ge(s["mix_ps"], NC2 * b + ch + 1)
                    own.done(dve.tensor_tensor(lnA[:, cols], ps[:, 4 + ch, :], hf[:, b, cols], ALU.add))
                    own.wait()
                    dve.scalar_tensor_tensor(xT[:, b, cols], lnA[:, cols], gate[:, 0, bass.ds(b, 1)],
                                             xT[:, b, cols], ALU.mult, ALU.add).then_inc(s["x1_ok"], 1)

            ln_keep(0)
            hres_end(0, 0)
            ln_keep(1)
            xn_end(1)
            prepare(0, None)
            OWN_PREPARE, OWN_FINISH = 6 * HALVES, (N_FIRST + 1) * NC2
            passed(dve)
            with dve.Fori(0, NB - 1) as b:
                own.enter(b, OWN_PREPARE + OWN_FINISH + NC2)
                q = N_FIRST + N_LN_MAMBA * b
                states(b)
                finish(b, q, True)
                prepare(b + 1, q + 2)
                own.leave(NB - 1)
            states(NB - 1)
            finish(NB - 1, None, False)
            q = N_LN_MAMBA * NB - 1
            ln_keep(q)
            ln_end(hf[:, NB - 1, :], mod[:, 4, NB - 1:NB], mod[:, 3, NB - 1:NB], q, "batch_ok")

            for name in ("halves_ok", "shifted"):
                dve.sem_inc(s[name], 2)
            for name in ("qk_ok", "f_out"):
                dve.sem_inc(s[name], 1)
            dve.wait_ge(s["batch_ok"], NC2 * NB + 1)
            dve.wait_ge(s["parked"], 16 * NB)
            dve.tensor_copy(ident16[:], ident[:]).then_inc(s["ident16_ok"], 1)
            dve.memset(kT[:, :, 0:WIN], 0.0)
            dve.memset(vtok[0:WIN, 0, :], 0.0)
            dve.memset(gbuf[:, L:], 0.0)

            def shift_to(dst, b):
                dve.tensor_copy(dst[0:DH, :], hf[0:DH, b, :])
                return dve.tensor_copy(dst[DH:P, 1:L], hf[DH:P, b, 0:L - 1])

            def halves(I, st):
                ch, j = st // BLOCKS, st % BLOCKS
                n = STEPS * I + st
                t = 2 * (j % 2)
                cols = slice(ch * BANK, (ch + 1) * BANK)
                dve.wait_ge(s["sq_ok"], n + 3)
                dve.wait_ge(s["raw_ok"], n + 1)
                dve.tensor_tensor(qcos[:, st % 2, :], ps[:, st % 2, :], tables[:, t, cols], ALU.mult)
                dve.tensor_tensor(qsin[:, st % 2, :], ps[:, 2 + st % 2, :], tables[:, t + 1, cols], ALU.mult)\
                    .then_inc(s["halves_ok"], 1)

            def norm_piece(I, ch, k):
                K = NC2 * I + ch
                rows = slice(0, 3 * GRP)
                if k == 0:
                    dve.wait_ge(s["norm_exp"], K + 1)
                    dve.tensor_scalar(ninv[rows, :], ninv[rows, :], 1e12, None, ALU.min).then_inc(s["norm_min"], 1)
                if k == 1:
                    dve.wait_ge(s["norm_hi"], K + 1)
                    dve.tensor_tensor(nrest[rows, :], ninv[rows, :], nparts[rows, :], ALU.subtract)\
                        .then_inc(s["norm_rest"], 1)
                if k == 2:
                    dve.wait_ge(s["norm_mid"], K + 1)
                    third = slice(GRP, 2 * GRP)
                    dve.tensor_tensor(nparts[third, :], nrest[third, :], nparts[third, :], ALU.subtract)\
                        .then_inc(s["norm_ok"], 1)

            def scaled(I, f):
                ch, j = f // BLOCKS, f % BLOCKS
                hp, n = j // 2, STEPS * I + f
                dve.wait_ge(s["qbd_ok"], 1)
                dve.wait_ge(s["inv_ps"], n + 1)
                dve.wait_ge(s["raw_ok"], n + 3)
                if j % 2:
                    kk = kT[:, hp, WIN + ch * BANK:WIN + (ch + 1) * BANK]
                    dve.tensor_tensor(kk, kk, ps[:, inv_bank(f), :], ALU.mult).then_inc(s["qk_ok"], 1)
                else:
                    for h in range(2):
                        rows = slice(h * DH, (h + 1) * DH)
                        win = "p (w i) -> p w i"
                        tt = dve.tensor_tensor(qbd[rows, hp, ch * CQ:(ch + 1) * CQ, h * WIN:(h + 1) * WIN],
                                               qraw[ch][rows, hp, :].rearrange(win, i=WIN),
                                               ps[rows, inv_bank(f), :].rearrange(win, i=WIN), ALU.mult)
                    tt.then_inc(s["qk_ok"], 1)

            def row_max(I, g):
                dve.wait_ge(s["sim_ps"], GROUPS * I + g + 1)
                dve.tensor_reduce(smax[:, g % 2, :], ps[:, g % 2, :].rearrange("p (w j) -> p w j", j=P),
                                  AX, ALU.max).then_inc(s["max_ok"], 1)

            def shift_in(I, g):
                n = GROUPS * I + g
                dve.wait_ge(s["max_ok"], n + 1)
                dve.wait_ge(s["exp_ok"], n + 1)
                dve.tensor_tensor(sc[:, g % 2, :].rearrange("p (w j) -> p w j", j=P),
                                  ps[:, g % 2, :].rearrange("p (w j) -> p w j", j=P),
                                  smax[:, g % 2, :].unsqueeze(2).broadcast_to([P, QUAD, P]),
                                  ALU.subtract).then_inc(s["shifted"], 1)

            def row_sum(I, g):
                dve.wait_ge(s["exp_ok"], GROUPS * I + g + 3)
                dve.tensor_reduce(ssum[:, g % 2, :], ex[:, g % 2, :].rearrange("p (w j) -> p w j", j=P),
                                  AX, ALU.add).then_inc(s["sum_ok"], 1)

            def row_rec(I, g):
                n = GROUPS * I + g
                dve.wait_ge(s["sum_ok"], n + 1)
                dve.wait_ge(s["prob_ok"], n + 1)
                dve.reciprocal(srec[:, g % 2, :], ssum[:, g % 2, :]).then_inc(s["rsum_ok"], 1)

            def attn_add(I, b, ch, bank):
                cols = slice(ch * BANK, (ch + 1) * BANK)
                dve.wait_ge(s["wo_ps"], NC2 * I + ch + 1)
                dve.tensor_tensor(hf[:, b, cols], hf[:, b, cols], ps[:, bank, :], ALU.add).then_inc(s["attn_ok"], 1)

            def close(J, b):
                attn_add(J, b, 1, 5)
                dve.wait_ge(s["attn_ok"], NC2 * J + 2)
                passed(dve)
                dve.memset(fs[DH:P, 0:1], 0.0)
                shift_to(fs, b).then_inc(s["fs_ok"], 1)

            def ffn_norm(l, J, step):
                if step not in LN_AT:
                    return
                what, ch = LN_AT[step]
                K = NC2 * J + ch
                if what == "dev":
                    dve.wait_ge(s["f_sq"], K + 1)
                    dve.tensor_copy(fdev, ps[:, 5, :]).then_inc(s["f_kept"], 1)
                if what == "norm":
                    dve.wait_ge(s["f_kept"], K + 1)
                    dve.wait_ge(s["f_bc"], K + 1)
                    dve.tensor_tensor(fdev, fdev, ps[:, 5, :], ALU.mult).then_inc(s["f_norm"], 1)
                    dve.wait_ge(s["f_norm"], K + 1)
                    dve.tensor_scalar(fin[:, ch * BANK:(ch + 1) * BANK], fdev, at["ln_g"][:, l:l + 1],
                                      at["ln_b2"][:, l:l + 1], ALU.mult, ALU.add).then_inc(s["f_in"], 1)

            def ffn_piece(l, J, b, step, alone=False):
                ll = bass.ds(l, 1)
                if step not in FFN_AT:
                    return
                what, ch, f = FFN_AT[step]
                K = NC2 * J + ch
                if what == "ag":
                    rows = FROWS[f]
                    dve.wait_ge(s["ag_ps"], FB * K + f + 1)
                    dve.tensor_scalar(abuf[0:rows, f * BANK:(f + 1) * BANK],
                                      ps[0:rows, row_banks(f, alone)[0], :],
                                      b1s[0:rows, ll, 0, f], None, ALU.add).then_inc(s["av_ok"], 1)
                if what == "w2":
                    cols = slice(ch * BANK, (ch + 1) * BANK)
                    dve.wait_ge(s["w2_ps"], K + 1)
                    dve.scalar_tensor_tensor(hf[:, b, cols], ps[:, 6, :], at["b2"][:, ll], hf[:, b, cols],
                                             ALU.add, ALU.add).then_inc(s["f_out"], 1)

            def body(l, b, I, lj, bj, J):
                if l:
                    dve.wait_ge(s["f_out"], NC2 * (I - NB + 1) + 1)
                    passed(dve)
                dve.memset(hs[DH:P, 0:1], 0.0)
                shift_to(hs, b).then_inc(s["hs_ok"], 1)
                dve.wait_ge(s["prob_ok"], GROUPS * I + 2)
                for st in range(STEPS + 1):
                    if st in INV_AT:
                        scaled(I, 2 * (st - min(INV_AT)))
                    if st < STEPS:
                        halves(I, st)
                    if st == 1 and J is not None:
                        close(J, bj)
                    if st - 1 in NORM_AT:
                        norm_piece(I, 0, NORM_AT.index(st - 1))
                    if st in INV_AT:
                        scaled(I, 2 * (st - min(INV_AT)) + 1)
                    if J is not None:
                        ffn_norm(lj, J, st)
                dve.wait_ge(s["raw_ok"], STEPS * (I + 1) + 2)
                for g in range(GROUPS + 3):
                    if 1 <= g <= GROUPS:
                        row_sum(I, g - 1)
                    if g < GROUPS:
                        row_max(I, g)
                    if 1 <= g <= GROUPS:
                        row_rec(I, g - 1)
                    if g < GROUPS:
                        shift_in(I, g)
                    if g < 3:
                        norm_piece(I, 1, g)
                    for j in FINAL_AT.get(g, ()):
                        scaled(I, BLOCKS + j)
                    if J is not None:
                        ffn_piece(lj, J, bj, g)
                    if g == WO_AT:
                        attn_add(I, b, 0, 5)

            for l in range(LAYERS):
                first = l * NB
                dve.wait_ge(s["attn_in"], 16 * N_ATTN * (l + 1))
                dve.wait_ge(s["consts_in"], 16 * len(phase_loads))
                for t in range(4):
                    dve.tensor_scalar(tables[:, t, :], tables[:, t, :], qv[:, l, t:t + 1], None, ALU.mult)\
                        .then_inc(s["weights_ok"], 1)
                dve.wait_ge(s["weights_ok"], 6 * (l + 1))
                body(l, 0, first, l - 1, NB - 1, first - 1 if l else None)
                passed(dve)
                with dve.Fori(1, NB) as b:
                    body(l, b, first + b, l, b - 1, first + b - 1)
            J = LAYERS * NB - 1
            close(J, NB - 1)

            def end(b, cols):
                dve.scalar_tensor_tensor(xend[:, b, cols], hf[:, b, cols], gate[:, 1, b:b + 1], xend[:, b, cols],
                                         ALU.mult, ALU.add).then_inc(s["end_ok"], 1)

            for step in LN_AT:
                ffn_norm(LAYERS - 1, J, step)
            dve.wait_ge(s["f_out"], NC2 * J + 1)
            dve.wait_ge(s["x1_back"], 16)
            for step in FFN_AT:
                if FFN_AT[step][:2] == ("w2", 0):
                    for b, cols in end_pieces[:NB - 1]:
                        end(b, cols)
                ffn_piece(LAYERS - 1, J, NB - 1, step, alone=True)
                if FFN_AT[step][0] == "w2":
                    ch = FFN_AT[step][1]
                    dve.wait_ge(s["f_out"], NC2 * J + ch + 2)
                    end(*end_pieces[NB - 1 + ch])

        @block.gpsimd
        def _(pool):
            def inverse_root(ch, var_ready, n, done):
                pool.wait_ge(s[var_ready], n)
                pool.tensor_tensor(rstd[:, ch, :], ln_var[:, ch, :], minus_half[:, 0:1].broadcast_to([P, TILES]),
                                   ALU.pow).then_inc(s[done], 1)

            def layer_norm(q):
                for ch in range(NC2):
                    inverse_root(ch, "ln_eps", NC2 * q + ch + 1, "ln_rstd")

            pool.sem_inc(s["hc_ok"], 2 * HALVES)
            pool.memset(minus_half[:], -0.5).then_inc(s["pool_step"], 1)
            pool.wait_ge(s["pool_step"], 1)
            pool.dma_start(select[0:3 * GRP], k_select).then_inc(s["select_in"], 16)

            def prepare(b, norm):
                if norm is not None:
                    layer_norm(norm)
                third = slice(GRP, 2 * GRP)
                for g in range(NG):
                    pool.wait_ge(s["bc_mid"], NG * b + g + 1)
                    pool.tensor_tensor(bcs[third, g, :], left(g, third), bcs[third, g, :], ALU.subtract)\
                        .then_inc(s["bc_ok"], 1)

            def states(b, q, norms):
                def product(par, G):
                    pool.wait_ge(s["h_ok"], G + 3)
                    pool.wait_ge(s["c_ok"], G + 2)
                    for m in range(HALVES):
                        pool.wait_ge(s["y_acc"], HALVES * G + m + 1)
                        pool.tensor_tensor(hC[par][:, m, :], hst[par][:, m, :], Csb[par], ALU.mult)\
                            .then_inc(s["hc_ok"], 1)

                passed(pool)
                with pool.Fori(0, GRP - 1) as i:
                    for par in range(2):
                        product(par, b * NS + 2 * i + par)
                product(0, b * NS + NS - 2)
                if norms:
                    layer_norm(q)
                pool.wait_ge(s["hc_last"], HALVES * (b + 1))
                pool.wait_ge(s["hc_ok"], HALVES * (b * NS + NS + 1))
                pool.sem_inc(s["hc_ok"], HALVES)
                if norms:
                    layer_norm(q + 1)

            for q in range(N_FIRST):
                layer_norm(q)
            prepare(0, None)
            with pool.Fori(0, NB - 1) as b:
                q = N_FIRST + N_LN_MAMBA * b
                states(b, q, True)
                prepare(b + 1, q + 2)
            states(NB - 1, None, False)
            layer_norm(N_LN_MAMBA * NB - 1)
            pool.sem_inc(s["raw_ok"], 2)
            pool.sem_inc(s["prob_ok"], 2)
            pool.sem_inc(s["ff_ok"], 1)
            pool.wait_ge(s["mix_ps"], NC2 * NB)
            pool.dma_start(unhead[0:3 * GRP], k_spread).then_inc(s["select_in"], 16)
            pool.dma_start(mask, k_mask).then_inc(s["select_in"], 16)

            def raw(I, st):
                ch, j = st // BLOCKS, st % BLOCKS
                hp, n = j // 2, STEPS * I + st
                dst = kT[:, hp, WIN + ch * BANK:WIN + (ch + 1) * BANK] if j % 2 else qraw[ch][:, hp, :]
                pool.wait_ge(s["halves_ok"], n + 3)
                pool.tensor_tensor(dst, qcos[:, st % 2, :], qsin[:, st % 2, :], ALU.add).then_inc(s["raw_ok"], 1)

            def probs(I, g):
                n = GROUPS * I + g
                pool.wait_ge(s["rsum_ok"], n + 1)
                pool.wait_ge(s["pt_ps"], n + 1)
                pool.tensor_tensor(pr[:, g % 2, :].rearrange("p (w j) -> p w j", j=P),
                                   ex[:, g % 2, :].rearrange("p (w j) -> p w j", j=P),
                                   srec[:, g % 2, :].unsqueeze(2).broadcast_to([P, QUAD, P]),
                                   ALU.mult).then_inc(s["prob_ok"], 1)

            def ffn_norm(J, step):
                if step in LN_AT and LN_AT[step][0] == "var":
                    ch = LN_AT[step][1]
                    inverse_root(ch, "f_eps", NC2 * J + ch + 1, "f_rstd")

            def ffn_piece(J, step):
                for at_step, ch in GELU_AT.items():
                    K = NC2 * J + ch
                    for f in {0: (0,), 1: (1, 2)}.get(step - at_step, ()):
                        pool.wait_ge(s["gelu_ok"], K + 1)
                        pool.wait_ge(s["av_ok"], FB * K + FB)
                        rows, cols = FROWS[f], slice(f * BANK, (f + 1) * BANK)
                        tt = pool.tensor_tensor(abuf[0:rows, cols], abuf[0:rows, cols], gbuf[0:rows, cols], ALU.mult)
                        if f == FB - 1:
                            tt.then_inc(s["ff_ok"], 1)

            def body(I, J):
                for st in range(STEPS):
                    raw(I, st)
                    if J is not None:
                        ffn_norm(J, st)
                for g in range(GROUPS):
                    probs(I, g)
                    if J is not None:
                        ffn_piece(J, g)

            for l in range(LAYERS):
                first = l * NB
                pool.wait_ge(s["attn_in"], 16 * N_ATTN * (l + 1))
                w4 = w_qkv[:, 0:2 * INNER].rearrange("p (h a d) -> p h a d", a=2, d=DH // 2)
                r4 = w_rot.rearrange("p (h a d) -> p h a d", a=2, d=DH // 2)
                for a in range(2):
                    pool.tensor_copy(r4[:, :, a, :], w4[:, :, 1 - a, :]).then_inc(s["weights_ok"], 1)
                if l == 0:
                    pool.wait_ge(s["batch_ok"], NC2 * NB + 1)
                    pool.wait_ge(s["parked"], 16 * NB)
                    pool.memset(qbd, 0.0).then_inc(s["qbd_ok"], 1)
                body(first, first - 1 if l else None)
                passed(pool)
                with pool.Fori(1, NB) as b:
                    body(first + b, first + b - 1)
            for step in LN_AT:
                ffn_norm(LAYERS * NB - 1, step)
            for what, ch, f in FFN_AT.values():
                if what == "ag":
                    K, rows, cols = NC2 * (LAYERS * NB - 1) + ch, FROWS[f], slice(f * BANK, (f + 1) * BANK)
                    pool.wait_ge(s["g_ok"], FB * K + f + 1)
                    pool.wait_ge(s["av_ok"], FB * K + f + 1)
                    tt = pool.tensor_tensor(abuf[0:rows, cols], abuf[0:rows, cols], gbuf[0:rows, cols], ALU.mult)
                    if f == FB - 1:
                        tt.then_inc(s["ff_ok"], 1)


def columns(v):
    return np.ascontiguousarray(v.reshape(-1, P).T)


def packed_vectors(a):
    half = DH // 2
    qk = []
    for l in range(LAYERS):
        for name in ("L0_ffn_q_scale", "L0_ffn_k_scale"):
            v = a[name][l]
            qk += [np.tile(v, 2), np.tile(np.concatenate([v[half:], v[:half]]), 2)]
    b1 = np.zeros((LAYERS, 2, FB, P), np.float32)
    for part in range(2):
        for f, rows in enumerate(FROWS):
            b1[:, part, f, :rows] = a["L0_ffn_b1"][:, part * HID + f * P:part * HID + f * P + rows]
    named = {"ln_w": a["L0_attn_ln_w"], "ln_b": a["L0_attn_ln_b"], "c": a["L0_c"], "conv_b": a["L0_attn_conv_b"],
             "b_dt": a["L0_attn_b_dt"], "D": a["L0_attn_D"], "qk": np.stack(qk), "ln_g": a["L0_ffn_ln_g"],
             "ln_b2": a["L0_ffn_ln_b"], "b2": a["L0_ffn_b2"], "b1": b1}
    return np.concatenate([columns(named[n]) for n in VECS], 1)


def constants():
    ident = np.eye(P, dtype=np.float32)
    centre = ident - np.float32(1.0 / P)
    heads = np.zeros((P, BLOCKS, 3 * GRP), np.float32)
    for j in range(BLOCKS):
        for h in range(2):
            for r in range(3):
                heads[h * DH:(h + 1) * DH, j, r * GRP + 2 * j + h] = 1.0
    spread = np.ascontiguousarray(heads.transpose(2, 1, 0))
    select = np.zeros((3 * GRP, GRP, P), np.float32)
    for r in range(3 * GRP):
        select[r, r % GRP] = 1.0
    no = np.float32(-3.0e38)
    i, j = np.arange(WIN)[:, None], np.arange(WIN)[None, :]
    own = np.where(j <= i, np.float32(0), no)
    prev = np.where(j >= i, np.float32(0), no)
    usual, first = np.concatenate([prev, own], 1), np.concatenate([np.full_like(own, no), own], 1)
    mask = np.stack([np.concatenate([first] + [usual] * (QUAD - 1), 1), np.concatenate([usual] * QUAD, 1)], 1)
    mask = np.concatenate([mask, mask], 0).astype(np.float32)
    half = np.arange(0, DH, 2, dtype=np.float32)
    freq = np.float32(1.0) / np.float32(10000.0) ** (half / np.float32(DH))
    t = np.arange(L, dtype=np.float32)
    angle = t[:, None] * freq[None, :]
    base = (half + np.float32(0.4 * DH)) / np.float32(1.4 * DH)
    power = (t - L // 2) / np.float32(WIN // 2)
    scale = base[None, :] ** power[:, None]
    angle, scale = (np.concatenate([a, a], 1).T for a in (angle, scale))
    sign = np.where(np.arange(DH) < DH // 2, -1.0, 1.0).astype(np.float32)[:, None]
    cos, sin = np.cos(angle), np.sin(angle) * sign
    tables = np.stack([cos * scale * 8, sin * scale * 8, cos / scale, sin / scale], 1)
    tables = np.concatenate([tables, tables], 0).astype(np.float32)
    return {"k_ident": ident, "k_centre": centre, "k_heads": heads, "k_spread": spread, "k_select": select, "k_mask": mask,
            "k_tables": tables}


def kernel(**inputs):
    import concourse.bacc as bacc
    from concourse.bass_utils import run_bass_kernel_spmd

    nc = bacc.Bacc("TRN2", target_bir_lowering=False, num_devices=1)
    a = {n: np.asarray(v) for n, v in inputs.items()}
    arrays = {"x": np.ascontiguousarray(a["L0_attn_x"].transpose(2, 0, 1)), "vecs": packed_vectors(a)}
    for n in ("attn_W_in", "attn_conv_w", "attn_W_xproj", "attn_W_dt", "attn_A_log", "attn_W_out",
              "ffn_wqkv", "ffn_wo", "ffn_w1", "ffn_w2", "wmod"):
        arrays[n] = np.ascontiguousarray(a["L0_" + n])
    arrays.update(constants())
    args = [nc.dram_tensor("in_" + n, a.shape, mybir.dt.from_np(a.dtype), kind="ExternalInput").ap()
            for n, a in arrays.items()]
    y = nc.dram_tensor("out_y", (D, NB, L), F32, kind="ExternalOutput").ap()
    adaln_block(nc, *args, y)
    r = run_bass_kernel_spmd(nc, [{"in_" + n: a for n, a in arrays.items()}], core_ids=[0])
    return np.ascontiguousarray(r.results[0]["out_y"].transpose(1, 2, 0))
```
